# Optimizing a Trainium2 kernel written in Bass

```python
import numpy as np
import jax
import jax.numpy as jnp

def _softmax(x, axis=-1):
    return jax.nn.softmax(x, axis=axis)

def _gelu(x):
    return jax.nn.gelu(x, approximate=True)

def _silu(x):
    return jax.nn.silu(x)

def _sigmoid(x):
    return jax.nn.sigmoid(x)

def _layernorm(x, axis=-1, eps=1e-05):
    m = jnp.mean(x, axis=axis, keepdims=True)
    v = jnp.var(x, axis=axis, keepdims=True)
    return (x - m) / jnp.sqrt(v + eps)

def _scatter_add(tgt, idx, src, axis=0):
    return tgt.at[idx].add(src)

def _segment_sum(src, seg, n):
    return jax.ops.segment_sum(src, seg, n)
kernel_name = 'mk_gnn_resnorm_d4_gnn_r64_ffb69f'

def setup_inputs(seed: int=0):
    np.random.seed(seed)
    _w = jnp.asarray

    def _rec_inputs():
        import jax
        import jax.numpy as jnp
        _gk = jax.random.key(seed)
        x = -0.0008691 + 1 * jax.random.normal(jax.random.fold_in(_gk, 1), (100000, 128), jnp.float32)
        src = jax.random.randint(jax.random.fold_in(_gk, 2), (25000,), 0, 100000, jnp.int32)
        dst = jax.random.randint(jax.random.fold_in(_gk, 3), (25000,), 0, 100000, jnp.int32)
        _o = jnp.argsort(dst, stable=True)
        src = src[_o]
        dst = dst[_o]
        edge_attr_3 = -0.000451519 + 1.00018 * jax.random.normal(jax.random.fold_in(_gk, 12), (25000, 3), jnp.float32)
        edge_weight = jax.random.uniform(jax.random.fold_in(_gk, 14), (25000,), jnp.float32, 0.0, 0.999998)
        return (x, src, dst, edge_attr_3, edge_weight)
    x, src, dst, edge_attr_3, edge_weight = _rec_inputs()

    def _L0_gnn_setup():
        import jax, jax.numpy as jnp
        import numpy as np
        N_NODES = 10000
        N_EDGES = 10000
        D_FEAT = 128
        D_OUT = 128
        key = jax.random.key(seed)
        k_h, k_w, k_src, k_dst = jax.random.split(key, 4)
        h = jax.random.normal(k_h, (N_NODES, D_FEAT), dtype=jnp.float32)
        W = jax.random.normal(k_w, (2 * D_FEAT, D_OUT), dtype=jnp.float32) * (1.0 / np.sqrt(2 * D_FEAT))
        b = jnp.zeros((D_OUT,), dtype=jnp.float32)
        edge_src = jax.random.randint(k_src, (N_EDGES,), 0, N_NODES, dtype=jnp.int32)
        edge_dst = jax.random.randint(k_dst, (N_EDGES,), 0, N_NODES, dtype=jnp.int32)
        return {'h': h, 'W': W, 'b': b, 'edge_src': edge_src, 'edge_dst': edge_dst, 'n_dst': N_NODES}
    _L0_gnn_all = _L0_gnn_setup()
    _L0_gnn_in = {k: v for k, v in _L0_gnn_all.items() if k in ('W', 'b')}
    del _L0_gnn_all

    def _L1_gnn_setup():
        import jax, jax.numpy as jnp
        import numpy as np
        N_LAYERS = 3

        def _lgconv(x, src, dst, norm, n):
            msgs = x[src] * norm[:, None]
            return jax.ops.segment_sum(msgs, dst, num_segments=n)
        key = jax.random.key(seed)
        k1, k2 = jax.random.split(key)
        n_users, d, n_edges = (50000, 128, 9375)
        edge_index = jax.random.randint(k1, (2, n_edges), 0, n_users, dtype=jnp.int64)
        user_emb = jax.random.normal(k2, (n_users, d), dtype=jnp.float32)
        return {'edge_index': edge_index, 'user_emb': user_emb}
    _L1_gnn_all = _L1_gnn_setup()
    _L1_gnn_in = {k: v for k, v in _L1_gnn_all.items() if k in ()}
    del _L1_gnn_all

    def _L2_gnn_setup():
        import jax, jax.numpy as jnp
        import numpy as np
        ALPHA = 0.2
        NEG_SLOPE = 0.01

        def _gcn_norm(edge_index, n):
            src, dst = (edge_index[0], edge_index[1])
            loop = jnp.arange(n, dtype=src.dtype)
            src_a = jnp.concatenate([src, loop])
            dst_a = jnp.concatenate([dst, loop])
            deg = jax.ops.segment_sum(jnp.ones_like(dst_a, dtype=jnp.float32), dst_a, num_segments=n)
            dinv = jnp.where(deg > 0, jax.lax.rsqrt(deg), 0.0)
            norm = dinv[src_a] * dinv[dst_a]
            return (src_a, dst_a, norm)

        def _propagate(h, src_a, dst_a, norm, n):
            return jax.ops.segment_sum(h[src_a] * norm[:, None], dst_a, num_segments=n)
        key = jax.random.key(seed)
        ks = jax.random.split(key, 8)
        N, F, H, O, E = (50000, 128, 128, 128, 12500)
        x = jax.random.normal(ks[0], (N, F), dtype=jnp.float32)
        edge_index = jax.random.randint(ks[1], (2, E), 0, N)
        s = 0.05
        W1 = jax.random.normal(ks[2], (F, H), dtype=jnp.float32) * s
        b1 = jnp.zeros((H,), dtype=jnp.float32)
        W2 = jax.random.normal(ks[3], (H, H), dtype=jnp.float32) * s
        b2 = jnp.zeros((H,), dtype=jnp.float32)
        W3 = jax.random.normal(ks[4], (H, O), dtype=jnp.float32) * s
        b3 = jnp.zeros((O,), dtype=jnp.float32)
        return {'x': x, 'W1': W1, 'b1': b1, 'W2': W2, 'b2': b2, 'W3': W3, 'b3': b3, 'edge_index': edge_index}
    _L2_gnn_all = _L2_gnn_setup()
    _L2_gnn_in = {k: v for k, v in _L2_gnn_all.items() if k in ('W1', 'b1', 'W2', 'b2', 'W3', 'b3')}
    del _L2_gnn_all

    def _L3_gnn_setup():
        import jax, jax.numpy as jnp
        import numpy as np
        N = 50000
        E = 12500
        MUL = 32
        NB = 8
        R_MAX = 1.0
        AVG = 16.0
        SQ3 = 3.0 ** 0.5

        def _radial_embedding(r):
            x = jnp.clip(r / R_MAX, 0.0, 1.0)
            centers = jnp.arange(NB, dtype=jnp.float32) / (NB - 1)
            sigma = 1.0 / (NB - 1)
            emb = jnp.exp(-0.5 * ((x[:, None] - centers[None, :]) / sigma) ** 2)
            emb = emb * NB ** 0.5 * (r <= R_MAX).astype(jnp.float32)[:, None]
            return emb
        key = jax.random.key(seed)
        k = jax.random.split(key, 12)
        inp = {'node_feats': jax.random.normal(k[0], (N, 4 * MUL), dtype=jnp.float32), 'edge_vec': jax.random.normal(k[1], (E, 3), dtype=jnp.float32), 'edge_length': jax.random.uniform(k[2], (E,), dtype=jnp.float32), 'senders': jax.random.randint(k[3], (E,), 0, N, dtype=jnp.int32), 'receivers': jax.random.randint(k[4], (E,), 0, N, dtype=jnp.int32), 'num_nodes': N, 'W_up0': jax.random.normal(k[5], (MUL, MUL), dtype=jnp.float32), 'W_up1': jax.random.normal(k[6], (MUL, MUL), dtype=jnp.float32), 'mlp_w0': jax.random.normal(k[7], (NB, 64), dtype=jnp.float32) / NB ** 0.5, 'mlp_b0': jnp.zeros((64,), dtype=jnp.float32), 'mlp_w1': jax.random.normal(k[8], (64, 64), dtype=jnp.float32) / 8.0, 'mlp_b1': jnp.zeros((64,), dtype=jnp.float32), 'mlp_w2': jax.random.normal(k[9], (64, 4 * MUL), dtype=jnp.float32) / 8.0, 'mlp_b2': jnp.zeros((4 * MUL,), dtype=jnp.float32), 'W_out0': jax.random.normal(k[10], (2 * MUL, MUL), dtype=jnp.float32), 'W_out1': jax.random.normal(k[11], (2 * MUL, MUL), dtype=jnp.float32)}
        return inp
    _L3_gnn_all = _L3_gnn_setup()
    _L3_gnn_in = {k: v for k, v in _L3_gnn_all.items() if k in ('W_up0', 'W_up1', 'mlp_w0', 'mlp_b0', 'mlp_w1', 'mlp_b1', 'mlp_w2', 'mlp_b2', 'W_out0', 'W_out1')}
    del _L3_gnn_all
    return {'x': x, 'src': src, 'dst': dst, 'edge_attr_3': edge_attr_3, 'edge_weight': edge_weight, 'L0_gnn_W': _L0_gnn_in['W'], 'L0_gnn_b': _L0_gnn_in['b'], 'L2_gnn_W1': _L2_gnn_in['W1'], 'L2_gnn_b1': _L2_gnn_in['b1'], 'L2_gnn_W2': _L2_gnn_in['W2'], 'L2_gnn_b2': _L2_gnn_in['b2'], 'L2_gnn_W3': _L2_gnn_in['W3'], 'L2_gnn_b3': _L2_gnn_in['b3'], 'L3_gnn_W_up0': _L3_gnn_in['W_up0'], 'L3_gnn_W_up1': _L3_gnn_in['W_up1'], 'L3_gnn_mlp_w0': _L3_gnn_in['mlp_w0'], 'L3_gnn_mlp_b0': _L3_gnn_in['mlp_b0'], 'L3_gnn_mlp_w1': _L3_gnn_in['mlp_w1'], 'L3_gnn_mlp_b1': _L3_gnn_in['mlp_b1'], 'L3_gnn_mlp_w2': _L3_gnn_in['mlp_w2'], 'L3_gnn_mlp_b2': _L3_gnn_in['mlp_b2'], 'L3_gnn_W_out0': _L3_gnn_in['W_out0'], 'L3_gnn_W_out1': _L3_gnn_in['W_out1']}

def reference(x, src, dst, edge_attr_3, edge_weight, L0_gnn_W, L0_gnn_b, L2_gnn_W1, L2_gnn_b1, L2_gnn_W2, L2_gnn_b2, L2_gnn_W3, L2_gnn_b3, L3_gnn_W_up0, L3_gnn_W_up1, L3_gnn_mlp_w0, L3_gnn_mlp_b0, L3_gnn_mlp_w1, L3_gnn_mlp_b1, L3_gnn_mlp_w2, L3_gnn_mlp_b2, L3_gnn_W_out0, L3_gnn_W_out1):
    import jax
    import jax.numpy as jnp

    def _L0_gnn_ref(h, W, b, edge_src, edge_dst, n_dst):
        import jax, jax.numpy as jnp
        import numpy as np
        N_NODES = 10000
        N_EDGES = 10000
        D_FEAT = 128
        D_OUT = 128
        msgs = jnp.take(h, edge_src, axis=0)
        sums = jax.ops.segment_sum(msgs, edge_dst, num_segments=n_dst)
        cnt = jax.ops.segment_sum(jnp.ones((edge_src.shape[0],), dtype=h.dtype), edge_dst, num_segments=n_dst)
        h_neigh = sums / jnp.maximum(cnt, 1.0)[:, None]
        h_dst = h[:n_dst]
        return jnp.concatenate([h_dst, h_neigh], axis=1) @ W + b

    def _L1_gnn_ref(edge_index, user_emb):
        import jax, jax.numpy as jnp
        import numpy as np
        N_LAYERS = 3

        def _lgconv(x, src, dst, norm, n):
            msgs = x[src] * norm[:, None]
            return jax.ops.segment_sum(msgs, dst, num_segments=n)
        n = user_emb.shape[0]
        src, dst = (edge_index[0], edge_index[1])
        ones = jnp.ones(src.shape[0], dtype=user_emb.dtype)
        deg = jax.ops.segment_sum(ones, dst, num_segments=n)
        dinv = jnp.where(deg > 0, jax.lax.rsqrt(jnp.maximum(deg, 1.0)), 0.0)
        norm = dinv[src] * dinv[dst]
        x = user_emb
        acc = x
        for _ in range(N_LAYERS):
            x = _lgconv(x, src, dst, norm, n)
            acc = acc + x
        return acc / (N_LAYERS + 1)

    def _L2_gnn_ref(x, W1, b1, W2, b2, W3, b3, edge_index):
        import jax, jax.numpy as jnp
        import numpy as np
        ALPHA = 0.2
        NEG_SLOPE = 0.01

        def _gcn_norm(edge_index, n):
            src, dst = (edge_index[0], edge_index[1])
            loop = jnp.arange(n, dtype=src.dtype)
            src_a = jnp.concatenate([src, loop])
            dst_a = jnp.concatenate([dst, loop])
            deg = jax.ops.segment_sum(jnp.ones_like(dst_a, dtype=jnp.float32), dst_a, num_segments=n)
            dinv = jnp.where(deg > 0, jax.lax.rsqrt(deg), 0.0)
            norm = dinv[src_a] * dinv[dst_a]
            return (src_a, dst_a, norm)

        def _propagate(h, src_a, dst_a, norm, n):
            return jax.ops.segment_sum(h[src_a] * norm[:, None], dst_a, num_segments=n)
        n = x.shape[0]
        src_a, dst_a, norm = _gcn_norm(edge_index, n)

        def gcn_layer(h, W, b):
            return _propagate(h @ W, src_a, dst_a, norm, n) + b
        h = jax.nn.relu(gcn_layer(x, W1, b1))
        h = jax.nn.relu(gcn_layer(h, W2, b2))
        h = gcn_layer(h, W3, b3)
        h = (1.0 - ALPHA) * _propagate(h, src_a, dst_a, norm, n) + ALPHA * h
        return jax.nn.leaky_relu(h, NEG_SLOPE)

    def _L3_gnn_ref(node_feats, edge_vec, edge_length, senders, receivers, num_nodes, W_up0, W_up1, mlp_w0, mlp_b0, mlp_w1, mlp_b1, mlp_w2, mlp_b2, W_out0, W_out1):
        import jax, jax.numpy as jnp
        import numpy as np
        N = 50000
        E = 12500
        MUL = 32
        NB = 8
        R_MAX = 1.0
        AVG = 16.0
        SQ3 = 3.0 ** 0.5

        def _radial_embedding(r):
            x = jnp.clip(r / R_MAX, 0.0, 1.0)
            centers = jnp.arange(NB, dtype=jnp.float32) / (NB - 1)
            sigma = 1.0 / (NB - 1)
            emb = jnp.exp(-0.5 * ((x[:, None] - centers[None, :]) / sigma) ** 2)
            emb = emb * NB ** 0.5 * (r <= R_MAX).astype(jnp.float32)[:, None]
            return emb
        f32 = jnp.float32
        rhat = edge_vec / (jnp.linalg.norm(edge_vec, axis=-1, keepdims=True) + 1e-12)
        Y1 = SQ3 * rhat
        emb = _radial_embedding(edge_length)
        h = jax.nn.silu(emb @ mlp_w0 + mlp_b0)
        h = jax.nn.silu(h @ mlp_w1 + mlp_b1)
        w = (h @ mlp_w2 + mlp_b2).reshape(-1, 4, MUL)
        s = node_feats[:, :MUL]
        v = node_feats[:, MUL:].reshape(-1, MUL, 3)
        xs = s @ W_up0 / f32(MUL) ** 0.5
        xv = jnp.einsum('nmc,mk->nkc', v, W_up1) / f32(MUL) ** 0.5
        ss = xs[senders]
        vv = xv[senders]
        m0 = w[:, 0] * ss
        m1 = w[:, 1][:, :, None] * ss[:, :, None] * Y1[:, None, :]
        m2 = w[:, 2][:, :, None] * vv
        m3 = w[:, 3] * (jnp.einsum('emc,ec->em', vv, Y1) / SQ3)
        mid_s = jnp.concatenate([m0, m3], axis=1)
        mid_v = jnp.concatenate([m1, m2], axis=1)
        msg_s = jax.ops.segment_sum(mid_s, receivers, num_segments=num_nodes)
        msg_v = jax.ops.segment_sum(mid_v, receivers, num_segments=num_nodes)
        out_s = msg_s @ W_out0 / f32(2 * MUL) ** 0.5
        out_v = jnp.einsum('nmc,mk->nkc', msg_v, W_out1) / f32(2 * MUL) ** 0.5
        out = jnp.concatenate([out_s, out_v.reshape(-1, 3 * MUL)], axis=1)
        return out / max(AVG, 1e-08)
    edge_index = jnp.stack([src, dst])
    x = _layernorm(x + _L0_gnn_ref(x, L0_gnn_W, L0_gnn_b, src, dst, 100000), axis=-1)
    x = _layernorm(x + _L1_gnn_ref(edge_index, x), axis=-1)
    x = _layernorm(x + _L2_gnn_ref(x, L2_gnn_W1, L2_gnn_b1, L2_gnn_W2, L2_gnn_b2, L2_gnn_W3, L2_gnn_b3, edge_index), axis=-1)
    x = _layernorm(x + _L3_gnn_ref(x, edge_attr_3, edge_weight, src, dst, 100000, L3_gnn_W_up0, L3_gnn_W_up1, L3_gnn_mlp_w0, L3_gnn_mlp_b0, L3_gnn_mlp_w1, L3_gnn_mlp_b1, L3_gnn_mlp_w2, L3_gnn_mlp_b2, L3_gnn_W_out0, L3_gnn_W_out1), axis=-1)
    return x

_drawn_inputs = setup_inputs


def setup_inputs(seed=0):
    import zlib

    import numpy as np

    out = dict(_drawn_inputs(seed))
    spreads = {'L0_gnn_b': (0.0, 0.1),
     'L2_gnn_b1': (0.0, 0.727),
     'L2_gnn_b2': (0.0, 0.31),
     'L2_gnn_b3': (0.0, 0.1),
     'L3_gnn_mlp_b0': (0.0, 0.8),
     'L3_gnn_mlp_b1': (0.0, 0.8),
     'L3_gnn_mlp_b2': (0.0, 0.8)}
    factors = {'edge_attr_3': 6.035,
     'edge_weight': 6.185,
     'L3_gnn_W_up0': 5.969,
     'L3_gnn_W_up1': 6.1,
     'L3_gnn_mlp_w0': 5.133,
     'L3_gnn_mlp_w1': 4.33,
     'L3_gnn_mlp_w2': 4.284,
     'L3_gnn_W_out0': 8.0,
     'L3_gnn_W_out1': 5.07}
    for name, (base, spread) in spreads.items():
        noise = np.random.default_rng([zlib.crc32(name.encode()), seed]).standard_normal(out[name].shape)
        drawn = base * np.exp(spread * noise) if base else spread * noise
        out[name] = jnp.asarray(drawn.astype(out[name].dtype))
    for name, factor in factors.items():
        out[name] = (out[name] * factor).astype(out[name].dtype)
    return out
```

```python
from contextlib import ExitStack

import concourse.bass as bass
from concourse import mybir

F32 = mybir.dt.float32
BF16 = mybir.dt.bfloat16
I32 = mybir.dt.int32
ALU = mybir.AluOpType
ACT = mybir.ActivationFunctionType
AX_X = mybir.AxisListType.X

N, E, D = 100000, 25000, 128
P = 125
J = 4
C = P * J
T = E // P
PAIRS = E // (2 * C)
NODE_PAIRS = N // (2 * C)
ROUNDS = 9
TK = T // 2
EPS = 1e-5
MUL = 32
NB = 8
HID = 64
SLOPE = 0.01
ALPHA = 0.2
SPLIT = ((0, 112), (112, P))
LOAD = 16 * len(SPLIT)
SRC, NODE = "source rows", "node rows"
A12, B12 = (1.5625 + EPS) / 1.5625, EPS * EPS / 1.5625
A34, B34 = 1.0 + EPS, EPS * EPS


class Steps:

    def __init__(self, eng, sem, per, index):
        self.eng, self.sem, self.per, self.index, self.n = eng, sem, per, index, 0

    def inc(self, ins):
        self.n += 1
        ins.then_inc(self.sem, 1)

    def wait(self):
        self.eng.wait_ge(self.sem, self.index * self.per + self.n)

    def so_far(self):
        return self.index * self.per + self.n

    def then(self, ins):
        self.inc(ins)
        self.wait()

    def end(self):
        assert self.n == self.per, f"{self.n} steps, not {self.per}"


def gnn_kernel(nc, a, out):
    with ExitStack() as ctx:
        def sb(name, shape, dt=F32):
            return ctx.enter_context(nc.sbuf_tensor(name, shape, dt))

        def sem(name):
            return ctx.enter_context(nc.semaphore(name))

        def dram(name, shape):
            return nc.dram_tensor(name, shape, F32, kind="Internal").ap()

        def pair_of(name, shape, dt=F32):
            return [sb(f"{name}_{b}", shape, dt) for b in range(2)]

        def pair_sem(name):
            return [sem(f"{name}_{b}") for b in range(2)]

        table = [dram(f"table{r}", (E + 1 if r < 3 else 2 * E, D)) for r in range(8)]
        radial = dram("radial", (2 * PAIRS, NB, C))
        edge_w = dram("edge_w", (E, D))

        mask = sb("mask", [128, E], BF16)
        ident = sb("ident", [128, 128])
        ones = sb("ones", [128, C])
        zero_row = sb("zero_row", [1, D])
        src_i = sb("src_i", [P, T], I32)
        dst_i = sb("dst_i", [P, T], I32)
        next_i = sb("next_i", [P, T], I32)
        slot_or_zero = sb("slot_or_zero", [P, T], I32)
        slot_or_local = sb("slot_or_local", [P, T], I32)
        out_row = sb("out_row", [P, T], I32)
        names = ("srcp1 j1 tile1 cnt sq1 dv1 rcnt deg dv2 cnt16 c3 c7 d7 e7 f7 dstf tmpa tmpb own").split()
        col = {n: sb(f"col_{n}", [P, T]) for n in names}
        attr = sb("attr", [P, T, 3])
        y_unit = sb("y_unit", [P, T, 3])
        y1 = sb("y1", [P, T, 3])
        iota1 = sb("iota1", [P, P])
        dst_tile = sb("dst_tile", [TK, 2, 2, P], I32)
        dst_next = sb("dst_next", [TK, 2, 2, P], I32)
        tf = sb("tf", [TK, 2, 2, P])
        tl = sb("tl", [TK, 2, 2, P])
        diff = sb("diff", [TK, 2, P + 1])
        first = sb("first", [TK, 2])
        w_up = sb("w_up", [128, 128])
        w_sage_self = sb("w_sage_self", [128, 128])
        w_sage_neigh = sb("w_sage_neigh", [128, 128])
        w_gcn = [sb(f"w_gcn{i}", [128, 128]) for i in range(3)]
        b_col = sb("b_col", [128, 2])
        b_row = [sb(f"b_row{i}", [128, 128]) for i in range(4)]
        b_rest = sb("b_rest", [128, 128])
        b_part = sb("b_part", [128, 128], BF16)
        b_wide = [sb(f"b_wide{i}", [96, J * 128], BF16) for i in range(2)]
        pick3 = sb("pick3", [96, 128], BF16)
        wo_in = sb("wo_in", [128, 64])
        w_out = [sb(f"w_out{i}", [128, 128]) for i in range(2)]
        mw0 = sb("mw0", [NB, HID])
        mw1 = sb("mw1", [HID, HID])
        mw2 = sb("mw2", [HID + 1, D])
        mb = sb("mb", [HID, 2])
        centre = sb("centre", [NB, 1])
        eps_col = sb("eps_col", [128, 3])

        iw = pair_of("iw", [P, 2 * J], I32)
        g_src = pair_of("g_src", [P, J, D])
        g_dst = pair_of("g_dst", [P, J, D])
        x_in = pair_of("x_in", [P, J, D])
        xT = pair_of("xT", [128, C])
        z_sb = pair_of("z_sb", [P, J, D])
        z_st = pair_of("z_st", [P, J, 6])
        z_mv = pair_of("z_mv", [P, J, 2])
        z_sd = pair_of("z_sd", [P, J])
        z_rs = pair_of("z_rs", [P, J])
        x2 = pair_of("x2", [P, J, D])
        x2T = pair_of("x2T", [128, C])
        h1T = pair_of("h1T", [128, C])
        h2T = pair_of("h2T", [128, C])
        h3r = pair_of("h3r", [P, J, D])
        v_sb = pair_of("v_sb", [P, J, D])
        u_st = pair_of("u_st", [P, J, 6])
        u_mv = pair_of("u_mv", [P, J, 2])
        u_sd = pair_of("u_sd", [P, J])
        u_rs = pair_of("u_rs", [P, J])
        u_nb = pair_of("u_nb", [P, J])
        x_out = pair_of("x_out", [P, J, D])
        loc = [pair_of(f"loc{i}", [P, J, D]) for i in range(3)]
        run = pair_of("run", [128, C])
        xdT = pair_of("xdT", [128, C])
        run_self = xdT
        self_in = [g_dst, loc[1], loc[2]]
        e1 = pair_of("e1", [P, J, D])
        e2 = pair_of("e2", [P, J, D])
        e3 = loc[0]
        e_st = pair_of("e_st", [P, J, 6])
        e_mv = pair_of("e_mv", [P, J, 2])
        e_v = pair_of("e_v", [P, J])
        e_sd = pair_of("e_sd", [P, J])
        e_rs = pair_of("e_rs", [P, J])
        e_sc = pair_of("e_sc", [P, J])
        e_out = pair_of("e_out", [P, J, D])
        work = pair_of("work", [128, 5, 512])
        ow = pair_of("ow", [P, J], I32)
        dst_wide = [work[b][:, 0, 0:C + 1].bitcast(I32) for b in range(2)]
        src_wide = [work[b][0:TK, 1, 0:C].bitcast(I32) for b in range(2)]
        step_u = [[work[b][0:TK, 2 + h, 0:C] for b in range(2)] for h in range(2)]
        cnt_row = [work[b][:, 4, 0:C] for b in range(2)]
        found = sb("found", [P, J, P])
        length = [work[b][0:NB, 0, 0:C] for b in range(2)]
        rad_in = [work[b][0:NB, 1, 0:C] for b in range(2)]
        rad_square = [work[b][0:NB, 2, 0:C] for b in range(2)]
        rad_gauss = [work[b][0:NB, 3, 0:C] for b in range(2)]
        rad_emb = [work[b][0:NB, 4, 0:C] for b in range(2)]
        emb_in = [work[b][0:NB, 0, 0:C] for b in range(2)]
        hid1 = [work[b][0:HID, 1, 0:C] for b in range(2)]
        hid2 = [work[b][0:HID + 1, 2, 0:C] for b in range(2)]
        w_rows = [work[b][0:P, 3, :].rearrange("p (j d) -> p j d", j=J) for b in range(2)]
        mid = [work[b][0:P, 0:2, :].rearrange("p q (j d) -> p (q j) d", j=J // 2) for b in range(2)]
        w1s = [work[b][0:P, 2, 0:J * MUL].rearrange("p (j m) -> p j m", j=J) for b in range(2)]
        vy = [work[b][0:P, 3, 0:J * 3 * MUL].rearrange("p (j c m) -> p j c m", j=J, c=3) for b in range(2)]
        vsum = [[work[b][0:P, 4, q * J * MUL:(q + 1) * J * MUL].rearrange("p (j m) -> p j m", j=J)
                 for b in range(2)] for q in range(2)]
        ps = {n: ctx.enter_context(nc.psum_tensor(f"ps_{n}", [128, 512], F32))
              for n in ("xT", "z", "x2T", "h1", "h2", "h3", "e", "r")}

        def rows(name):
            return ps[name][0:P, 0:J * D].rearrange("p (j d) -> p j d", j=J)

        def flat(t):
            return t[:, :, :].rearrange("p j d -> p (j d)")

        s = {n: sem(n) for n in (
            "setup_in setup_pool setup_dve setup_act setup_out cols "
            "p_mask p_count p_step p_find p_found "
            "x_T x_T_sb z_ps z_sb z_var z_std x2_rdy x2_T x2_T_sb h1_ps h1_sb h2_ps h2_sb h3_ps h3_relu "
            "u_step z_step z_step2 u_step2 ow_rdy rad_one u_var u_std u_scl x_out_rdy loc1_ps loc1_sb loc2_ps loc2_sb loc3_sb v_rdy "
            "e_T e_self_T e_dT_sb scan self_add e_rows e_ps_free e_var e_std e_rdy e_scaled e_biased e_w e_vv "
            "step0 step3 step7 step8 "
            "rad_sq rad_x rad_exp rad_m rad_rdy m1_ps m1_sb m2_ps m2_sb m3_ps m3_sb "
            "xg_T xg_sb up_ps msg msg_step mid_T mid_sb1 mid_sb2 msgo_ps run_T idx"
        ).split()}
        got_src = pair_sem("got_src")
        got_dst = pair_sem("got_dst")
        got_x = pair_sem("got_x")
        got_self = pair_sem("got_self")
        got_prep = pair_sem("got_prep")
        got_ew = pair_sem("got_ew")
        got_rad = pair_sem("got_rad")
        got_w = pair_sem("got_w")
        put_e = pair_sem("put_e")
        put_x = pair_sem("put_x")
        put_loc = pair_sem("put_loc")
        put_rad = pair_sem("put_rad")
        put_w = pair_sem("put_w")
        put_fin = pair_sem("put_fin")

        def wait_own(eng, sm, value):
            if isinstance(value, int):
                eng.wait_ge(sm, value)
                return
            held = eng.to_reg(value)
            eng.wait_ge(s["cols"], 1)
            eng.wait_ge(sm, held)

        def wait(eng, name, index, sep=False):
            if isinstance(index, int) and index < 0:
                return
            (wait_own if sep else lambda e, x, v: e.wait_ge(x, v))(eng, s[name], index + 1)

        def wait_dma(eng, sm, times, each, sep=False):
            if isinstance(times, int) and times <= 0:
                return
            (wait_own if sep else lambda e, x, v: e.wait_ge(x, v))(eng, sm, times * each)

        def bc(x, n=D):
            return x.unsqueeze(2).to_broadcast([x.shape[0], x.shape[1], n])

        def cols(name, g):
            return col[name][:, bass.ds(g * J, J)]

        def b4(x):
            return x.unsqueeze(1).to_broadcast([x.shape[0], J, x.shape[1]])

        def edge_rows(t, g, base=0):
            return t[bass.ds(g * C + base, C), :].rearrange("(j p) d -> p j d", p=P)

        def node_rows(t, g):
            return t[bass.ds(g * C, C), :].rearrange("(p j) d -> p j d", j=J)

        def transfer(eng, dst, src, sm):
            for lo, hi in SPLIT:
                eng.dma_start(dst[lo:hi], src[lo:hi]).then_inc(sm, 16)

        FREED = {0: 0, 3: 1, 7: 2, 8: 3}

        def halves(r, k):
            def kind(K):
                return None if K < 0 or K >= PAIRS + NODE_PAIRS else SRC if K < PAIRS else NODE
            return kind(r * PAIRS + k), kind(r * PAIRS + k - 1)

        def rounds(eng, body):
            for r in range(ROUNDS - 1):
                peeled = 1 if r else 2
                for k in range(peeled):
                    body(r, k, *halves(r, k))
                with eng.Fori(peeled, PAIRS) as k:
                    body(r, k, *halves(r, peeled))

        block = ctx.enter_context(nc.Block())
        n_setup_in = [0]

        @block.sync
        def _(sp):
            def setup(dst, src):
                sp.dma_start(dst, src).then_inc(s["setup_in"], 16)
                n_setup_in[0] += 16

            setup(src_i[:, :], a["src_pt"])
            setup(dst_i[:, :], a["dst_pt"])
            setup(next_i[:, :], a["next_pt"])
            setup(attr[:, :, :], a["attr_pt"])
            tiles = a["dst_ext"][1:1 + E].rearrange("(t p) -> t p", p=P)
            nexts = a["dst_ext"][2:2 + E].rearrange("(t p) -> t p", p=P)
            for h in range(2):
                setup(dst_tile[:, h, 1, :], tiles[h * TK:(h + 1) * TK, :])
                setup(dst_next[:, h, 1, :], nexts[h * TK:(h + 1) * TK, :])
                lo = 1 if h == 0 else 0
                setup(dst_tile[lo:TK, h, 0, :], tiles[h * TK + lo - 1:(h + 1) * TK - 1, :])
                setup(dst_next[lo:TK, h, 0, :], nexts[h * TK + lo - 1:(h + 1) * TK - 1, :])
            setup(w_sage_self[:, :], a["W_sage"][0:D, :])
            setup(w_sage_neigh[:, :], a["W_sage"][D:2 * D, :])
            for i in range(3):
                setup(w_gcn[i][:, :], a[f"W{i + 1}"])
            for i in range(2):
                setup(b_col[:, i:i + 1], a[f"b{i + 1}"].rearrange("(p o) -> p o", o=1))
            for i, n in enumerate(("b_sage", "b1", "b2", "b3")):
                setup(b_row[i][:, :], a[n].unsqueeze(0).to_broadcast([128, D]))
            for i in range(2):
                setup(wo_in[0:MUL, i * MUL:(i + 1) * MUL], a["W_out0"][i * MUL:(i + 1) * MUL, :])
                for c in range(3):
                    setup(wo_in[MUL * (c + 1):MUL * (c + 2), i * MUL:(i + 1) * MUL],
                          a["W_out1"][i * MUL:(i + 1) * MUL, :])
            setup(mw0[:, :], a["mlp_w0"])
            setup(mw1[:, :], a["mlp_w1"])
            setup(mw2[0:HID, :], a["mlp_w2"])
            setup(mw2[HID:HID + 1, :], a["mlp_b2"].unsqueeze(0))
            for i in range(2):
                setup(mb[:, i:i + 1], a[f"mlp_b{i}"].rearrange("(p o) -> p o", o=1))
            sp.wait_ge(s["setup_dve"], 2)
            for r in range(3):
                sp.dma_start(table[r][E:E + 1, :], zero_row[:, :]).then_inc(s["setup_out"], 16)
            sp.dma_start(w_up[0:MUL, 0:MUL], a["W_up0"]).then_inc(s["setup_out"], 16)
            for c in range(3):
                sp.dma_start(w_up[MUL + c:MUL + c + 3 * (MUL - 1) + 1:3, MUL * (c + 1):MUL * (c + 2)],
                             a["W_up1"]).then_inc(s["setup_out"], 16)

            def prep_load(k, b):
                g = 2 * k + b
                if not isinstance(k, int):
                    wait_own(sp, s["p_mask"], 3 * g - 3)
                sp.dma_start(dst_wide[b], a["dst_ext"][bass.ds(g * C, C + 1)].unsqueeze(0)
                             .to_broadcast([128, C + 1])).then_inc(got_prep[b], 16)
                sp.dma_start(src_wide[b], a["src"][bass.ds(g * C, C)].unsqueeze(0)
                             .to_broadcast([TK, C])).then_inc(got_prep[b], 16)
            for b in range(2):
                prep_load(0, b)
            with sp.Fori(1, PAIRS) as k:
                for b in range(2):
                    prep_load(k, b)

            selfs = {3: (0, 1, 2), 4: (3,), 5: (4,), 6: (5,), 7: (6, 3)}

            def loads(r, k, first_half):
                for b in range(2):
                    g = 2 * k + b
                    if first_half == NODE:
                        n = (r - 1) * PAIRS + k
                        wait(sp, "x_T", 2 * (n + PAIRS) + b - 2, sep=True)
                        transfer(sp, x_in[b][:, :, :], node_rows(a["x"], 2 * n + b), got_x[b])
                    if r in selfs:
                        wait(sp, "e_rdy", 2 * (r * PAIRS + k) + b - 2, sep=True)
                        for i, t in enumerate(selfs[r]):
                            transfer(sp, self_in[i][b][:, :, :], edge_rows(table[t], g), got_self[b])
                    if r == 5:
                        wait(sp, "rad_rdy", g - 2, sep=True)
                        sp.dma_start(length[b], a["edge_weight"][bass.ds(g * C, C)].unsqueeze(0)
                                     .to_broadcast([NB, C])).then_inc(got_ew[b], 16)
                    if r == 6:
                        wait(sp, "m1_ps", g - 2, sep=True)
                        sp.dma_start(emb_in[b], radial[bass.ds(g, 1)].rearrange("o n c -> (o n) c")
                                     ).then_inc(got_rad[b], 16)

            def stores(r, k, second_half):
                for b in range(2):
                    g = 2 * k + b
                    if second_half == SRC:
                        d = 2 * (k - 1) + b if r == 0 else 2 * (PAIRS - 1) + b
                        for nm in ("x2_rdy", "loc1_sb", "loc2_sb", "loc3_sb"):
                            wait(sp, nm, d, sep=True)
                        for t, buf in ((3, x2[b]), (4, loc[0][b]), (5, loc[1][b]), (6, loc[2][b])):
                            transfer(sp, edge_rows(table[t], d, E), buf[:, :, :], put_loc[b])
                        wait(sp, "x_out_rdy", d, sep=True)
                        transfer(sp, edge_rows(table[7], d, E), x_out[b][:, :, :], put_x[b])
                    if second_half == NODE:
                        n = 2 * ((r - 1) * PAIRS + k - 1) + b
                        wait(sp, "x_out_rdy", n + 2 * PAIRS, sep=True)
                        transfer(sp, node_rows(out, n), x_out[b][:, :, :], put_x[b])
                    wait(sp, "e_rdy", 2 * (r * PAIRS + k) + b, sep=True)
                    transfer(sp, edge_rows(table[r], g), e_out[b][:, :, :], put_e[b])
                    if r == 5:
                        wait(sp, "rad_rdy", g, sep=True)
                        sp.dma_start(radial[bass.ds(g, 1)].rearrange("o n c -> (o n) c"), rad_emb[b]
                                     ).then_inc(put_rad[b], 16)
                    if r == 6:
                        wait(sp, "m3_sb", g, sep=True)
                        transfer(sp, edge_rows(edge_w, g), w_rows[b], put_w[b])

            for r in range(ROUNDS - 1):
                if r:
                    for b in range(2):
                        sp.wait_ge(put_e[b], LOAD * PAIRS * r)
                        if r == 3:
                            sp.wait_ge(put_loc[b], 4 * LOAD * PAIRS)
                        if r == 6:
                            sp.wait_ge(put_rad[b], 16 * PAIRS)
                loads(r, 0, halves(r, 0)[0])
                loads(r, 1, halves(r, 1)[0])
                stores(r, 0, halves(r, 0)[1])
                with sp.Fori(2, PAIRS) as k:
                    loads(r, k, halves(r, 1)[0])
                    stores(r, k - 1, halves(r, 1)[1])
                stores(r, PAIRS - 1, halves(r, 1)[1])

            for b in range(2):
                sp.wait_ge(put_e[b], LOAD * PAIRS * (ROUNDS - 1))
                sp.wait_ge(put_w[b], LOAD * PAIRS)

            def loads8(k):
                for b in range(2):
                    g = 2 * k + b
                    if not isinstance(k, int):
                        wait(sp, "msg", g - 2, sep=True)
                        wait(sp, "e_ps_free", 6 * PAIRS + g - 2, sep=True)
                    transfer(sp, self_in[0][b][:, :, :], edge_rows(table[7], g), got_self[b])
                    transfer(sp, self_in[1][b][:, :, :], edge_rows(edge_w, g), got_w[b])
            loads8(0)
            with sp.Fori(1, PAIRS) as k:
                loads8(k)
            for b in range(2):
                sp.wait_ge(put_x[b], LOAD * (PAIRS + NODE_PAIRS))
                sp.wait_ge(put_fin[b], 16 * J * PAIRS)

        @block.gpsimd
        def _(pool):
            pool.memset(ident[:, :], 0.0).then_inc(s["setup_pool"], 1)
            pool.iota(iota1[:, :], pattern=[[1, P]], base=1, channel_multiplier=0,
                      allow_small_or_imprecise_dtypes=True).then_inc(s["setup_pool"], 1)
            pool.iota(col["own"][:, :], pattern=[[P, T]], base=E, channel_multiplier=1,
                      allow_small_or_imprecise_dtypes=True).then_inc(s["setup_pool"], 1)
            pool.iota(centre[:, :], pattern=[[0, 1]], base=0, channel_multiplier=-1,
                      allow_small_or_imprecise_dtypes=True).then_inc(s["setup_pool"], 1)
            pool.wait_ge(s["setup_pool"], 4)
            pool.affine_select(out=ident[:, :], in_=ident[:, :], compare_op=ALU.not_equal, fill=1.0,
                               base=0, pattern=[[-1, 128]], channel_multiplier=1
                               ).then_inc(s["setup_pool"], 1)
            pool.wait_ge(s["setup_in"], n_setup_in[0])

            def gather(dst, src, index, sm):
                for j in range(J):
                    pool.indirect_dma_start(
                        out=dst[:, j, :], out_offset=None, in_=src,
                        in_offset=bass.IndirectOffsetOnAxis(ap=index[:, j:j + 1], axis=0)
                    ).then_inc(sm, 16)

            def body(r, k):
                for b in range(2):
                    G = 2 * (r * PAIRS + k) + b
                    t = (2 * k + b) * J
                    index = src_i if r == 0 else slot_or_zero if r < 4 else slot_or_local
                    if r == 0:
                        wait(pool, "x_T", G - 2, sep=True)
                    wait(pool, "e_T", G - 2, sep=True)
                    pool.tensor_copy(iw[b][:, 0:J], index[:, bass.ds(t, J)]).then_inc(s["idx"], 1)
                    pool.tensor_copy(iw[b][:, J:2 * J], dst_i[:, bass.ds(t, J)]).then_inc(s["idx"], 1)
                    wait_own(pool, s["idx"], 2 * (G + 1))
                    gather(g_src[b], a["x"] if r == 0 else table[r - 1], iw[b], got_src[b])
                    if r == 0:
                        gather(g_dst[b], a["x"], iw[b][:, J:2 * J], got_dst[b])

            for r in range(ROUNDS - 1):
                if r:
                    pool.wait_ge(s["cols"], 3)
                    pool.wait_ge(s["setup_out"], 7 * 16)
                    for b in range(2):
                        pool.wait_ge(put_e[b], LOAD * PAIRS * r)
                        if r >= 4:
                            pool.wait_ge(put_loc[b], 4 * LOAD * PAIRS)
                body(r, 0)
                with pool.Fori(1, PAIRS) as k:
                    body(r, k)

            for b in range(2):
                pool.wait_ge(put_e[b], LOAD * PAIRS * (ROUNDS - 1))
                pool.wait_ge(put_x[b], LOAD * (PAIRS + NODE_PAIRS))

            def gather8(k):
                for b in range(2):
                    g = 2 * k + b
                    wait(pool, "xg_T", g - 2, sep=True)
                    pool.tensor_copy(iw[b][:, 0:J], slot_or_local[:, bass.ds(g * J, J)]
                                     ).then_inc(s["idx"], 1)
                    wait_own(pool, s["idx"], 32 * PAIRS + g + 1)
                    gather(g_src[b], table[7], iw[b], got_src[b])

            def scatter8(k):
                for b in range(2):
                    g = 2 * k + b
                    wait_dma(pool, put_fin[b], k, 16 * J, sep=True)
                    pool.tensor_copy(ow[b][:, :], out_row[:, bass.ds(g * J, J)]).then_inc(s["ow_rdy"], 1)
                    wait_own(pool, s["ow_rdy"], g + 1)
                    wait(pool, "e_rdy", 2 * (8 * PAIRS + k) + b, sep=True)
                    for j in range(J):
                        pool.indirect_dma_start(
                            out=out, out_offset=bass.IndirectOffsetOnAxis(ap=ow[b][:, j:j + 1], axis=0),
                            in_=e_out[b][:, j, :], in_offset=None, bounds_check=N - 1,
                            oob_is_err=False).then_inc(put_fin[b], 16)
            gather8(0)
            gather8(1)
            scatter8(0)
            with pool.Fori(2, PAIRS) as k:
                gather8(k)
                scatter8(k - 1)
            scatter8(PAIRS - 1)
            for b in range(2):
                pool.wait_ge(put_fin[b], 16 * J * PAIRS)

        @block.tensor
        def _(pe):
            mm = nc.tensor.matmul

            def to_cols(bank, src):
                for j in range(J):
                    i = nc.tensor.transpose(ps[bank][:, j * P:(j + 1) * P], src(j), ident[0:P, 0:P])
                return i

            def to_rows(bank, src):
                for j in range(J):
                    i = nc.tensor.transpose(rows(bank)[:, j, :], src[:, j * P:(j + 1) * P], ident[:, :])
                return i

            def by_rows(bank, lhs, w, bias=None):
                for j in range(J):
                    i = mm(rows(bank)[:, j, :], lhs[:, j * P:(j + 1) * P], w, start=(j == 0 if bias is not None else True),
                           stop=bias is None, skip_group_check=True)
                if bias is not None:
                    i = mm(ps[bank][0:P, 0:J * D], pick3[:, 0:P], b_wide[bias][:, :], start=False,
                           stop=True, skip_group_check=True)
                return i

            pe.wait_ge(s["setup_pool"], 5)
            pe.wait_ge(s["cols"], 1)
            def find(k):
                for b in range(2):
                    g = 2 * k + b
                    pe.wait_ge(s["p_mask"], 3 * g + 3)
                    pe.wait_ge(s["p_count"], g + 1)
                    if not (isinstance(k, int) and b == 0):
                        pe.wait_ge(s["p_found"], g)
                    fr = ps["e"][0:P, 0:J * (P + 1)].rearrange("p (j c) -> p j c", j=J)
                    for j in range(J):
                        for h in range(2):
                            mm(fr[:, j, :], step_u[h][b][:, j * P:(j + 1) * P], diff[:, h, :],
                               start=(h == 0), stop=(h == 1))
                    for j in range(J):
                        i = mm(ps["r"][0:P, j:j + 1], cnt_row[b][:, j * P:(j + 1) * P], ident[:, 0:1],
                               start=True, stop=True)
                    i.then_inc(s["p_find"], 1)
            find(0)
            with pe.Fori(1, PAIRS) as k:
                find(k)
            pe.wait_ge(s["p_found"], 2 * PAIRS)

            def body(r, k, first_half, second_half):
                K = r * PAIRS + k

                def edge_in(b):
                    G, g = 2 * K + b, 2 * k + b
                    if r == 0:
                        wait(pe, "e_ps_free", g - 1)
                        wait_dma(pe, got_dst[b], k + 1, 16 * J)
                        to_cols("e", lambda j: g_dst[b][:, j, :]).then_inc(s["e_T"], 1)
                        return
                    if r in (4, 5, 6):
                        wait(pe, "e_scaled", 2 * (K - 4 * PAIRS) + b - 1)
                    else:
                        wait(pe, "scan", G - 1)
                    wait_dma(pe, got_src[b], K + 1, 16 * J)
                    to_cols("e", lambda j: g_src[b][:, j, :]).then_inc(s["e_T"], 1)
                    if r in (4, 5, 6):
                        wait_dma(pe, got_self[b], 3 * PAIRS + (r - 4) * PAIRS + k + 1, LOAD)
                        to_cols("r", lambda j: self_in[0][b][:, j, :]).then_inc(s["e_self_T"], 1)

                def edge_out(b):
                    G, g = 2 * K + b, 2 * k + b
                    if r == 0:
                        wait(pe, "e_dT_sb", 2 * k + b)
                        by_rows("r", xdT[b], w_sage_self[:, :], bias=0)
                        wait(pe, "scan", G)
                        by_rows("e", run[b], w_sage_neigh[:, :]).then_inc(s["e_rows"], 1)
                    elif r in (4, 5, 6):
                        wait(pe, "self_add", 2 * (K - 4 * PAIRS) + b)
                        by_rows("e", run_self[b], w_gcn[r - 4][:, :]).then_inc(s["e_rows"], 1)
                    else:
                        if r in (1, 2):
                            wait(pe, "e_rdy", G - 1)
                        elif not (isinstance(k, int) and b == 0):
                            wait(pe, "e_ps_free", FREED[r] * 2 * PAIRS + g - 1)
                        wait(pe, "scan", G)
                        to_rows("r", run[b]).then_inc(s["e_rows"], 1)

                def x_to_cols(b):
                    if not first_half:
                        return
                    n = 2 * K + b
                    wait(pe, "x_T_sb", n - 1)
                    if r == 0:
                        wait_dma(pe, got_src[b], k + 1, 16 * J)
                        to_cols("xT", lambda j: g_src[b][:, j, :]).then_inc(s["x_T"], 1)
                    else:
                        wait_dma(pe, got_x[b], K - PAIRS + 1, LOAD)
                        to_cols("xT", lambda j: x_in[b][:, j, :]).then_inc(s["x_T"], 1)

                def sage(b):
                    if not first_half:
                        return
                    n = 2 * K + b
                    wait(pe, "z_sb", n - 1)
                    wait(pe, "x_T_sb", n)
                    by_rows("z", xT[b], w_sage_self[:, :], bias=0).then_inc(s["z_ps"], 1)

                m = 2 * (K - 1)

                def x2_to_cols(b):
                    if not second_half:
                        return
                    wait(pe, "x2_T_sb", m + b - 1)
                    if r < 2:
                        wait(pe, "loc2_sb", m + b - 1 if second_half == SRC else 2 * PAIRS - 1)
                    wait(pe, "x2_rdy", m + b)
                    to_cols("x2T", lambda j: x2[b][:, j, :]).then_inc(s["x2_T"], 1)

                def gcn1(b):
                    if not second_half:
                        return
                    wait(pe, "h1_sb", m + b - 1)
                    wait(pe, "x2_T_sb", m + b)
                    mm(ps["h1"][:, 0:C], w_gcn[0][:, :], x2T[b][:, :], start=True, stop=True
                       ).then_inc(s["h1_ps"], 1)

                def gcn2(b):
                    if not second_half:
                        return
                    wait(pe, "h2_sb", m + b - 1)
                    wait(pe, "h1_sb", m + b)
                    mm(ps["h2"][:, 0:C], w_gcn[1][:, :], h1T[b][:, :], start=True, stop=True
                       ).then_inc(s["h2_ps"], 1)

                def gcn3(b):
                    if not second_half:
                        return
                    wait(pe, "v_rdy", m + b - 1)
                    wait(pe, "h3_relu", m + b - 1)
                    if r < 2:
                        wait(pe, "loc3_sb", m + b - 1 if second_half == SRC else 2 * PAIRS - 1)
                    wait(pe, "h2_sb", m + b)
                    by_rows("h3", h2T[b], w_gcn[2][:, :], bias=1).then_inc(s["h3_ps"], 1)

                def local_rows(b, i):
                    if second_half != SRC:
                        return
                    wait(pe, f"h{i}_sb", m + b)
                    if i == 2:
                        wait(pe, "loc1_sb", m + b)
                    to_rows("x2T", (h1T, h2T)[i - 1][b]).then_inc(s[f"loc{i}_ps"], 1)

                def radial_1(b):
                    g = 2 * k + b
                    if r == 6:
                        wait(pe, "m1_sb", g - 1)
                        wait_dma(pe, got_rad[b], k + 1, 16)
                        mm(ps["h1"][0:HID, 0:C], mw0[:, :], emb_in[b], start=True, stop=True
                           ).then_inc(s["m1_ps"], 1)

                def radial_2(b):
                    g = 2 * k + b
                    if r == 6:
                        wait(pe, "m2_sb", g - 1)
                        wait(pe, "m1_sb", g, sep=True)
                        mm(ps["h2"][0:HID, 0:C], mw1[:, :], hid1[b], start=True, stop=True
                           ).then_inc(s["m2_ps"], 1)

                def radial_3(b):
                    g = 2 * k + b
                    if r == 6:
                        wait(pe, "m3_sb", g - 1)
                        wait(pe, "m2_sb", g)
                        pe.wait_ge(s["rad_one"], 2)
                        by_rows("h3", hid2[b], mw2[:, :]).then_inc(s["m3_ps"], 1)

                A, B = 0, 1
                edge_in(A)
                x2_to_cols(A)
                x_to_cols(A)
                gcn1(A)
                radial_1(A)
                sage(A)
                edge_out(A)
                local_rows(A, 1)
                radial_2(A)
                gcn2(A)
                local_rows(A, 2)
                x2_to_cols(B)
                x_to_cols(B)
                edge_in(B)
                gcn1(B)
                radial_1(B)
                sage(B)
                gcn3(A)
                radial_3(A)
                gcn2(B)
                radial_2(B)
                edge_out(B)
                local_rows(B, 1)
                local_rows(B, 2)
                gcn3(B)
                radial_3(B)

            rounds(pe, body)

            def body8(k):
                for b in range(2):
                    wait(pe, "xg_sb", 2 * k + b - 1)
                    wait_dma(pe, got_src[b], 8 * PAIRS + k + 1, 16 * J)
                    to_cols("e", lambda j: g_src[b][:, j, :]).then_inc(s["xg_T"], 1)
                    wait(pe, "msg", 2 * k + b - 1)
                    wait(pe, "xg_sb", 2 * k + b)
                    by_rows("r", xdT[b], w_up[:, :]).then_inc(s["up_ps"], 1)
                for b in range(2):
                    g = 2 * k + b
                    wait(pe, "msg", g)
                    wait(pe, "mid_sb1", g - 1)
                    wait(pe, "mid_sb2", g - 1)
                    to_cols("h1", lambda j: mid[b][:, j, 0:D])
                    to_cols("h2", lambda j: mid[b][:, j, D:2 * D]).then_inc(s["mid_T"], 1)
                for b in range(2):
                    g = 2 * k + b
                    wait(pe, "mid_sb1", g)
                    wait(pe, "mid_sb2", g)
                    wait(pe, "scan", 16 * PAIRS + g - 1)
                    mm(ps["xT"][:, 0:C], w_out[0][:, :], h1T[b][:, :], start=True, stop=False)
                    mm(ps["xT"][:, 0:C], w_out[1][:, :], h2T[b][:, :], start=False, stop=True
                       ).then_inc(s["msgo_ps"], 1)
                for b in range(2):
                    g = 2 * k + b
                    wait(pe, "e_ps_free", 6 * PAIRS + g - 1)
                    wait(pe, "scan", 16 * PAIRS + g)
                    to_rows("z", run[b]).then_inc(s["run_T"], 1)
            body8(0)
            with pe.Fori(1, PAIRS) as k:
                body8(k)

        @block.scalar
        def _(act):
            def f(out_, in_, func, bias=0.0, scale=1.0):
                return nc.scalar.activation(out_, in_, func, bias=bias, scale=scale)

            act.wait_ge(s["cols"], 2)
            f(col["sq1"][:, :], col["cnt"][:, :], ACT.Sqrt).then_inc(s["setup_act"], 1)
            f(col["tmpb"][:, :], col["deg"][:, :], ACT.Sqrt).then_inc(s["setup_act"], 1)
            f(col["tmpa"][:, :], col["dstf"][:, :], ACT.Sqrt).then_inc(s["setup_act"], 1)

            def body(r, k, first_half, second_half):
                K = r * PAIRS + k
                m = 2 * (K - 1)

                def dst_cols(b):
                    if r == 0:
                        wait(act, "e_T", 2 * k + b)
                        wait(act, "e_rows", 2 * k + b - 2)
                        f(xdT[b][:, :], ps["e"][:, 0:C], ACT.Copy).then_inc(s["e_dT_sb"], 1)

                def x_cols(b):
                    if first_half:
                        wait(act, "x_T", 2 * K + b)
                        wait(act, "z_ps", 2 * K + b - 2)
                        if r == 0:
                            wait(act, "scan", 2 * K + b - 2)
                        f(xT[b][:, :], ps["xT"][:, 0:C], ACT.Copy).then_inc(s["x_T_sb"], 1)

                def z_rows(b):
                    if first_half:
                        wait(act, "z_ps", 2 * K + b)
                        wait(act, "x2_rdy", 2 * K + b - 2)
                        f(flat(z_sb[b]), ps["z"][0:P, :], ACT.Copy).then_inc(s["z_sb"], 1)

                def z_root(b):
                    if first_half:
                        wait(act, "z_var", 2 * K + b)
                        f(z_sd[b][:, :], z_mv[b][:, :, 1], ACT.Sqrt, bias=eps_col[0:P, 1:2], scale=A12
                          ).then_inc(s["z_std"], 1)

                def x2_cols(b):
                    if second_half:
                        wait(act, "x2_T", m + b)
                        wait(act, "h1_ps", m + b - 2)
                        f(x2T[b][:, :], ps["x2T"][:, 0:C], ACT.Copy).then_inc(s["x2_T_sb"], 1)

                def relu(b, i):
                    if second_half:
                        wait(act, f"h{i}_ps", m + b)
                        wait(act, f"h{i + 1}_ps", m + b - 2)
                        if r < 2:
                            wait(act, f"loc{i}_ps", m + b - 2 if second_half == SRC else 2 * PAIRS - 1)
                        f((h1T, h2T)[i - 1][b][:, :], ps[f"h{i}"][:, 0:C], ACT.Relu,
                          bias=b_col[:, i - 1:i]).then_inc(s[f"h{i}_sb"], 1)

                def local(b, i):
                    if second_half == SRC:
                        wait(act, f"loc{i}_ps" if i < 3 else "h3_ps", m + b)
                        wait_dma(act, put_loc[b], K - 1, 4 * LOAD)
                        f(flat(loc[i - 1][b]), ps["x2T" if i < 3 else "h3"][0:P, :], ACT.Copy
                          ).then_inc(s[f"loc{i}_sb"], 1)

                def leaky_part(b):
                    if second_half:
                        wait(act, "h3_ps", m + b)
                        wait(act, "u_var", m + b - 2)
                        f(flat(h3r[b]), ps["h3"][0:P, :], ACT.Relu, scale=1.0 - SLOPE
                          ).then_inc(s["h3_relu"], 1)

                def u_root(b):
                    if second_half:
                        wait(act, "u_var", m + b)
                        wait(act, "u_scl", m + b - 2)
                        src_mode = second_half == SRC
                        f(u_sd[b][:, :], u_mv[b][:, :, 1], ACT.Sqrt,
                          bias=eps_col[0:P, 0:1] if src_mode else eps_col[0:P, 2:3],
                          scale=1.0 if src_mode else A34).then_inc(s["u_std"], 1)

                def x_result(b):
                    if second_half:
                        wait_dma(act, put_x[b], K - 1, LOAD)
                        wait(act, "u_scl", m + b)
                        for j in range(J):
                            i = f(x_out[b][:, j, :], v_sb[b][:, j, :], ACT.Identity,
                                  bias=u_nb[b][:, j:j + 1], scale=u_rs[b][:, j:j + 1])
                        i.then_inc(s["x_out_rdy"], 1)

                def by_col(out_, in_, name, g, func=ACT.Copy):
                    for j in range(J):
                        i = f(out_[:, j, :], in_[:, j, :], func,
                              scale=col[name][:, bass.ds(g * J + j, 1)])
                    return i

                def edge_1(b):
                    G, g = 2 * K + b, 2 * k + b
                    if r in (4, 5, 6):
                        wait(act, "e_rows", G)
                        wait(act, "e_biased", 2 * (K - 4 * PAIRS) + b - 2, sep=True)
                        by_col(e1[b], rows("e"), "dv2", g).then_inc(s["e_scaled"], 1)
                    if r == 7:
                        wait_dma(act, got_self[b], 6 * PAIRS + 2 * (k + 1), LOAD)
                        wait(act, "e_rdy", G - 2, sep=True)
                        by_col(e1[b], self_in[0][b], "c7", g).then_inc(s["e_w"], 1)
                        by_col(e3[b], self_in[1][b], "d7", g).then_inc(s["e_w"], 1)

                def edge_2(b):
                    G, g = 2 * K + b, 2 * k + b
                    if r in (0, 3, 7):
                        nth = {0: 0, 3: 1, 7: 2}[r] * 2 * PAIRS + g
                        wait(act, "e_var", nth)
                        f(e_sd[b][:, :], e_mv[b][:, :, 1] if r == 0 else e_v[b][:, :], ACT.Sqrt,
                          bias=eps_col[0:P, 0:1]).then_inc(s["e_std"], 1)
                    if r in (4, 5, 6):
                        wait_dma(act, put_e[b], K, LOAD)
                        wait(act, "e_biased", 2 * (K - 4 * PAIRS) + b, sep=True)
                        by_col(e_out[b], e2[b], "dv2", g, ACT.Relu if r < 6 else ACT.Copy
                               ).then_inc(s["e_rdy"], 1)

                def radial_5(b):
                    g = 2 * k + b
                    if r == 5:
                        wait(act, "rad_x", g)
                        f(rad_square[b], rad_in[b], ACT.Square, bias=centre[:, 0:1], scale=float(NB - 1)
                          ).then_inc(s["rad_sq"], 1)
                        wait(act, "rad_sq", g)
                        wait(act, "rad_rdy", g - 2)
                        f(rad_gauss[b], rad_square[b], ACT.Exp, scale=-0.5).then_inc(s["rad_exp"], 1)

                def radial_6(b, i):
                    g = 2 * k + b
                    if r == 6:
                        wait(act, f"m{i}_ps", g)
                        wait(act, f"m{i + 1}_ps", g - 2)
                        f((hid1[b], hid2[b][0:HID, :])[i - 1], ps[f"h{i}"][0:HID, 0:C], ACT.Silu,
                          bias=mb[:, i - 1:i]).then_inc(s[f"m{i}_sb"], 1)

                A, B = 0, 1
                dst_cols(A)
                x2_cols(A)
                x_cols(A)
                relu(A, 1)
                radial_6(A, 1)
                z_rows(A)
                edge_1(A)
                local(A, 1)
                relu(A, 2)
                radial_6(A, 2)
                local(A, 2)
                edge_2(A)
                x2_cols(B)
                x_cols(B)
                dst_cols(B)
                relu(B, 1)
                radial_6(B, 1)
                z_rows(B)
                z_root(A)
                local(A, 3)
                leaky_part(A)
                relu(B, 2)
                radial_6(B, 2)
                edge_1(B)
                radial_5(A)
                z_root(B)
                u_root(A)
                x_result(A)
                edge_2(B)
                radial_5(B)
                local(B, 1)
                local(B, 2)
                local(B, 3)
                leaky_part(B)
                u_root(B)
                x_result(B)

            rounds(act, body)

            def body8(k):
                for b in range(2):
                    g = 2 * k + b
                    wait(act, "xg_T", g)
                    wait(act, "up_ps", g - 2)
                    f(xdT[b][:, :], ps["e"][:, 0:C], ACT.Copy).then_inc(s["xg_sb"], 1)
                for b in range(2):
                    g = 2 * k + b
                    wait(act, "mid_T", g)
                    wait(act, "msgo_ps", g - 2)
                    f(h1T[b][:, :], ps["h1"][:, 0:C], ACT.Copy).then_inc(s["mid_sb1"], 1)
                    f(h2T[b][:, :], ps["h2"][:, 0:C], ACT.Copy).then_inc(s["mid_sb2"], 1)
                for b in range(2):
                    g = 2 * k + b
                    wait(act, "e_var", 6 * PAIRS + g)
                    f(e_sd[b][:, :], e_mv[b][:, :, 1], ACT.Sqrt, bias=eps_col[0:P, 0:1]
                      ).then_inc(s["e_std"], 1)
            body8(0)
            with act.Fori(1, PAIRS) as k:
                body8(k)

        @block.vector
        def _(dve):
            v = nc.vector
            st = Steps(dve, s["setup_dve"], 0, 0)
            st.inc(v.memset(zero_row[:, :], 0.0))
            st.inc(v.memset(w_up[:, :], 0.0))
            st.inc(v.memset(ones[:, :], 1.0))
            st.inc(v.memset(eps_col[:, 0:1], EPS))
            st.inc(v.memset(eps_col[:, 1:2], B12))
            st.inc(v.memset(eps_col[:, 2:3], B34))
            st.inc(v.memset(pick3[:, :], 0.0))
            for i in range(2):
                st.inc(v.memset(w_out[i][:, :], 0.0))
                st.inc(v.memset(run[i][:, :], 0.0))
                st.inc(v.memset(cnt_row[i], 0.0))
            st.inc(v.memset(dst_tile[0:1, 0, 0, :], 0))
            st.inc(v.memset(dst_next[0:1, 0, 0, :], 0))
            st.wait()
            for q in range(3):
                st.inc(v.memset(pick3[32 * q:32 * q + 1, :], 1.0))
            dve.wait_ge(s["setup_in"], n_setup_in[0])
            dve.wait_ge(s["setup_pool"], 5)
            st.inc(v.tensor_copy(tf[:, :, :, :], dst_tile[:, :, :, :]))
            st.inc(v.tensor_copy(first[:, :], dst_tile[:, :, 1, 0]))
            st.inc(v.tensor_tensor(tl[:, :, :, :], dst_tile[:, :, :, :], dst_next[:, :, :, :], ALU.not_equal))
            st.inc(v.tensor_tensor(w_sage_self[:, :], w_sage_self[:, :], ident[:, :], ALU.add))
            st.inc(v.tensor_copy(col["srcp1"][:, :], src_i[:, :]))
            st.inc(v.tensor_copy(col["dstf"][:, :], dst_i[:, :]))
            st.inc(v.tensor_tensor(col["tmpa"][:, :], dst_i[:, :], next_i[:, :], ALU.not_equal))
            st.inc(v.tensor_scalar(mw0[:, :], mw0[:, :], float(NB) ** 0.5, None, ALU.mult))
            for i in range(2):
                for c in range(4):
                    p0 = MUL * c
                    dst = w_out[i][0:MUL, 0:MUL] if c == 0 else \
                        w_out[i][p0:p0 + MUL, MUL + c - 1:MUL + c - 1 + 3 * (MUL - 1) + 1:3]
                    st.inc(v.tensor_scalar(dst, wo_in[p0:p0 + MUL, i * MUL:(i + 1) * MUL],
                                           1.0 / (8.0 * 16.0), None, ALU.mult))
            for i, row in ((0, b_row[0]), (1, b_row[3])):
                st.then(v.tensor_copy(b_rest[:, :], row[:, :]))
                for q in range(3):
                    p0 = 32 * q
                    st.then(v.tensor_copy(b_part[:, :], b_rest[:, :]))
                    st.inc(v.tensor_copy(b_wide[i][p0:p0 + 32, 0:D], b_part[p0:p0 + 32, :]))
                    st.then(v.tensor_tensor(b_rest[:, :], b_rest[:, :], b_part[:, :], ALU.subtract))
                for j in range(1, J):
                    st.inc(v.tensor_copy(b_wide[i][:, j * D:(j + 1) * D], b_wide[i][:, 0:D]))
            st.wait()
            st.then(v.scalar_tensor_tensor(out=tf[:, :, :, :].rearrange("p h q c -> p (h q c)"),
                                           in0=tl[:, :, :, :].rearrange("p h q c -> p (h q c)"), scalar=0.5,
                                           in1=tf[:, :, :, :].rearrange("p h q c -> p (h q c)"),
                                           op0=ALU.mult, op1=ALU.add))
            st.then(v.tensor_scalar(tf[:, :, :, :], tf[:, :, :, :], 0.5, None, ALU.add))
            st.then(v.tensor_tensor(diff[:, :, 0:P], tf[:, :, 1, :], tf[:, :, 0, :], ALU.subtract))
            st.then(v.tensor_copy(diff[0:1, 0, 0:P], tf[0:1, 0, 1, :]))
            st.inc(v.memset(diff[:, :, P:P + 1], 1.0))
            st.inc(v.tensor_scalar(col["srcp1"][:, :], col["srcp1"][:, :], 1.0, None, ALU.add))
            st.then(v.tensor_scalar(col["dstf"][:, :], col["dstf"][:, :], float(-N), None, ALU.add))
            st.then(v.tensor_tensor(col["dstf"][:, :], col["dstf"][:, :], col["tmpa"][:, :], ALU.mult))
            st.then(v.tensor_scalar(col["dstf"][:, :], col["dstf"][:, :], float(N), None, ALU.add))
            st.inc(v.tensor_copy(out_row[:, :], col["dstf"][:, :]))
            st.inc(v.tensor_tensor(y1[:, :, :], attr[:, :, :], attr[:, :, :], ALU.mult))
            dve.wait_ge(s["setup_out"], 7 * 16)
            st.inc(v.tensor_scalar(w_up[:, :], w_up[:, :], float(MUL) ** -0.5, None, ALU.mult))
            st.wait()
            st.then(v.tensor_reduce(col["dstf"][:, :], y1[:, :, :], AX_X, ALU.add))
            v.memset(found[:, :, :], 0.0).then_inc(s["cols"], 1)
            dve.wait_ge(s["cols"], 1)

            def prepare(k):
                for b in range(2):
                    g = 2 * k + b
                    wait_dma(dve, got_prep[b], k + 1, 32)
                    v.tensor_tensor(mask[:, bass.ds(g * C, C)], dst_wide[b][:, 1:C + 1],
                                    dst_wide[b][:, 0:C], ALU.is_equal).then_inc(s["p_mask"], 1)
                    if not isinstance(k, int):
                        dve.wait_ge(s["p_find"], g - 1)
                    for h in range(2):
                        v.tensor_scalar(step_u[h][b], src_wide[b], first[:, h:h + 1], None,
                                        ALU.is_ge).then_inc(s["p_mask"], 1)
                    dve.wait_ge(s["p_mask"], 3 * g + 3)
                    if not (isinstance(k, int) and b == 0):
                        dve.wait_ge(s["p_count"], g)
                    v.tensor_tensor_scan(cnt_row[b], mask[:, bass.ds(g * C, C)], ones[:, :],
                                         cnt_row[1 - b][:, C - 1:C], ALU.mult, ALU.add
                                         ).then_inc(s["p_count"], 1)
                    if b == 1:
                        read_found(k, 0)
                        read_found(k, 1)

            def read_found(k, b):
                g = 2 * k + b
                wait_own(dve, s["p_find"], g + 1)
                fr = ps["e"][0:P, 0:J * (P + 1)].rearrange("p (j c) -> p j c", j=J)
                v.tensor_copy(col["cnt"][:, bass.ds(g * J, J)], ps["r"][0:P, 0:J]).then_inc(s["p_step"], 1)
                v.tensor_copy(col["tile1"][:, bass.ds(g * J, J)], fr[:, :, P]).then_inc(s["p_step"], 1)
                for j in range(J):
                    v.scalar_tensor_tensor(out=found[:, j, :], in0=fr[:, j, 0:P],
                                           scalar=col["srcp1"][:, bass.ds(g * J + j, 1)],
                                           in1=iota1[:, :], op0=ALU.is_equal, op1=ALU.mult
                                           ).then_inc(s["p_step"], 1)
                wait_own(dve, s["p_step"], 6 * (g + 1))
                v.tensor_reduce(col["j1"][:, bass.ds(g * J, J)], found[:, :, :], AX_X, ALU.add
                                ).then_inc(s["p_found"], 1)
                dve.wait_ge(s["p_found"], g + 1)

            prepare(0)
            with dve.Fori(1, PAIRS) as k:
                prepare(k)

            v.tensor_scalar(col["deg"][:, :], col["cnt"][:, :], 1.0, None, ALU.add).then_inc(s["cols"], 1)
            st.inc(v.tensor_scalar(col["tile1"][:, :], col["tile1"][:, :], float(P), float(-P - 1), ALU.mult, ALU.add))
            st.inc(v.tensor_scalar(col["d7"][:, :], col["j1"][:, :], 0.5, None, ALU.is_ge))
            st.wait()
            st.then(v.tensor_tensor(col["j1"][:, :], col["j1"][:, :], col["tile1"][:, :], ALU.add))
            st.inc(v.tensor_scalar(col["c7"][:, :], col["j1"][:, :], float(-E), None, ALU.add))
            st.then(v.tensor_tensor(col["e7"][:, :], col["j1"][:, :], col["own"][:, :], ALU.subtract))
            st.inc(v.tensor_tensor(col["c7"][:, :], col["c7"][:, :], col["d7"][:, :], ALU.mult))
            st.then(v.tensor_tensor(col["e7"][:, :], col["e7"][:, :], col["d7"][:, :], ALU.mult))
            st.inc(v.tensor_scalar(col["c7"][:, :], col["c7"][:, :], float(E), None, ALU.add))
            st.then(v.tensor_tensor(col["e7"][:, :], col["e7"][:, :], col["own"][:, :], ALU.add))
            st.inc(v.tensor_copy(slot_or_zero[:, :], col["c7"][:, :]))
            st.then(v.tensor_copy(slot_or_local[:, :], col["e7"][:, :]))
            dve.wait_ge(s["cols"], 2)
            dve.wait_ge(s["setup_act"], 3)
            st.inc(v.reciprocal(col["rcnt"][:, :], col["cnt"][:, :]))
            st.inc(v.reciprocal(col["dv1"][:, :], col["sq1"][:, :]))
            st.inc(v.reciprocal(col["dv2"][:, :], col["tmpb"][:, :]))
            st.inc(v.tensor_scalar(col["cnt16"][:, :], col["cnt"][:, :], 1.0 / 16.0, None, ALU.mult))
            st.inc(v.tensor_scalar(col["c7"][:, :], col["deg"][:, :], ALPHA / (1 - ALPHA), 1.0, ALU.mult, ALU.add))
            st.inc(v.tensor_scalar(col["d7"][:, :], col["deg"][:, :], 1.0 / (1 - ALPHA), None, ALU.mult))
            st.then(v.tensor_scalar(col["tmpa"][:, :], col["tmpa"][:, :], 1e-12, None, ALU.add))
            st.then(v.reciprocal(col["tmpb"][:, :], col["tmpa"][:, :]))
            st.inc(v.tensor_tensor(y_unit[:, :, :], attr[:, :, :], bc(col["tmpb"][:, :], 3), ALU.mult))
            st.inc(v.tensor_tensor(col["c3"][:, :], col["sq1"][:, :], col["dv2"][:, :], ALU.mult))
            st.inc(v.tensor_tensor(col["e7"][:, :], col["dv2"][:, :], col["dv2"][:, :], ALU.mult))
            st.inc(v.tensor_scalar(col["f7"][:, :], col["dv2"][:, :], 1 - ALPHA, None, ALU.mult))
            st.wait()
            st.inc(v.tensor_scalar(col["c3"][:, :], col["c3"][:, :], 0.25, None, ALU.mult))
            st.inc(v.tensor_scalar(col["e7"][:, :], col["e7"][:, :], (1 - ALPHA) ** 2, None, ALU.mult))
            st.inc(v.tensor_scalar(y1[:, :, :], y_unit[:, :, :], 3.0 ** 0.5, None, ALU.mult))
            st.wait()
            v.memset(found[:, :, :], 0.0).then_inc(s["cols"], 1)

            def stats(q, x, sts, mv):
                for j in range(J):
                    q.inc(v.bn_stats(sts[:, j, :], x[:, j, :]))
                wait_own(dve, q.sem, q.so_far())
                for j in range(J):
                    i = v.bn_aggr(mv[:, j, :], sts[:, j, :])
                    if j < J - 1:
                        q.inc(i)
                return i

            def normed(x_, x, mv, scale):
                for j in range(J):
                    i = v.tensor_scalar(x_[:, j, :], x[:, j, :], mv[:, j, 0:1], scale[:, j:j + 1],
                                        ALU.subtract, ALU.mult)
                return i

            def body(r, k, first_half, second_half):
                K = r * PAIRS + k
                m = 2 * (K - 1)

                def scan(b):
                    G, g = 2 * K + b, 2 * k + b
                    if r == 0:
                        wait(dve, "x_T_sb", G)
                    else:
                        wait(dve, "e_T", G)
                    wait(dve, "e_rows", G - 2)
                    wait(dve, "scan", G - 1)
                    v.tensor_tensor_scan(run[b][:, :], mask[:, bass.ds(g * C, C)],
                                         xT[b][:, :] if r == 0 else ps["e"][:, 0:C], run[1 - b][:, C - 1:C],
                                         ALU.mult, ALU.add).then_inc(s["scan"], 1)
                    if r in (4, 5, 6):
                        q = 2 * (K - 4 * PAIRS) + b
                        wait(dve, "scan", G)
                        wait(dve, "e_self_T", q)
                        v.tensor_tensor(run_self[b][:, :], ps["r"][:, 0:C], run[b][:, :], ALU.add
                                        ).then_inc(s["self_add"], 1)

                def z_stats(b):
                    if first_half:
                        n = 2 * K + b
                        wait(dve, "z_sb", n)
                        q = Steps(dve, s["z_step"], 2 * J - 1, n)
                        stats(q, z_sb[b], z_st[b], z_mv[b]).then_inc(s["z_var"], 1)
                        q.end()

                def x2_rows(b):
                    if first_half:
                        n = 2 * K + b
                        if second_half:
                            wait(dve, "x2_T", m + b)
                            wait(dve, "v_rdy", m + b)
                        if second_half == SRC:
                            wait_dma(dve, put_loc[b], K, 4 * LOAD)
                        wait(dve, "z_std", n)
                        v.reciprocal(z_rs[b][:, :], z_sd[b][:, :]).then_inc(s["z_step2"], 1)
                        dve.wait_ge(s["z_step2"], n + 1)
                        normed(x2[b], z_sb[b], z_mv[b], z_rs[b]).then_inc(s["x2_rdy"], 1)

                def u_rows(b):
                    if second_half:
                        n = m + b
                        q = Steps(dve, s["u_step"], 2 * J, n)
                        wait(dve, "x_out_rdy", n - 2)
                        wait(dve, "x2_rdy", n)
                        wait(dve, "h3_relu", n)
                        v.scalar_tensor_tensor(out=flat(v_sb[b]), in0=ps["h3"][0:P, :], scalar=SLOPE,
                                               in1=flat(x2[b]), op0=ALU.mult, op1=ALU.add
                                               ).then_inc(s["v_rdy"], 1)
                        wait(dve, "v_rdy", n)
                        q.then(v.tensor_tensor(flat(v_sb[b]), flat(v_sb[b]), flat(h3r[b]), ALU.add))
                        stats(q, v_sb[b], u_st[b], u_mv[b]).then_inc(s["u_var"], 1)
                        q.end()

                def u_scale(b):
                    if second_half:
                        n = m + b
                        wait(dve, "u_std", n)
                        v.reciprocal(u_rs[b][:, :], u_sd[b][:, :]).then_inc(s["u_step2"], 1)
                        dve.wait_ge(s["u_step2"], n + 1)
                        v.scalar_tensor_tensor(out=u_nb[b][:, :], in0=u_mv[b][:, :, 0], scalar=-1.0,
                                               in1=u_rs[b][:, :], op0=ALU.mult, op1=ALU.mult
                                               ).then_inc(s["u_scl"], 1)

                def edge_rows_1(b):
                    G, g = 2 * K + b, 2 * k + b
                    if r in (4, 5, 6):
                        n = 2 * (K - 4 * PAIRS) + b
                        wait(dve, "e_scaled", n)
                        wait(dve, "e_rdy", G - 2)
                        v.tensor_tensor(e2[b][:, :, :], e1[b][:, :, :], b4(b_row[r - 3][0:P, :]), ALU.add
                                        ).then_inc(s["e_biased"], 1)
                        return
                    wait(dve, "e_rows", G)
                    if r in (1, 2):
                        wait_dma(dve, put_e[b], K, LOAD)
                        v.tensor_tensor(e_out[b][:, :, :], rows("r"), bc(cols("rcnt", g)), ALU.mult
                                        ).then_inc(s["e_rdy"], 1)
                        return
                    if r == 0:
                        q = Steps(dve, s["step0"], 2 * J, g)
                        q.then(v.tensor_tensor(e1[b][:, :, :], rows("e"), bc(cols("rcnt", g)), ALU.mult))
                        v.tensor_tensor(e2[b][:, :, :], rows("r"), e1[b][:, :, :], ALU.add
                                        ).then_inc(s["e_ps_free"], 1)
                        wait(dve, "e_ps_free", G)
                        stats(q, e2[b], e_st[b], e_mv[b]).then_inc(s["e_var"], 1)
                        q.end()
                    if r == 3:
                        q = Steps(dve, s["step3"], 2 * J + 3, g)
                        v.tensor_tensor(e1[b][:, :, :], rows("r"), bc(cols("rcnt", g)), ALU.mult
                                        ).then_inc(s["e_ps_free"], 1)
                        wait_dma(dve, got_self[b], 3 * (k + 1), LOAD)
                        q.inc(v.tensor_tensor(e3[b][:, :, :], self_in[1][b][:, :, :], self_in[2][b][:, :, :], ALU.add))
                        wait(dve, "e_ps_free", 2 * PAIRS + g)
                        q.wait()
                        q.then(v.tensor_tensor(e1[b][:, :, :], e1[b][:, :, :], e3[b][:, :, :], ALU.add))
                        q.then(v.scalar_tensor_tensor(out=flat(e2[b]), in0=flat(self_in[0][b]), scalar=5.0,
                                                      in1=flat(e1[b]), op0=ALU.mult, op1=ALU.add))
                        q.then(stats(q, e2[b], e_st[b], e_mv[b]))
                        v.tensor_tensor(e_v[b][:, :], e_mv[b][:, :, 1], cols("cnt16", g), ALU.mult
                                        ).then_inc(s["e_var"], 1)
                        q.end()
                    if r == 7:
                        q = Steps(dve, s["step7"], 2 * J + 2, g)
                        wait(dve, "e_w", 2 * g + 1)
                        v.tensor_tensor(e2[b][:, :, :], rows("r"), e1[b][:, :, :], ALU.add
                                        ).then_inc(s["e_ps_free"], 1)
                        wait(dve, "e_ps_free", 4 * PAIRS + g)
                        q.then(v.scalar_tensor_tensor(out=flat(e1[b]), in0=flat(e2[b]), scalar=SLOPE,
                                                      in1=flat(e2[b]), op0=ALU.mult, op1=ALU.max))
                        q.then(v.tensor_tensor(e2[b][:, :, :], e1[b][:, :, :], e3[b][:, :, :], ALU.add))
                        q.then(stats(q, e2[b], e_st[b], e_mv[b]))
                        v.tensor_tensor(e_v[b][:, :], e_mv[b][:, :, 1], cols("e7", g), ALU.mult
                                        ).then_inc(s["e_var"], 1)
                        q.end()

                def edge_rows_2(b):
                    if r not in (0, 3, 7):
                        return
                    g = 2 * k + b
                    nth = {0: 0, 3: 1, 7: 2}[r] * 2 * PAIRS + g
                    wait(dve, "e_std", nth)
                    v.reciprocal(e_rs[b][:, :], e_sd[b][:, :]).then_inc(s["e_vv"], 1)
                    dve.wait_ge(s["e_vv"], 2 * nth + 1)
                    v.tensor_tensor(e_sc[b][:, :], e_rs[b][:, :], cols({0: "dv1", 3: "c3", 7: "f7"}[r], g),
                                    ALU.mult).then_inc(s["e_vv"], 1)
                    wait_dma(dve, put_e[b], K, LOAD)
                    dve.wait_ge(s["e_vv"], 2 * nth + 2)
                    normed(e_out[b], e2[b], e_mv[b], e_sc[b]).then_inc(s["e_rdy"], 1)

                def radial_in(b):
                    g = 2 * k + b
                    if r == 5:
                        wait(dve, "rad_sq", g - 2)
                        wait_dma(dve, got_ew[b], k + 1, 16)
                        v.tensor_scalar(rad_in[b], length[b], 0.0, 1.0, ALU.max, ALU.min
                                        ).then_inc(s["rad_x"], 1)

                def radial_out(b):
                    g = 2 * k + b
                    if r == 5:
                        wait_dma(dve, put_rad[b], k, 16)
                        wait(dve, "rad_exp", g)
                        v.scalar_tensor_tensor(out=rad_emb[b], in0=length[b], scalar=1.0,
                                               in1=rad_gauss[b], op0=ALU.is_le, op1=ALU.mult
                                               ).then_inc(s["rad_rdy"], 1)
                    if r == 6:
                        wait_dma(dve, put_w[b], k, LOAD)
                        wait(dve, "m3_ps", g)
                        v.tensor_copy(w_rows[b], rows("h3")).then_inc(s["m3_sb"], 1)

                if r == 6 and isinstance(k, int):
                    for b in range(2):
                        v.memset(work[b][HID:HID + 1, 2, :], 1.0).then_inc(s["rad_one"], 1)
                A, B = 0, 1
                scan(A)
                radial_in(A)
                z_stats(A)
                edge_rows_1(A)
                radial_in(B)
                scan(B)
                edge_rows_2(A)
                z_stats(B)
                radial_out(A)
                u_rows(A)
                edge_rows_1(B)
                u_scale(A)
                x2_rows(A)
                edge_rows_2(B)
                radial_out(B)
                u_rows(B)
                u_scale(B)
                x2_rows(B)

            rounds(dve, body)

            def body8(k):
                for b in range(2):
                    g = 2 * k + b
                    q = Steps(dve, s["msg_step"], 7, g)
                    up = rows("r")
                    vec = up[:, :, MUL:4 * MUL].rearrange("p j (c m) -> p j c m", c=3)
                    w = self_in[1][b]
                    yu = y_unit[:, bass.ds(g * J, J), :].unsqueeze(3).to_broadcast([P, J, 3, MUL])
                    ys = y1[:, bass.ds(g * J, J), :].unsqueeze(3).to_broadcast([P, J, 3, MUL])

                    def over_c(x):
                        return x.unsqueeze(2).to_broadcast([P, J, 3, MUL])

                    wait(dve, "mid_T", g - 2)
                    wait_dma(dve, got_w[b], k + 1, LOAD)
                    wait(dve, "up_ps", g)
                    q.inc(v.tensor_tensor(mid[b][:, :, 0:MUL], up[:, :, 0:MUL], w[:, :, 0:MUL], ALU.mult))
                    q.inc(v.tensor_tensor(w1s[b], up[:, :, 0:MUL], w[:, :, MUL:2 * MUL], ALU.mult))
                    q.inc(v.tensor_tensor(mid[b][:, :, 5 * MUL:8 * MUL].rearrange("p j (c m) -> p j c m", c=3),
                                          vec, over_c(w[:, :, 2 * MUL:3 * MUL]), ALU.mult))
                    q.then(v.tensor_tensor(vy[b], vec, yu, ALU.mult))
                    q.inc(v.tensor_tensor(mid[b][:, :, MUL:4 * MUL].rearrange("p j (c m) -> p j c m", c=3),
                                          over_c(w1s[b]), ys, ALU.mult))
                    q.then(v.tensor_tensor(vsum[0][b], vy[b][:, :, 0, :], vy[b][:, :, 1, :], ALU.add))
                    q.then(v.tensor_tensor(vsum[1][b], vsum[0][b], vy[b][:, :, 2, :], ALU.add))
                    q.end()
                    v.tensor_tensor(mid[b][:, :, 4 * MUL:5 * MUL], vsum[1][b], w[:, :, 3 * MUL:4 * MUL],
                                    ALU.mult).then_inc(s["msg"], 1)
                for b in range(2):
                    g = 2 * k + b
                    wait(dve, "msgo_ps", g)
                    wait(dve, "run_T", g - 2)
                    wait(dve, "scan", 16 * PAIRS + g - 1)
                    v.tensor_tensor_scan(run[b][:, :], mask[:, bass.ds(g * C, C)], ps["xT"][:, 0:C],
                                         run[1 - b][:, C - 1:C], ALU.mult, ALU.add).then_inc(s["scan"], 1)
                for b in range(2):
                    g = 2 * k + b
                    q = Steps(dve, s["step8"], 2 * J - 1, g)
                    wait_dma(dve, got_self[b], 8 * PAIRS + k + 1, LOAD)
                    wait(dve, "run_T", g)
                    v.tensor_tensor(e2[b][:, :, :], rows("z"), self_in[0][b][:, :, :], ALU.add
                                    ).then_inc(s["e_ps_free"], 1)
                    wait(dve, "e_ps_free", 6 * PAIRS + g)
                    stats(q, e2[b], e_st[b], e_mv[b]).then_inc(s["e_var"], 1)
                    q.end()
                for b in range(2):
                    g = 2 * k + b
                    wait(dve, "e_std", 6 * PAIRS + g)
                    v.reciprocal(e_rs[b][:, :], e_sd[b][:, :]).then_inc(s["e_vv"], 1)
                    wait_dma(dve, put_fin[b], k, 16 * J)
                    dve.wait_ge(s["e_vv"], 12 * PAIRS + g + 1)
                    normed(e_out[b], e2[b], e_mv[b], e_rs[b]).then_inc(s["e_rdy"], 1)
            body8(0)
            with dve.Fori(1, PAIRS) as k:
                body8(k)


def kernel(x, src, dst, edge_attr_3, edge_weight, L0_gnn_W, L0_gnn_b, L2_gnn_W1, L2_gnn_b1, L2_gnn_W2,
           L2_gnn_b2, L2_gnn_W3, L2_gnn_b3, L3_gnn_W_up0, L3_gnn_W_up1, L3_gnn_mlp_w0, L3_gnn_mlp_b0,
           L3_gnn_mlp_w1, L3_gnn_mlp_b1, L3_gnn_mlp_w2, L3_gnn_mlp_b2, L3_gnn_W_out0, L3_gnn_W_out1):
    import numpy as _np
    import concourse.bacc as _bacc
    from concourse import mybir as _mybir
    from concourse.bass_utils import run_bass_kernel_spmd as _run

    src, dst = _np.asarray(src), _np.asarray(dst)
    none = _np.full(1, -1, dst.dtype)
    dst_ext = _np.concatenate([none, dst, none])
    by_tile = lambda v: _np.ascontiguousarray(v.reshape(T, P).T)
    arrays = {
        "x": x, "src": src, "dst_ext": dst_ext, "src_pt": by_tile(src), "dst_pt": by_tile(dst),
        "next_pt": by_tile(dst_ext[2:]),
        "attr_pt": _np.ascontiguousarray(_np.asarray(edge_attr_3).reshape(T, P, 3).transpose(1, 0, 2)),
        "edge_weight": edge_weight, "W_sage": L0_gnn_W, "b_sage": L0_gnn_b, "W1": L2_gnn_W1,
        "b1": L2_gnn_b1, "W2": L2_gnn_W2, "b2": L2_gnn_b2, "W3": L2_gnn_W3, "b3": L2_gnn_b3,
        "W_up0": L3_gnn_W_up0, "W_up1": L3_gnn_W_up1, "mlp_w0": L3_gnn_mlp_w0,
        "mlp_b0": L3_gnn_mlp_b0, "mlp_w1": L3_gnn_mlp_w1, "mlp_b1": L3_gnn_mlp_b1,
        "mlp_w2": L3_gnn_mlp_w2, "mlp_b2": L3_gnn_mlp_b2, "W_out0": L3_gnn_W_out0,
        "W_out1": L3_gnn_W_out1,
    }
    nc = _bacc.Bacc("TRN2", target_bir_lowering=False, num_devices=1)
    held, args = {}, {}
    for name, v in arrays.items():
        v = _np.ascontiguousarray(v)
        held[f"in_{name}_dram"] = v
        args[name] = nc.dram_tensor(f"in_{name}_dram", v.shape, _mybir.dt.from_np(v.dtype),
                                    kind="ExternalInput").ap()
    out = nc.dram_tensor("out_0_dram", (N, D), _mybir.dt.float32, kind="ExternalOutput").ap()
    gnn_kernel(nc, args, out)
    r = _run(nc, [held], core_ids=[0])
    return r.results[0]["out_0_dram"]
```

```python
from contextlib import ExitStack

import concourse.bass as bass
from concourse import mybir

F32 = mybir.dt.float32
BF16 = mybir.dt.bfloat16
I32 = mybir.dt.int32
ALU = mybir.AluOpType
ACT = mybir.ActivationFunctionType
AX_X = mybir.AxisListType.X

N, E, D = 100000, 25000, 128
P = 125
J = 4
C = P * J
T = E // P
PAIRS = E // (2 * C)
NODE_PAIRS = N // (2 * C)
ROUNDS = 9
TK = T // 2
EPS = 1e-5
MUL = 32
NB = 8
HID = 64
SLOPE = 0.01
ALPHA = 0.2
SPLIT = ((0, 112), (112, P))
LOAD = 16 * len(SPLIT)
SRC, NODE = "source rows", "node rows"
A12, B12 = (1.5625 + EPS) / 1.5625, EPS * EPS / 1.5625
A34, B34 = 1.0 + EPS, EPS * EPS


class Steps:

    def __init__(self, eng, sem, per, index):
        self.eng, self.sem, self.per, self.index, self.n = eng, sem, per, index, 0

    def inc(self, ins):
        self.n += 1
        ins.then_inc(self.sem, 1)

    def wait(self):
        self.eng.wait_ge(self.sem, self.index * self.per + self.n)

    def so_far(self):
        return self.index * self.per + self.n

    def then(self, ins):
        self.inc(ins)
        self.wait()

    def end(self):
        assert self.n == self.per, f"{self.n} steps, not {self.per}"


def gnn_kernel(nc, a, out):
    with ExitStack() as ctx:
        def sb(name, shape, dt=F32):
            return ctx.enter_context(nc.sbuf_tensor(name, shape, dt))

        def sem(name):
            return ctx.enter_context(nc.semaphore(name))

        def dram(name, shape):
            return nc.dram_tensor(name, shape, F32, kind="Internal").ap()

        def pair_of(name, shape, dt=F32):
            return [sb(f"{name}_{b}", shape, dt) for b in range(2)]

        def pair_sem(name):
            return [sem(f"{name}_{b}") for b in range(2)]

        table = [dram(f"table{r}", (E + 1 if r < 3 else 2 * E, D)) for r in range(8)]
        radial = dram("radial", (2 * PAIRS, NB, C))
        edge_w = dram("edge_w", (E, D))

        mask = sb("mask", [128, E], BF16)
        ident = sb("ident", [128, 128])
        ones = sb("ones", [128, C])
        zero_row = sb("zero_row", [1, D])
        src_i = sb("src_i", [P, T], I32)
        dst_i = sb("dst_i", [P, T], I32)
        next_i = sb("next_i", [P, T], I32)
        slot_or_zero = sb("slot_or_zero", [P, T], I32)
        slot_or_local = sb("slot_or_local", [P, T], I32)
        out_row = sb("out_row", [P, T], I32)
        names = ("srcp1 j1 tile1 cnt sq1 dv1 rcnt deg dv2 cnt16 c3 c7 d7 e7 f7 dstf tmpa tmpb own").split()
        col = {n: sb(f"col_{n}", [P, T]) for n in names}
        attr = sb("attr", [P, T, 3])
        y_unit = sb("y_unit", [P, T, 3])
        y1 = sb("y1", [P, T, 3])
        iota1 = sb("iota1", [P, P])
        dst_tile = sb("dst_tile", [TK, 2, 2, P], I32)
        dst_next = sb("dst_next", [TK, 2, 2, P], I32)
        tf = sb("tf", [TK, 2, 2, P])
        tl = sb("tl", [TK, 2, 2, P])
        diff = sb("diff", [TK, 2, P + 1])
        first = sb("first", [TK, 2])
        w_up = sb("w_up", [128, 128])
        w_sage_self = sb("w_sage_self", [128, 128])
        w_sage_neigh = sb("w_sage_neigh", [128, 128])
        w_gcn = [sb(f"w_gcn{i}", [128, 128]) for i in range(3)]
        b_col = sb("b_col", [128, 2])
        b_row = [sb(f"b_row{i}", [128, 128]) for i in range(4)]
        b_rest = sb("b_rest", [128, 128])
        b_part = sb("b_part", [128, 128], BF16)
        b_wide = [sb(f"b_wide{i}", [96, J * 128], BF16) for i in range(2)]
        pick3 = sb("pick3", [96, 128], BF16)
        wo_in = sb("wo_in", [128, 64])
        w_out = [sb(f"w_out{i}", [128, 128]) for i in range(2)]
        mw0 = sb("mw0", [NB, HID])
        mw1 = sb("mw1", [HID, HID])
        mw2 = sb("mw2", [HID + 1, D])
        mb = sb("mb", [HID, 2])
        centre = sb("centre", [NB, 1])
        eps_col = sb("eps_col", [128, 3])

        iw = pair_of("iw", [P, 2 * J], I32)
        g_src = pair_of("g_src", [P, J, D])
        g_dst = pair_of("g_dst", [P, J, D])
        x_in = pair_of("x_in", [P, J, D])
        xT = pair_of("xT", [128, C])
        z_sb = pair_of("z_sb", [P, J, D])
        z_st = pair_of("z_st", [P, J, 6])
        z_mv = pair_of("z_mv", [P, J, 2])
        z_sd = pair_of("z_sd", [P, J])
        z_rs = pair_of("z_rs", [P, J])
        x2 = [pair_of(f"x2_{q}", [P, J, D]) for q in range(2)]
        x2T = pair_of("x2T", [128, C])
        h1T = pair_of("h1T", [128, C])
        h2T = pair_of("h2T", [128, C])
        h3r = pair_of("h3r", [P, J, D])
        v_sb = pair_of("v_sb", [P, J, D])
        u_st = pair_of("u_st", [P, J, 6])
        u_mv = pair_of("u_mv", [P, J, 2])
        u_sd = pair_of("u_sd", [P, J])
        u_rs = pair_of("u_rs", [P, J])
        u_nb = pair_of("u_nb", [P, J])
        x_out = pair_of("x_out", [P, J, D])
        loc = [pair_of(f"loc{i}", [P, J, D]) for i in range(3)]
        run = pair_of("run", [128, C])
        xdT = pair_of("xdT", [128, C])
        run_self = xdT
        self_in = [g_dst, loc[1], loc[2]]
        e1 = pair_of("e1", [P, J, D])
        e2 = pair_of("e2", [P, J, D])
        e3 = loc[0]
        e_st = pair_of("e_st", [P, J, 6])
        e_mv = pair_of("e_mv", [P, J, 2])
        e_v = pair_of("e_v", [P, J])
        e_sd = pair_of("e_sd", [P, J])
        e_rs = pair_of("e_rs", [P, J])
        e_sc = pair_of("e_sc", [P, J])
        e_out = pair_of("e_out", [P, J, D])
        work = pair_of("work", [128, 5, 512])
        ow = pair_of("ow", [P, J], I32)
        dst_wide = [work[b][:, 0, 0:C + 1].bitcast(I32) for b in range(2)]
        src_wide = [work[b][0:TK, 1, 0:C].bitcast(I32) for b in range(2)]
        step_u = [[work[b][0:TK, 2 + h, 0:C] for b in range(2)] for h in range(2)]
        cnt_row = [work[b][:, 4, 0:C] for b in range(2)]
        found = sb("found", [P, J, P])
        length = [work[b][0:NB, 0, 0:C] for b in range(2)]
        rad_in = [work[b][0:NB, 1, 0:C] for b in range(2)]
        rad_square = [work[b][0:NB, 2, 0:C] for b in range(2)]
        rad_gauss = [work[b][0:NB, 3, 0:C] for b in range(2)]
        rad_emb = [work[b][0:NB, 4, 0:C] for b in range(2)]
        emb_in = [work[b][0:NB, 0, 0:C] for b in range(2)]
        hid1 = [work[b][0:HID, 1, 0:C] for b in range(2)]
        hid2 = [work[b][0:HID + 1, 2, 0:C] for b in range(2)]
        w_rows = [work[b][0:P, 3, :].rearrange("p (j d) -> p j d", j=J) for b in range(2)]
        mid = [work[b][0:P, 0:2, :].rearrange("p q (j d) -> p (q j) d", j=J // 2) for b in range(2)]
        w1s = [work[b][0:P, 2, 0:J * MUL].rearrange("p (j m) -> p j m", j=J) for b in range(2)]
        vy = [work[b][0:P, 3, 0:J * 3 * MUL].rearrange("p (j c m) -> p j c m", j=J, c=3) for b in range(2)]
        vsum = [[work[b][0:P, 4, q * J * MUL:(q + 1) * J * MUL].rearrange("p (j m) -> p j m", j=J)
                 for b in range(2)] for q in range(2)]
        ps = {n: ctx.enter_context(nc.psum_tensor(f"ps_{n}", [128, 512], F32))
              for n in ("xT", "z", "x2T", "h1", "h2", "h3", "e", "r")}

        def rows(name):
            return ps[name][0:P, 0:J * D].rearrange("p (j d) -> p j d", j=J)

        def flat(t):
            return t[:, :, :].rearrange("p j d -> p (j d)")

        s = {n: sem(n) for n in (
            "setup_in setup_pool setup_dve setup_act setup_out cols "
            "p_mask p_count p_step p_find p_found "
            "x_T x_T_sb z_ps z_sb z_var z_std x2_rdy x2_T x2_T_sb h1_ps h1_sb h2_ps h2_sb h3_ps h3_relu "
            "u_step z_step z_step2 u_step2 ow_rdy rad_one u_var u_std u_scl x_out_rdy loc1_ps loc1_sb loc2_ps loc2_sb loc3_sb v_rdy "
            "e_T e_self_T e_dT_sb scan self_add e_rows e_ps_free e_var e_std e_rdy e_scaled e_biased e_w e_vv "
            "step0 step3 step7 step8 "
            "rad_sq rad_x rad_exp rad_m rad_rdy m1_ps m1_sb m2_ps m2_sb m3_ps m3_sb "
            "xg_T xg_sb up_ps msg msg_step mid_T mid_sb1 mid_sb2 msgo_ps run_T idx"
        ).split()}
        got_src = pair_sem("got_src")
        got_dst = pair_sem("got_dst")
        got_x = pair_sem("got_x")
        got_self = pair_sem("got_self")
        got_prep = pair_sem("got_prep")
        got_ew = pair_sem("got_ew")
        got_rad = pair_sem("got_rad")
        got_w = pair_sem("got_w")
        put_e = pair_sem("put_e")
        put_x = pair_sem("put_x")
        put_loc = pair_sem("put_loc")
        put_l3 = pair_sem("put_l3")
        put_rad = pair_sem("put_rad")
        put_w = pair_sem("put_w")
        put_fin = pair_sem("put_fin")

        def wait_own(eng, sm, value):
            if isinstance(value, int):
                eng.wait_ge(sm, value)
                return
            held = eng.to_reg(value)
            eng.wait_ge(s["cols"], 1)
            eng.wait_ge(sm, held)

        def wait(eng, name, index, sep=False):
            if isinstance(index, int) and index < 0:
                return
            (wait_own if sep else lambda e, x, v: e.wait_ge(x, v))(eng, s[name], index + 1)

        def wait_dma(eng, sm, times, each, sep=False):
            if isinstance(times, int) and times <= 0:
                return
            (wait_own if sep else lambda e, x, v: e.wait_ge(x, v))(eng, sm, times * each)

        def bc(x, n=D):
            return x.unsqueeze(2).to_broadcast([x.shape[0], x.shape[1], n])

        def cols(name, g):
            return col[name][:, bass.ds(g * J, J)]

        def b4(x):
            return x.unsqueeze(1).to_broadcast([x.shape[0], J, x.shape[1]])

        def edge_rows(t, g, base=0):
            return t[bass.ds(g * C + base, C), :].rearrange("(j p) d -> p j d", p=P)

        def node_rows(t, g):
            return t[bass.ds(g * C, C), :].rearrange("(p j) d -> p j d", j=J)

        def transfer(eng, dst, src, sm):
            for lo, hi in SPLIT:
                eng.dma_start(dst[lo:hi], src[lo:hi]).then_inc(sm, 16)

        FREED = {0: 0, 3: 1, 7: 2, 8: 3}
        CHAIN = {0: 0, 1: 1, 2: 2, 4: 3, 5: 4, 6: 5}
        PEELED = {0: 3, 1: 3, 6: 2}

        class Parts:

            def __init__(self, r, k, like=None):
                at = CHAIN.get(r)
                self.K = None if at is None else at * PAIRS + k
                of = None if at is None else at * PAIRS + (k if like is None else like)
                self.first, self.second, self.third = (
                    None if of is None or not 0 <= of - i < PAIRS + NODE_PAIRS
                    else SRC if of - i < PAIRS else NODE for i in range(3))
                self.parity = None if of is None else of % 2
                self.old = None if of is None or of - 2 < 0 else SRC if of - 2 < PAIRS else NODE

        def rounds(eng, body):
            for r in range(ROUNDS - 1):
                peeled = PEELED.get(r, 1)
                by = 2 if r in CHAIN and r != 6 else 1
                for k in range(peeled):
                    body(r, k, Parts(r, k))
                with eng.Fori(0, (PAIRS - peeled) // by) as step:
                    for i in range(by):
                        k = step * by + (peeled + i)
                        body(r, k, Parts(r, k, peeled + i))

        block = ctx.enter_context(nc.Block())
        n_setup_in = [0]

        @block.sync
        def _(sp):
            def setup(dst, src):
                sp.dma_start(dst, src).then_inc(s["setup_in"], 16)
                n_setup_in[0] += 16

            setup(src_i[:, :], a["src_pt"])
            setup(dst_i[:, :], a["dst_pt"])
            setup(next_i[:, :], a["next_pt"])
            setup(attr[:, :, :], a["attr_pt"])
            tiles = a["dst_ext"][1:1 + E].rearrange("(t p) -> t p", p=P)
            nexts = a["dst_ext"][2:2 + E].rearrange("(t p) -> t p", p=P)
            for h in range(2):
                setup(dst_tile[:, h, 1, :], tiles[h * TK:(h + 1) * TK, :])
                setup(dst_next[:, h, 1, :], nexts[h * TK:(h + 1) * TK, :])
                lo = 1 if h == 0 else 0
                setup(dst_tile[lo:TK, h, 0, :], tiles[h * TK + lo - 1:(h + 1) * TK - 1, :])
                setup(dst_next[lo:TK, h, 0, :], nexts[h * TK + lo - 1:(h + 1) * TK - 1, :])
            setup(w_sage_self[:, :], a["W_sage"][0:D, :])
            setup(w_sage_neigh[:, :], a["W_sage"][D:2 * D, :])
            for i in range(3):
                setup(w_gcn[i][:, :], a[f"W{i + 1}"])
            for i in range(2):
                setup(b_col[:, i:i + 1], a[f"b{i + 1}"].rearrange("(p o) -> p o", o=1))
            for i, n in enumerate(("b_sage", "b1", "b2", "b3")):
                setup(b_row[i][:, :], a[n].unsqueeze(0).to_broadcast([128, D]))
            for i in range(2):
                setup(wo_in[0:MUL, i * MUL:(i + 1) * MUL], a["W_out0"][i * MUL:(i + 1) * MUL, :])
                for c in range(3):
                    setup(wo_in[MUL * (c + 1):MUL * (c + 2), i * MUL:(i + 1) * MUL],
                          a["W_out1"][i * MUL:(i + 1) * MUL, :])
            setup(mw0[:, :], a["mlp_w0"])
            setup(mw1[:, :], a["mlp_w1"])
            setup(mw2[0:HID, :], a["mlp_w2"])
            setup(mw2[HID:HID + 1, :], a["mlp_b2"].unsqueeze(0))
            for i in range(2):
                setup(mb[:, i:i + 1], a[f"mlp_b{i}"].rearrange("(p o) -> p o", o=1))
            sp.wait_ge(s["setup_dve"], 2)
            for r in range(3):
                sp.dma_start(table[r][E:E + 1, :], zero_row[:, :]).then_inc(s["setup_out"], 16)
            sp.dma_start(w_up[0:MUL, 0:MUL], a["W_up0"]).then_inc(s["setup_out"], 16)
            for c in range(3):
                sp.dma_start(w_up[MUL + c:MUL + c + 3 * (MUL - 1) + 1:3, MUL * (c + 1):MUL * (c + 2)],
                             a["W_up1"]).then_inc(s["setup_out"], 16)

            def prep_load(k, b):
                g = 2 * k + b
                if not isinstance(k, int):
                    wait_own(sp, s["p_mask"], 3 * g - 3)
                sp.dma_start(dst_wide[b], a["dst_ext"][bass.ds(g * C, C + 1)].unsqueeze(0)
                             .to_broadcast([128, C + 1])).then_inc(got_prep[b], 16)
                sp.dma_start(src_wide[b], a["src"][bass.ds(g * C, C)].unsqueeze(0)
                             .to_broadcast([TK, C])).then_inc(got_prep[b], 16)
            for b in range(2):
                prep_load(0, b)
            with sp.Fori(1, PAIRS) as k:
                for b in range(2):
                    prep_load(k, b)

            selfs = {3: (0, 1, 2), 4: (3,), 5: (4,), 6: (5,), 7: (6, 3)}

            def loads(r, k, part):
                for b in range(2):
                    g = 2 * k + b
                    if part.first == NODE:
                        wait(sp, "x_T", 2 * part.K + b - 2, sep=True)
                        transfer(sp, x_in[b][:, :, :], node_rows(a["x"], 2 * (part.K - PAIRS) + b), got_x[b])
                    if r in selfs:
                        wait(sp, "e_rdy", 2 * (r * PAIRS + k) + b - 2, sep=True)
                        for i, t in enumerate(selfs[r]):
                            transfer(sp, self_in[i][b][:, :, :], edge_rows(table[t], g), got_self[b])
                    if r == 3:
                        wait(sp, "rad_rdy", g - 2, sep=True)
                        sp.dma_start(length[b], a["edge_weight"][bass.ds(g * C, C)].unsqueeze(0)
                                     .to_broadcast([NB, C])).then_inc(got_ew[b], 16)
                    if r == 6:
                        wait(sp, "m1_ps", g - 2, sep=True)
                        sp.dma_start(emb_in[b], radial[bass.ds(g, 1)].rearrange("o n c -> (o n) c")
                                     ).then_inc(got_rad[b], 16)

            def stores(r, k, part):
                for b in range(2):
                    g = 2 * k + b
                    if part.third == SRC:
                        t = 2 * (part.K - 2) + b
                        wait(sp, "loc3_sb", t, sep=True)
                        transfer(sp, edge_rows(table[6], t, E), loc[2][b][:, :, :], put_l3[b])
                    if part.third:
                        t = 2 * (part.K - 2) + b
                        wait(sp, "x_out_rdy", t, sep=True)
                        to = edge_rows(table[7], t, E) if part.third == SRC else node_rows(out, t - 2 * PAIRS)
                        transfer(sp, to, x_out[b][:, :, :], put_x[b])
                    if part.second == SRC:
                        m = 2 * (part.K - 1) + b
                        for nm in ("x2_rdy", "loc1_sb", "loc2_sb"):
                            wait(sp, nm, m, sep=True)
                        for t, buf in ((3, x2[1 - part.parity][b]), (4, loc[0][b]), (5, loc[1][b])):
                            transfer(sp, edge_rows(table[t], m, E), buf[:, :, :], put_loc[b])
                    wait(sp, "e_rdy", 2 * (r * PAIRS + k) + b, sep=True)
                    transfer(sp, edge_rows(table[r], g), e_out[b][:, :, :], put_e[b])
                    if r == 3:
                        wait(sp, "rad_rdy", g, sep=True)
                        sp.dma_start(radial[bass.ds(g, 1)].rearrange("o n c -> (o n) c"), rad_emb[b]
                                     ).then_inc(put_rad[b], 16)
                    if r == 6:
                        wait(sp, "m3_sb", g, sep=True)
                        transfer(sp, edge_rows(edge_w, g), w_rows[b], put_w[b])

            for r in range(ROUNDS - 1):
                if r:
                    for b in range(2):
                        sp.wait_ge(put_e[b], LOAD * PAIRS * r)
                        if r == 3:
                            sp.wait_ge(put_loc[b], 3 * LOAD * PAIRS)
                            sp.wait_ge(put_l3[b], LOAD * PAIRS)
                        if r == 6:
                            sp.wait_ge(put_rad[b], 16 * PAIRS)
                peeled = PEELED.get(r, 1)
                by = 2 if r in CHAIN and r != 6 else 1
                loads(r, 0, Parts(r, 0))
                for k in range(1, peeled + 1):
                    loads(r, k, Parts(r, k))
                    stores(r, k - 1, Parts(r, k - 1))
                left = 1 if by == 1 else 2
                with sp.Fori(0, (PAIRS - left - peeled) // by) as step:
                    for i in range(by):
                        k = step * by + (peeled + i)
                        loads(r, k + 1, Parts(r, k + 1, peeled + i + 1))
                        stores(r, k, Parts(r, k, peeled + i))
                for k in range(PAIRS - left, PAIRS):
                    if k + 1 < PAIRS:
                        loads(r, k + 1, Parts(r, k + 1))
                    stores(r, k, Parts(r, k))

            for b in range(2):
                sp.wait_ge(put_e[b], LOAD * PAIRS * (ROUNDS - 1))
                sp.wait_ge(put_w[b], LOAD * PAIRS)

            def loads8(k):
                for b in range(2):
                    if not (isinstance(k, int) and k >= PAIRS):
                        g = 2 * k + b
                        if not isinstance(k, int):
                            wait(sp, "msg", g - 2, sep=True)
                        transfer(sp, self_in[1][b][:, :, :], edge_rows(edge_w, g), got_w[b])
                    if not (isinstance(k, int) and k == 0):
                        g = 2 * k + b - 2
                        wait(sp, "e_ps_free", 6 * PAIRS + g - 2, sep=True)
                        transfer(sp, self_in[0][b][:, :, :], edge_rows(table[7], g), got_self[b])
            loads8(0)
            with sp.Fori(1, PAIRS) as k:
                loads8(k)
            loads8(PAIRS)
            for b in range(2):
                sp.wait_ge(put_x[b], LOAD * (PAIRS + NODE_PAIRS))
                sp.wait_ge(put_fin[b], 16 * J * PAIRS)

        @block.gpsimd
        def _(pool):
            pool.memset(ident[:, :], 0.0).then_inc(s["setup_pool"], 1)
            pool.iota(iota1[:, :], pattern=[[1, P]], base=1, channel_multiplier=0,
                      allow_small_or_imprecise_dtypes=True).then_inc(s["setup_pool"], 1)
            pool.iota(col["own"][:, :], pattern=[[P, T]], base=E, channel_multiplier=1,
                      allow_small_or_imprecise_dtypes=True).then_inc(s["setup_pool"], 1)
            pool.iota(centre[:, :], pattern=[[0, 1]], base=0, channel_multiplier=-1,
                      allow_small_or_imprecise_dtypes=True).then_inc(s["setup_pool"], 1)
            pool.wait_ge(s["setup_pool"], 4)
            pool.affine_select(out=ident[:, :], in_=ident[:, :], compare_op=ALU.not_equal, fill=1.0,
                               base=0, pattern=[[-1, 128]], channel_multiplier=1
                               ).then_inc(s["setup_pool"], 1)
            pool.wait_ge(s["setup_in"], n_setup_in[0])

            def gather(dst, src, index, sm):
                for j in range(J):
                    pool.indirect_dma_start(
                        out=dst[:, j, :], out_offset=None, in_=src,
                        in_offset=bass.IndirectOffsetOnAxis(ap=index[:, j:j + 1], axis=0)
                    ).then_inc(sm, 16)

            def body(r, k):
                for b in range(2):
                    G = 2 * (r * PAIRS + k) + b
                    t = (2 * k + b) * J
                    index = src_i if r == 0 else slot_or_zero if r < 4 else slot_or_local
                    if r == 0:
                        wait(pool, "x_T", G - 2, sep=True)
                    wait(pool, "e_T", G - 2, sep=True)
                    pool.tensor_copy(iw[b][:, 0:J], index[:, bass.ds(t, J)]).then_inc(s["idx"], 1)
                    pool.tensor_copy(iw[b][:, J:2 * J], dst_i[:, bass.ds(t, J)]).then_inc(s["idx"], 1)
                    wait_own(pool, s["idx"], 2 * (G + 1))
                    gather(g_src[b], a["x"] if r == 0 else table[r - 1], iw[b], got_src[b])
                    if r == 0:
                        gather(g_dst[b], a["x"], iw[b][:, J:2 * J], got_dst[b])

            for r in range(ROUNDS - 1):
                if r:
                    pool.wait_ge(s["cols"], 3)
                    pool.wait_ge(s["setup_out"], 7 * 16)
                    for b in range(2):
                        pool.wait_ge(put_e[b], LOAD * PAIRS * r)
                        if r >= 4:
                            pool.wait_ge(put_loc[b], 3 * LOAD * PAIRS)
                            pool.wait_ge(put_l3[b], LOAD * PAIRS)
                body(r, 0)
                with pool.Fori(1, PAIRS) as k:
                    body(r, k)

            for b in range(2):
                pool.wait_ge(put_e[b], LOAD * PAIRS * (ROUNDS - 1))
                pool.wait_ge(put_x[b], LOAD * (PAIRS + NODE_PAIRS))

            def gather8(k):
                for b in range(2):
                    g = 2 * k + b
                    wait(pool, "xg_T", g - 2, sep=True)
                    pool.tensor_copy(iw[b][:, 0:J], slot_or_local[:, bass.ds(g * J, J)]
                                     ).then_inc(s["idx"], 1)
                    wait_own(pool, s["idx"], 32 * PAIRS + g + 1)
                    gather(g_src[b], table[7], iw[b], got_src[b])

            def scatter8(k):
                for b in range(2):
                    g = 2 * k + b
                    wait_dma(pool, put_fin[b], k, 16 * J, sep=True)
                    pool.tensor_copy(ow[b][:, :], out_row[:, bass.ds(g * J, J)]).then_inc(s["ow_rdy"], 1)
                    wait_own(pool, s["ow_rdy"], g + 1)
                    wait(pool, "e_rdy", 2 * (8 * PAIRS + k) + b, sep=True)
                    for j in range(J):
                        pool.indirect_dma_start(
                            out=out, out_offset=bass.IndirectOffsetOnAxis(ap=ow[b][:, j:j + 1], axis=0),
                            in_=e_out[b][:, j, :], in_offset=None, bounds_check=N - 1,
                            oob_is_err=False).then_inc(put_fin[b], 16)
            for k in range(3):
                gather8(k)
            scatter8(0)
            with pool.Fori(3, PAIRS) as k:
                gather8(k)
                scatter8(k - 2)
            scatter8(PAIRS - 2)
            scatter8(PAIRS - 1)
            for b in range(2):
                pool.wait_ge(put_fin[b], 16 * J * PAIRS)

        @block.tensor
        def _(pe):
            mm = nc.tensor.matmul

            def to_cols(bank, src):
                for j in range(J):
                    i = nc.tensor.transpose(ps[bank][:, j * P:(j + 1) * P], src(j), ident[0:P, 0:P])
                return i

            def to_rows(bank, src):
                for j in range(J):
                    i = nc.tensor.transpose(rows(bank)[:, j, :], src[:, j * P:(j + 1) * P], ident[:, :])
                return i

            def by_rows(bank, lhs, w, bias=None):
                for j in range(J):
                    i = mm(rows(bank)[:, j, :], lhs[:, j * P:(j + 1) * P], w, start=(j == 0 if bias is not None else True),
                           stop=bias is None, skip_group_check=True)
                if bias is not None:
                    i = mm(ps[bank][0:P, 0:J * D], pick3[:, 0:P], b_wide[bias][:, :], start=False,
                           stop=True, skip_group_check=True)
                return i

            pe.wait_ge(s["setup_pool"], 5)
            pe.wait_ge(s["cols"], 1)
            def find(k):
                for b in range(2):
                    g = 2 * k + b
                    pe.wait_ge(s["p_mask"], 3 * g + 3)
                    pe.wait_ge(s["p_count"], g + 1)
                    if not (isinstance(k, int) and b == 0):
                        pe.wait_ge(s["p_found"], g)
                    fr = ps["e"][0:P, 0:J * (P + 1)].rearrange("p (j c) -> p j c", j=J)
                    for j in range(J):
                        for h in range(2):
                            mm(fr[:, j, :], step_u[h][b][:, j * P:(j + 1) * P], diff[:, h, :],
                               start=(h == 0), stop=(h == 1))
                    for j in range(J):
                        i = mm(ps["r"][0:P, j:j + 1], cnt_row[b][:, j * P:(j + 1) * P], ident[:, 0:1],
                               start=True, stop=True)
                    i.then_inc(s["p_find"], 1)
            find(0)
            with pe.Fori(1, PAIRS) as k:
                find(k)
            pe.wait_ge(s["p_found"], 2 * PAIRS)

            def body(r, k, part):
                K = r * PAIRS + k

                def edge_in(b):
                    G, g = 2 * K + b, 2 * k + b
                    if r == 0:
                        wait(pe, "e_ps_free", g - 1)
                        wait_dma(pe, got_dst[b], k + 1, 16 * J)
                        to_cols("e", lambda j: g_dst[b][:, j, :]).then_inc(s["e_T"], 1)
                        return
                    if r in (4, 5, 6):
                        wait(pe, "e_scaled", 2 * (K - 4 * PAIRS) + b - 1)
                    else:
                        wait(pe, "scan", G - 1)
                    wait_dma(pe, got_src[b], K + 1, 16 * J)
                    to_cols("e", lambda j: g_src[b][:, j, :]).then_inc(s["e_T"], 1)
                    if r in (4, 5, 6):
                        wait_dma(pe, got_self[b], 3 * PAIRS + (r - 4) * PAIRS + k + 1, LOAD)
                        to_cols("r", lambda j: self_in[0][b][:, j, :]).then_inc(s["e_self_T"], 1)

                def edge_out(b):
                    G, g = 2 * K + b, 2 * k + b
                    if r == 0:
                        wait(pe, "e_dT_sb", 2 * k + b)
                        by_rows("r", xdT[b], w_sage_self[:, :], bias=0)
                        wait(pe, "scan", G)
                        by_rows("e", run[b], w_sage_neigh[:, :]).then_inc(s["e_rows"], 1)
                    elif r in (4, 5, 6):
                        wait(pe, "self_add", 2 * (K - 4 * PAIRS) + b)
                        by_rows("e", run_self[b], w_gcn[r - 4][:, :]).then_inc(s["e_rows"], 1)
                    else:
                        if r in (1, 2):
                            wait(pe, "e_rdy", G - 1)
                        elif not (isinstance(k, int) and b == 0):
                            wait(pe, "e_ps_free", FREED[r] * 2 * PAIRS + g - 1)
                        wait(pe, "scan", G)
                        to_rows("r", run[b]).then_inc(s["e_rows"], 1)

                if part.K is not None:
                    n0, m0, t0 = 2 * part.K, 2 * (part.K - 1), 2 * (part.K - 2)

                def x_to_cols(b):
                    if not part.first:
                        return
                    n = n0 + b
                    wait(pe, "x_T_sb", n - 1)
                    if r == 0:
                        wait_dma(pe, got_src[b], k + 1, 16 * J)
                        to_cols("xT", lambda j: g_src[b][:, j, :]).then_inc(s["x_T"], 1)
                    else:
                        wait_dma(pe, got_x[b], part.K - PAIRS + 1, LOAD)
                        to_cols("xT", lambda j: x_in[b][:, j, :]).then_inc(s["x_T"], 1)

                def sage(b):
                    if not part.first:
                        return
                    n = n0 + b
                    wait(pe, "z_sb", n - 1)
                    wait(pe, "x_T_sb", n)
                    by_rows("z", xT[b], w_sage_self[:, :], bias=0).then_inc(s["z_ps"], 1)

                def x2_to_cols(b):
                    if not part.second:
                        return
                    m = m0 + b
                    wait(pe, "x2_T_sb", m - 1)
                    wait(pe, "x2_rdy", m)
                    to_cols("x2T", lambda j: x2[1 - part.parity][b][:, j, :]).then_inc(s["x2_T"], 1)

                def gcn1(b):
                    if not part.second:
                        return
                    m = m0 + b
                    wait(pe, "h1_sb", m - 1)
                    if r < 2:
                        wait(pe, "loc1_sb", m - 1 if part.second == SRC else 2 * PAIRS - 1)
                    wait(pe, "x2_T_sb", m)
                    mm(ps["h1"][:, 0:C], w_gcn[0][:, :], x2T[b][:, :], start=True, stop=True
                       ).then_inc(s["h1_ps"], 1)

                def gcn2(b):
                    if not part.second:
                        return
                    m = m0 + b
                    wait(pe, "h2_sb", m - 1)
                    if r < 2:
                        wait(pe, "loc2_sb", m - 1 if part.second == SRC else 2 * PAIRS - 1)
                    wait(pe, "h1_sb", m)
                    mm(ps["h2"][:, 0:C], w_gcn[1][:, :], h1T[b][:, :], start=True, stop=True
                       ).then_inc(s["h2_ps"], 1)

                def gcn3(b):
                    if not part.third:
                        return
                    t = t0 + b
                    wait(pe, "v_rdy", t - 1)
                    wait(pe, "h3_relu", t - 1)
                    if r == 6 and k == 1:
                        wait(pe, "m3_sb", 1)
                    wait(pe, "h2_sb", t)
                    by_rows("h3", h2T[b], w_gcn[2][:, :], bias=1).then_inc(s["h3_ps"], 1)

                def local_rows(b, i):
                    if part.second != SRC:
                        return
                    wait(pe, f"h{i}_sb", m0 + b)
                    to_rows(f"h{i}", (h1T, h2T)[i - 1][b]).then_inc(s[f"loc{i}_ps"], 1)

                last = 2 * (PAIRS + NODE_PAIRS) - 1

                def radial_1(b):
                    g = 2 * k + b
                    if r == 6:
                        wait(pe, "m1_sb", g - 1)
                        wait(pe, "h1_sb", last)
                        wait_dma(pe, got_rad[b], k + 1, 16)
                        mm(ps["h1"][0:HID, 0:C], mw0[:, :], emb_in[b], start=True, stop=True
                           ).then_inc(s["m1_ps"], 1)

                def radial_2(b):
                    g = 2 * k + b
                    if r == 6:
                        wait(pe, "m2_sb", g - 1)
                        wait(pe, "h2_sb", last)
                        wait(pe, "m1_sb", g, sep=True)
                        mm(ps["h2"][0:HID, 0:C], mw1[:, :], hid1[b], start=True, stop=True
                           ).then_inc(s["m2_ps"], 1)

                def radial_3(b):
                    g = 2 * k + b
                    if r == 6:
                        wait(pe, "m3_sb", g - 1)
                        wait(pe, "h3_relu", last - 2 if isinstance(k, int) and k == 0 else last)
                        wait(pe, "v_rdy", last - 2 if isinstance(k, int) and k == 0 else last)
                        wait(pe, "m2_sb", g)
                        pe.wait_ge(s["rad_one"], 2)
                        by_rows("h3", hid2[b], mw2[:, :]).then_inc(s["m3_ps"], 1)

                A, B = 0, 1
                late = r == 6 and part.third
                gcn3(A)
                x2_to_cols(A)
                x_to_cols(A)
                edge_in(A)
                gcn1(A)
                gcn3(B)
                x2_to_cols(B)
                sage(A)
                x_to_cols(B)
                if not late:
                    radial_1(A)
                edge_out(A)
                local_rows(A, 1)
                gcn2(A)
                if not late:
                    radial_2(A)
                    radial_1(B)
                gcn1(B)
                edge_in(B)
                sage(B)
                if not late:
                    radial_3(A)
                    radial_2(B)
                local_rows(A, 2)
                local_rows(B, 1)
                edge_out(B)
                gcn2(B)
                if not late:
                    radial_3(B)
                local_rows(B, 2)
                if late:
                    for stage in (radial_1, radial_2, radial_3):
                        stage(A)
                        stage(B)

            rounds(pe, body)

            def body8(k, new, old):
                def up(b):
                    wait(pe, "msg", 2 * k + b - 1)
                    wait(pe, "xg_sb", 2 * k + b)
                    by_rows("r", xdT[b], w_up[:, :]).then_inc(s["up_ps"], 1)

                def gathered(b):
                    wait(pe, "xg_sb", 2 * k + b - 1)
                    wait_dma(pe, got_src[b], 8 * PAIRS + k + 1, 16 * J)
                    to_cols("e", lambda j: g_src[b][:, j, :]).then_inc(s["xg_T"], 1)

                def mids(b):
                    g = 2 * k + b
                    wait(pe, "msg", g)
                    wait(pe, "mid_sb1", g - 1)
                    wait(pe, "mid_sb2", g - 1)
                    to_cols("h1", lambda j: mid[b][:, j, 0:D])
                    to_cols("h2", lambda j: mid[b][:, j, D:2 * D]).then_inc(s["mid_T"], 1)

                def w_outs(b):
                    g = 2 * k - 2 + b
                    wait(pe, "mid_sb1", g)
                    wait(pe, "mid_sb2", g)
                    wait(pe, "scan", 16 * PAIRS + g - 1)
                    mm(ps["xT"][:, 0:C], w_out[0][:, :], h1T[b][:, :], start=True, stop=False)
                    mm(ps["xT"][:, 0:C], w_out[1][:, :], h2T[b][:, :], start=False, stop=True
                       ).then_inc(s["msgo_ps"], 1)

                def sums(b):
                    g = 2 * k - 2 + b
                    wait(pe, "e_ps_free", 6 * PAIRS + g - 1)
                    wait(pe, "scan", 16 * PAIRS + g)
                    to_rows("z", run[b]).then_inc(s["run_T"], 1)

                for b in range(2):
                    if new:
                        gathered(b)
                    if old:
                        w_outs(b)
                    if new:
                        up(b)
                for b in range(2):
                    if old:
                        sums(b)
                    if new:
                        mids(b)
            body8(0, True, False)
            body8(1, True, True)
            with pe.Fori(2, PAIRS) as k:
                body8(k, True, True)
            body8(PAIRS, False, True)

        @block.scalar
        def _(act):
            def f(out_, in_, func, bias=0.0, scale=1.0):
                return nc.scalar.activation(out_, in_, func, bias=bias, scale=scale)

            act.wait_ge(s["cols"], 2)
            f(col["sq1"][:, :], col["cnt"][:, :], ACT.Sqrt).then_inc(s["setup_act"], 1)
            f(col["tmpb"][:, :], col["deg"][:, :], ACT.Sqrt).then_inc(s["setup_act"], 1)
            f(col["tmpa"][:, :], col["dstf"][:, :], ACT.Sqrt).then_inc(s["setup_act"], 1)

            def body(r, k, part):
                K = r * PAIRS + k
                if part.K is not None:
                    n0, m0, t0 = 2 * part.K, 2 * (part.K - 1), 2 * (part.K - 2)

                def dst_cols(b):
                    if r == 0:
                        wait(act, "e_T", 2 * k + b)
                        wait(act, "e_rows", 2 * k + b - 2)
                        f(xdT[b][:, :], ps["e"][:, 0:C], ACT.Copy).then_inc(s["e_dT_sb"], 1)

                def x_cols(b):
                    if part.first:
                        wait(act, "x_T", n0 + b)
                        wait(act, "z_ps", n0 + b - 2)
                        if r == 0:
                            wait(act, "scan", 2 * K + b - 2)
                        f(xT[b][:, :], ps["xT"][:, 0:C], ACT.Copy).then_inc(s["x_T_sb"], 1)

                def z_rows(b):
                    if part.first:
                        wait(act, "z_ps", n0 + b)
                        wait(act, "x2_rdy", n0 + b - 2)
                        f(flat(z_sb[b]), ps["z"][0:P, :], ACT.Copy).then_inc(s["z_sb"], 1)

                def z_root(b):
                    if part.first:
                        wait(act, "z_var", n0 + b)
                        f(z_sd[b][:, :], z_mv[b][:, :, 1], ACT.Sqrt, bias=eps_col[0:P, 1:2], scale=A12
                          ).then_inc(s["z_std"], 1)

                def x2_cols(b):
                    if part.second:
                        wait(act, "x2_T", m0 + b)
                        wait(act, "h1_ps", m0 + b - 2)
                        f(x2T[b][:, :], ps["x2T"][:, 0:C], ACT.Copy).then_inc(s["x2_T_sb"], 1)

                def relu(b, i):
                    if part.second:
                        m = m0 + b
                        wait(act, f"h{i}_ps", m)
                        wait(act, f"h{i + 1}_ps", m - 2)
                        if r < 2:
                            wait(act, f"loc{i}_ps", m - 2 if part.second == SRC else 2 * PAIRS - 1)
                        f((h1T, h2T)[i - 1][b][:, :], ps[f"h{i}"][:, 0:C], ACT.Relu,
                          bias=b_col[:, i - 1:i]).then_inc(s[f"h{i}_sb"], 1)

                def local(b, i):
                    if part.second == SRC:
                        wait(act, f"loc{i}_ps", m0 + b)
                        wait_dma(act, put_loc[b], part.K - 1, 3 * LOAD)
                        f(flat(loc[i - 1][b]), ps[f"h{i}"][0:P, :], ACT.Copy).then_inc(s[f"loc{i}_sb"], 1)

                def leaky_part(b):
                    if part.third:
                        t = t0 + b
                        wait(act, "h3_ps", t)
                        if part.third == SRC:
                            wait_dma(act, put_l3[b], part.K - 2, LOAD)
                            f(flat(loc[2][b]), ps["h3"][0:P, :], ACT.Copy).then_inc(s["loc3_sb"], 1)
                        wait(act, "u_var", t - 2)
                        f(flat(h3r[b]), ps["h3"][0:P, :], ACT.Relu, scale=1.0 - SLOPE
                          ).then_inc(s["h3_relu"], 1)

                def u_root(b):
                    if part.third:
                        wait(act, "u_var", t0 + b)
                        wait(act, "u_scl", t0 + b - 2)
                        src_mode = part.third == SRC
                        f(u_sd[b][:, :], u_mv[b][:, :, 1], ACT.Sqrt,
                          bias=eps_col[0:P, 0:1] if src_mode else eps_col[0:P, 2:3],
                          scale=1.0 if src_mode else A34).then_inc(s["u_std"], 1)

                def x_result(b):
                    if part.third:
                        wait_dma(act, put_x[b], part.K - 2, LOAD)
                        wait(act, "u_scl", t0 + b)
                        for j in range(J):
                            i = f(x_out[b][:, j, :], v_sb[b][:, j, :], ACT.Identity,
                                  bias=u_nb[b][:, j:j + 1], scale=u_rs[b][:, j:j + 1])
                        i.then_inc(s["x_out_rdy"], 1)

                def by_col(out_, in_, name, g, func=ACT.Copy):
                    for j in range(J):
                        i = f(out_[:, j, :], in_[:, j, :], func,
                              scale=col[name][:, bass.ds(g * J + j, 1)])
                    return i

                def edge_1(b):
                    G, g = 2 * K + b, 2 * k + b
                    if r in (4, 5, 6):
                        wait(act, "e_rows", G)
                        wait(act, "e_biased", 2 * (K - 4 * PAIRS) + b - 2, sep=True)
                        by_col(e1[b], rows("e"), "dv2", g).then_inc(s["e_scaled"], 1)
                    if r == 7:
                        wait_dma(act, got_self[b], 6 * PAIRS + 2 * (k + 1), LOAD)
                        wait(act, "e_rdy", G - 2, sep=True)
                        by_col(e1[b], self_in[0][b], "c7", g).then_inc(s["e_w"], 1)
                        by_col(e3[b], self_in[1][b], "d7", g).then_inc(s["e_w"], 1)

                def edge_2(b):
                    G, g = 2 * K + b, 2 * k + b
                    if r in (0, 3, 7):
                        nth = {0: 0, 3: 1, 7: 2}[r] * 2 * PAIRS + g
                        wait(act, "e_var", nth)
                        f(e_sd[b][:, :], e_mv[b][:, :, 1] if r == 0 else e_v[b][:, :], ACT.Sqrt,
                          bias=eps_col[0:P, 0:1]).then_inc(s["e_std"], 1)
                    if r in (4, 5, 6):
                        wait_dma(act, put_e[b], K, LOAD)
                        wait(act, "e_biased", 2 * (K - 4 * PAIRS) + b, sep=True)
                        by_col(e_out[b], e2[b], "dv2", g, ACT.Relu if r < 6 else ACT.Copy
                               ).then_inc(s["e_rdy"], 1)

                def radial_emb(b):
                    g = 2 * k + b
                    if r == 3:
                        wait(act, "rad_x", g)
                        f(rad_square[b], rad_in[b], ACT.Square, bias=centre[:, 0:1], scale=float(NB - 1)
                          ).then_inc(s["rad_sq"], 1)
                        wait(act, "rad_sq", g)
                        wait(act, "rad_rdy", g - 2)
                        f(rad_gauss[b], rad_square[b], ACT.Exp, scale=-0.5).then_inc(s["rad_exp"], 1)

                def radial_6(b, i):
                    g = 2 * k + b
                    if r == 6:
                        wait(act, f"m{i}_ps", g)
                        wait(act, f"m{i + 1}_ps", g - 2)
                        f((hid1[b], hid2[b][0:HID, :])[i - 1], ps[f"h{i}"][0:HID, 0:C], ACT.Silu,
                          bias=mb[:, i - 1:i]).then_inc(s[f"m{i}_sb"], 1)

                A, B = 0, 1
                late = r == 6 and part.third
                leaky_part(A)
                x2_cols(A)
                x_cols(A)
                dst_cols(A)
                relu(A, 1)
                leaky_part(B)
                x2_cols(B)
                z_rows(A)
                x_cols(B)
                if not late:
                    radial_6(A, 1)
                u_root(A)
                edge_1(A)
                local(A, 1)
                x_result(A)
                z_root(A)
                relu(A, 2)
                if not late:
                    radial_6(A, 2)
                relu(B, 1)
                if not late:
                    radial_6(B, 1)
                dst_cols(B)
                edge_2(A)
                local(A, 2)
                local(B, 1)
                z_rows(B)
                if not late:
                    radial_6(B, 2)
                u_root(B)
                edge_1(B)
                radial_emb(A)
                radial_emb(B)
                x_result(B)
                z_root(B)
                relu(B, 2)
                local(B, 2)
                edge_2(B)
                if late:
                    for i in (1, 2):
                        radial_6(A, i)
                        radial_6(B, i)

            rounds(act, body)

            def body8(k, new, old):
                def gathered(b):
                    wait(act, "xg_T", 2 * k + b)
                    wait(act, "up_ps", 2 * k + b - 2)
                    f(xdT[b][:, :], ps["e"][:, 0:C], ACT.Copy).then_inc(s["xg_sb"], 1)

                def mids(b):
                    g = 2 * k + b
                    wait(act, "mid_T", g)
                    wait(act, "msgo_ps", g - 2)
                    f(h1T[b][:, :], ps["h1"][:, 0:C], ACT.Copy).then_inc(s["mid_sb1"], 1)
                    f(h2T[b][:, :], ps["h2"][:, 0:C], ACT.Copy).then_inc(s["mid_sb2"], 1)

                def root(b):
                    wait(act, "e_var", 6 * PAIRS + 2 * k - 2 + b)
                    f(e_sd[b][:, :], e_mv[b][:, :, 1], ACT.Sqrt, bias=eps_col[0:P, 0:1]
                      ).then_inc(s["e_std"], 1)

                if new:
                    gathered(0)
                    gathered(1)
                for b in range(2):
                    if new:
                        mids(b)
                    if old:
                        root(b)
            body8(0, True, False)
            body8(1, True, True)
            with act.Fori(2, PAIRS) as k:
                body8(k, True, True)
            body8(PAIRS, False, True)

        @block.vector
        def _(dve):
            v = nc.vector
            st = Steps(dve, s["setup_dve"], 0, 0)
            st.inc(v.memset(zero_row[:, :], 0.0))
            st.inc(v.memset(w_up[:, :], 0.0))
            st.inc(v.memset(ones[:, :], 1.0))
            st.inc(v.memset(eps_col[:, 0:1], EPS))
            st.inc(v.memset(eps_col[:, 1:2], B12))
            st.inc(v.memset(eps_col[:, 2:3], B34))
            st.inc(v.memset(pick3[:, :], 0.0))
            for i in range(2):
                st.inc(v.memset(w_out[i][:, :], 0.0))
                st.inc(v.memset(run[i][:, :], 0.0))
                st.inc(v.memset(cnt_row[i], 0.0))
            st.inc(v.memset(dst_tile[0:1, 0, 0, :], 0))
            st.inc(v.memset(dst_next[0:1, 0, 0, :], 0))
            st.wait()
            for q in range(3):
                st.inc(v.memset(pick3[32 * q:32 * q + 1, :], 1.0))
            dve.wait_ge(s["setup_in"], n_setup_in[0])
            dve.wait_ge(s["setup_pool"], 5)
            st.inc(v.tensor_copy(tf[:, :, :, :], dst_tile[:, :, :, :]))
            st.inc(v.tensor_copy(first[:, :], dst_tile[:, :, 1, 0]))
            st.inc(v.tensor_tensor(tl[:, :, :, :], dst_tile[:, :, :, :], dst_next[:, :, :, :], ALU.not_equal))
            st.inc(v.tensor_tensor(w_sage_self[:, :], w_sage_self[:, :], ident[:, :], ALU.add))
            st.inc(v.tensor_copy(col["srcp1"][:, :], src_i[:, :]))
            st.inc(v.tensor_copy(col["dstf"][:, :], dst_i[:, :]))
            st.inc(v.tensor_tensor(col["tmpa"][:, :], dst_i[:, :], next_i[:, :], ALU.not_equal))
            st.inc(v.tensor_scalar(mw0[:, :], mw0[:, :], float(NB) ** 0.5, None, ALU.mult))
            for i in range(2):
                for c in range(4):
                    p0 = MUL * c
                    dst = w_out[i][0:MUL, 0:MUL] if c == 0 else \
                        w_out[i][p0:p0 + MUL, MUL + c - 1:MUL + c - 1 + 3 * (MUL - 1) + 1:3]
                    st.inc(v.tensor_scalar(dst, wo_in[p0:p0 + MUL, i * MUL:(i + 1) * MUL],
                                           1.0 / (8.0 * 16.0), None, ALU.mult))
            for i, row in ((0, b_row[0]), (1, b_row[3])):
                st.then(v.tensor_copy(b_rest[:, :], row[:, :]))
                for q in range(3):
                    p0 = 32 * q
                    st.then(v.tensor_copy(b_part[:, :], b_rest[:, :]))
                    st.inc(v.tensor_copy(b_wide[i][p0:p0 + 32, 0:D], b_part[p0:p0 + 32, :]))
                    st.then(v.tensor_tensor(b_rest[:, :], b_rest[:, :], b_part[:, :], ALU.subtract))
                for j in range(1, J):
                    st.inc(v.tensor_copy(b_wide[i][:, j * D:(j + 1) * D], b_wide[i][:, 0:D]))
            st.wait()
            st.then(v.scalar_tensor_tensor(out=tf[:, :, :, :].rearrange("p h q c -> p (h q c)"),
                                           in0=tl[:, :, :, :].rearrange("p h q c -> p (h q c)"), scalar=0.5,
                                           in1=tf[:, :, :, :].rearrange("p h q c -> p (h q c)"),
                                           op0=ALU.mult, op1=ALU.add))
            st.then(v.tensor_scalar(tf[:, :, :, :], tf[:, :, :, :], 0.5, None, ALU.add))
            st.then(v.tensor_tensor(diff[:, :, 0:P], tf[:, :, 1, :], tf[:, :, 0, :], ALU.subtract))
            st.then(v.tensor_copy(diff[0:1, 0, 0:P], tf[0:1, 0, 1, :]))
            st.inc(v.memset(diff[:, :, P:P + 1], 1.0))
            st.inc(v.tensor_scalar(col["srcp1"][:, :], col["srcp1"][:, :], 1.0, None, ALU.add))
            st.then(v.tensor_scalar(col["dstf"][:, :], col["dstf"][:, :], float(-N), None, ALU.add))
            st.then(v.tensor_tensor(col["dstf"][:, :], col["dstf"][:, :], col["tmpa"][:, :], ALU.mult))
            st.then(v.tensor_scalar(col["dstf"][:, :], col["dstf"][:, :], float(N), None, ALU.add))
            st.inc(v.tensor_copy(out_row[:, :], col["dstf"][:, :]))
            st.inc(v.tensor_tensor(y1[:, :, :], attr[:, :, :], attr[:, :, :], ALU.mult))
            dve.wait_ge(s["setup_out"], 7 * 16)
            st.inc(v.tensor_scalar(w_up[:, :], w_up[:, :], float(MUL) ** -0.5, None, ALU.mult))
            st.wait()
            st.then(v.tensor_reduce(col["dstf"][:, :], y1[:, :, :], AX_X, ALU.add))
            v.memset(found[:, :, :], 0.0).then_inc(s["cols"], 1)
            dve.wait_ge(s["cols"], 1)

            def prepare(k):
                for b in range(2):
                    g = 2 * k + b
                    wait_dma(dve, got_prep[b], k + 1, 32)
                    v.tensor_tensor(mask[:, bass.ds(g * C, C)], dst_wide[b][:, 1:C + 1],
                                    dst_wide[b][:, 0:C], ALU.is_equal).then_inc(s["p_mask"], 1)
                    if not isinstance(k, int):
                        dve.wait_ge(s["p_find"], g - 1)
                    for h in range(2):
                        v.tensor_scalar(step_u[h][b], src_wide[b], first[:, h:h + 1], None,
                                        ALU.is_ge).then_inc(s["p_mask"], 1)
                    dve.wait_ge(s["p_mask"], 3 * g + 3)
                    if not (isinstance(k, int) and b == 0):
                        dve.wait_ge(s["p_count"], g)
                    v.tensor_tensor_scan(cnt_row[b], mask[:, bass.ds(g * C, C)], ones[:, :],
                                         cnt_row[1 - b][:, C - 1:C], ALU.mult, ALU.add
                                         ).then_inc(s["p_count"], 1)
                    if b == 1:
                        read_found(k, 0)
                        read_found(k, 1)

            def read_found(k, b):
                g = 2 * k + b
                wait_own(dve, s["p_find"], g + 1)
                fr = ps["e"][0:P, 0:J * (P + 1)].rearrange("p (j c) -> p j c", j=J)
                v.tensor_copy(col["cnt"][:, bass.ds(g * J, J)], ps["r"][0:P, 0:J]).then_inc(s["p_step"], 1)
                v.tensor_copy(col["tile1"][:, bass.ds(g * J, J)], fr[:, :, P]).then_inc(s["p_step"], 1)
                for j in range(J):
                    v.scalar_tensor_tensor(out=found[:, j, :], in0=fr[:, j, 0:P],
                                           scalar=col["srcp1"][:, bass.ds(g * J + j, 1)],
                                           in1=iota1[:, :], op0=ALU.is_equal, op1=ALU.mult
                                           ).then_inc(s["p_step"], 1)
                wait_own(dve, s["p_step"], 6 * (g + 1))
                v.tensor_reduce(col["j1"][:, bass.ds(g * J, J)], found[:, :, :], AX_X, ALU.add
                                ).then_inc(s["p_found"], 1)
                dve.wait_ge(s["p_found"], g + 1)

            prepare(0)
            with dve.Fori(1, PAIRS) as k:
                prepare(k)

            v.tensor_scalar(col["deg"][:, :], col["cnt"][:, :], 1.0, None, ALU.add).then_inc(s["cols"], 1)
            st.inc(v.tensor_scalar(col["tile1"][:, :], col["tile1"][:, :], float(P), float(-P - 1), ALU.mult, ALU.add))
            st.inc(v.tensor_scalar(col["d7"][:, :], col["j1"][:, :], 0.5, None, ALU.is_ge))
            st.wait()
            st.then(v.tensor_tensor(col["j1"][:, :], col["j1"][:, :], col["tile1"][:, :], ALU.add))
            st.inc(v.tensor_scalar(col["c7"][:, :], col["j1"][:, :], float(-E), None, ALU.add))
            st.then(v.tensor_tensor(col["e7"][:, :], col["j1"][:, :], col["own"][:, :], ALU.subtract))
            st.inc(v.tensor_tensor(col["c7"][:, :], col["c7"][:, :], col["d7"][:, :], ALU.mult))
            st.then(v.tensor_tensor(col["e7"][:, :], col["e7"][:, :], col["d7"][:, :], ALU.mult))
            st.inc(v.tensor_scalar(col["c7"][:, :], col["c7"][:, :], float(E), None, ALU.add))
            st.then(v.tensor_tensor(col["e7"][:, :], col["e7"][:, :], col["own"][:, :], ALU.add))
            st.inc(v.tensor_copy(slot_or_zero[:, :], col["c7"][:, :]))
            st.then(v.tensor_copy(slot_or_local[:, :], col["e7"][:, :]))
            dve.wait_ge(s["cols"], 2)
            dve.wait_ge(s["setup_act"], 3)
            st.inc(v.reciprocal(col["rcnt"][:, :], col["cnt"][:, :]))
            st.inc(v.reciprocal(col["dv1"][:, :], col["sq1"][:, :]))
            st.inc(v.reciprocal(col["dv2"][:, :], col["tmpb"][:, :]))
            st.inc(v.tensor_scalar(col["cnt16"][:, :], col["cnt"][:, :], 1.0 / 16.0, None, ALU.mult))
            st.inc(v.tensor_scalar(col["c7"][:, :], col["deg"][:, :], ALPHA / (1 - ALPHA), 1.0, ALU.mult, ALU.add))
            st.inc(v.tensor_scalar(col["d7"][:, :], col["deg"][:, :], 1.0 / (1 - ALPHA), None, ALU.mult))
            st.then(v.tensor_scalar(col["tmpa"][:, :], col["tmpa"][:, :], 1e-12, None, ALU.add))
            st.then(v.reciprocal(col["tmpb"][:, :], col["tmpa"][:, :]))
            st.inc(v.tensor_tensor(y_unit[:, :, :], attr[:, :, :], bc(col["tmpb"][:, :], 3), ALU.mult))
            st.inc(v.tensor_tensor(col["c3"][:, :], col["sq1"][:, :], col["dv2"][:, :], ALU.mult))
            st.inc(v.tensor_tensor(col["e7"][:, :], col["dv2"][:, :], col["dv2"][:, :], ALU.mult))
            st.inc(v.tensor_scalar(col["f7"][:, :], col["dv2"][:, :], 1 - ALPHA, None, ALU.mult))
            st.wait()
            st.inc(v.tensor_scalar(col["c3"][:, :], col["c3"][:, :], 0.25, None, ALU.mult))
            st.inc(v.tensor_scalar(col["e7"][:, :], col["e7"][:, :], (1 - ALPHA) ** 2, None, ALU.mult))
            st.inc(v.tensor_scalar(y1[:, :, :], y_unit[:, :, :], 3.0 ** 0.5, None, ALU.mult))
            st.wait()
            v.memset(found[:, :, :], 0.0).then_inc(s["cols"], 1)

            def stats(q, x, sts, mv):
                for j in range(J):
                    q.inc(v.bn_stats(sts[:, j, :], x[:, j, :]))
                wait_own(dve, q.sem, q.so_far())
                for j in range(J):
                    i = v.bn_aggr(mv[:, j, :], sts[:, j, :])
                    if j < J - 1:
                        q.inc(i)
                return i

            def normed(x_, x, mv, scale):
                for j in range(J):
                    i = v.tensor_scalar(x_[:, j, :], x[:, j, :], mv[:, j, 0:1], scale[:, j:j + 1],
                                        ALU.subtract, ALU.mult)
                return i

            def body(r, k, part):
                K = r * PAIRS + k
                if part.K is not None:
                    n0, t0 = 2 * part.K, 2 * (part.K - 2)

                def scan(b):
                    G, g = 2 * K + b, 2 * k + b
                    if r == 0:
                        wait(dve, "x_T_sb", G)
                    else:
                        wait(dve, "e_T", G)
                    wait(dve, "e_rows", G - 2)
                    wait(dve, "scan", G - 1)
                    v.tensor_tensor_scan(run[b][:, :], mask[:, bass.ds(g * C, C)],
                                         xT[b][:, :] if r == 0 else ps["e"][:, 0:C], run[1 - b][:, C - 1:C],
                                         ALU.mult, ALU.add).then_inc(s["scan"], 1)
                    if r in (4, 5, 6):
                        q = 2 * (K - 4 * PAIRS) + b
                        wait(dve, "scan", G)
                        wait(dve, "e_self_T", q)
                        v.tensor_tensor(run_self[b][:, :], ps["r"][:, 0:C], run[b][:, :], ALU.add
                                        ).then_inc(s["self_add"], 1)

                def z_stats(b):
                    if part.first:
                        n = n0 + b
                        wait(dve, "z_sb", n)
                        q = Steps(dve, s["z_step"], 2 * J - 1, n)
                        stats(q, z_sb[b], z_st[b], z_mv[b]).then_inc(s["z_var"], 1)
                        q.end()

                def x2_rows(b):
                    if part.first:
                        n = n0 + b
                        wait(dve, "x2_T", n - 4)
                        wait(dve, "v_rdy", n - 4)
                        if part.old == SRC:
                            wait_dma(dve, put_loc[b], part.K - 1, 3 * LOAD)
                        wait(dve, "z_std", n)
                        v.reciprocal(z_rs[b][:, :], z_sd[b][:, :]).then_inc(s["z_step2"], 1)
                        dve.wait_ge(s["z_step2"], n + 1)
                        normed(x2[part.parity][b], z_sb[b], z_mv[b], z_rs[b]).then_inc(s["x2_rdy"], 1)

                def u_rows(b):
                    if part.third:
                        n = t0 + b
                        q = Steps(dve, s["u_step"], 2 * J, n)
                        wait(dve, "x_out_rdy", n - 2)
                        wait(dve, "x2_rdy", n)
                        wait(dve, "h3_relu", n)
                        v.scalar_tensor_tensor(out=flat(v_sb[b]), in0=ps["h3"][0:P, :], scalar=SLOPE,
                                               in1=flat(x2[part.parity][b]), op0=ALU.mult, op1=ALU.add
                                               ).then_inc(s["v_rdy"], 1)
                        wait(dve, "v_rdy", n)
                        q.then(v.tensor_tensor(flat(v_sb[b]), flat(v_sb[b]), flat(h3r[b]), ALU.add))
                        stats(q, v_sb[b], u_st[b], u_mv[b]).then_inc(s["u_var"], 1)
                        q.end()

                def u_scale(b):
                    if part.third:
                        n = t0 + b
                        wait(dve, "u_std", n)
                        v.reciprocal(u_rs[b][:, :], u_sd[b][:, :]).then_inc(s["u_step2"], 1)
                        dve.wait_ge(s["u_step2"], n + 1)
                        v.scalar_tensor_tensor(out=u_nb[b][:, :], in0=u_mv[b][:, :, 0], scalar=-1.0,
                                               in1=u_rs[b][:, :], op0=ALU.mult, op1=ALU.mult
                                               ).then_inc(s["u_scl"], 1)

                def edge_rows_1(b):
                    G, g = 2 * K + b, 2 * k + b
                    if r in (4, 5, 6):
                        n = 2 * (K - 4 * PAIRS) + b
                        wait(dve, "e_scaled", n)
                        wait(dve, "e_rdy", G - 2)
                        v.tensor_tensor(e2[b][:, :, :], e1[b][:, :, :], b4(b_row[r - 3][0:P, :]), ALU.add
                                        ).then_inc(s["e_biased"], 1)
                        return
                    wait(dve, "e_rows", G)
                    if r in (1, 2):
                        wait_dma(dve, put_e[b], K, LOAD)
                        v.tensor_tensor(e_out[b][:, :, :], rows("r"), bc(cols("rcnt", g)), ALU.mult
                                        ).then_inc(s["e_rdy"], 1)
                        return
                    if r == 0:
                        q = Steps(dve, s["step0"], 2 * J, g)
                        q.then(v.tensor_tensor(e1[b][:, :, :], rows("e"), bc(cols("rcnt", g)), ALU.mult))
                        v.tensor_tensor(e2[b][:, :, :], rows("r"), e1[b][:, :, :], ALU.add
                                        ).then_inc(s["e_ps_free"], 1)
                        wait(dve, "e_ps_free", G)
                        stats(q, e2[b], e_st[b], e_mv[b]).then_inc(s["e_var"], 1)
                        q.end()
                    if r == 3:
                        q = Steps(dve, s["step3"], 2 * J + 3, g)
                        v.tensor_tensor(e1[b][:, :, :], rows("r"), bc(cols("rcnt", g)), ALU.mult
                                        ).then_inc(s["e_ps_free"], 1)
                        wait_dma(dve, got_self[b], 3 * (k + 1), LOAD)
                        q.inc(v.tensor_tensor(e3[b][:, :, :], self_in[1][b][:, :, :], self_in[2][b][:, :, :], ALU.add))
                        wait(dve, "e_ps_free", 2 * PAIRS + g)
                        q.wait()
                        q.then(v.tensor_tensor(e1[b][:, :, :], e1[b][:, :, :], e3[b][:, :, :], ALU.add))
                        q.then(v.scalar_tensor_tensor(out=flat(e2[b]), in0=flat(self_in[0][b]), scalar=5.0,
                                                      in1=flat(e1[b]), op0=ALU.mult, op1=ALU.add))
                        q.then(stats(q, e2[b], e_st[b], e_mv[b]))
                        v.tensor_tensor(e_v[b][:, :], e_mv[b][:, :, 1], cols("cnt16", g), ALU.mult
                                        ).then_inc(s["e_var"], 1)
                        q.end()
                    if r == 7:
                        q = Steps(dve, s["step7"], 2 * J + 2, g)
                        wait(dve, "e_w", 2 * g + 1)
                        v.tensor_tensor(e2[b][:, :, :], rows("r"), e1[b][:, :, :], ALU.add
                                        ).then_inc(s["e_ps_free"], 1)
                        wait(dve, "e_ps_free", 4 * PAIRS + g)
                        q.then(v.scalar_tensor_tensor(out=flat(e1[b]), in0=flat(e2[b]), scalar=SLOPE,
                                                      in1=flat(e2[b]), op0=ALU.mult, op1=ALU.max))
                        q.then(v.tensor_tensor(e2[b][:, :, :], e1[b][:, :, :], e3[b][:, :, :], ALU.add))
                        q.then(stats(q, e2[b], e_st[b], e_mv[b]))
                        v.tensor_tensor(e_v[b][:, :], e_mv[b][:, :, 1], cols("e7", g), ALU.mult
                                        ).then_inc(s["e_var"], 1)
                        q.end()

                def edge_rows_2(b):
                    if r not in (0, 3, 7):
                        return
                    g = 2 * k + b
                    nth = {0: 0, 3: 1, 7: 2}[r] * 2 * PAIRS + g
                    wait(dve, "e_std", nth)
                    v.reciprocal(e_rs[b][:, :], e_sd[b][:, :]).then_inc(s["e_vv"], 1)
                    dve.wait_ge(s["e_vv"], 2 * nth + 1)
                    v.tensor_tensor(e_sc[b][:, :], e_rs[b][:, :], cols({0: "dv1", 3: "c3", 7: "f7"}[r], g),
                                    ALU.mult).then_inc(s["e_vv"], 1)
                    wait_dma(dve, put_e[b], K, LOAD)
                    dve.wait_ge(s["e_vv"], 2 * nth + 2)
                    normed(e_out[b], e2[b], e_mv[b], e_sc[b]).then_inc(s["e_rdy"], 1)

                def radial_in(b):
                    g = 2 * k + b
                    if r == 3:
                        wait(dve, "rad_sq", g - 2)
                        wait_dma(dve, got_ew[b], k + 1, 16)
                        v.tensor_scalar(rad_in[b], length[b], 0.0, 1.0, ALU.max, ALU.min
                                        ).then_inc(s["rad_x"], 1)

                def radial_out(b):
                    g = 2 * k + b
                    if r == 3:
                        wait_dma(dve, put_rad[b], k, 16)
                        wait(dve, "rad_exp", g)
                        v.scalar_tensor_tensor(out=rad_emb[b], in0=length[b], scalar=1.0,
                                               in1=rad_gauss[b], op0=ALU.is_le, op1=ALU.mult
                                               ).then_inc(s["rad_rdy"], 1)
                    if r == 6:
                        wait_dma(dve, put_w[b], k, LOAD)
                        wait(dve, "m3_ps", g)
                        v.tensor_copy(w_rows[b], rows("h3")).then_inc(s["m3_sb"], 1)

                if r == 6 and isinstance(k, int):
                    for b in range(2):
                        v.memset(work[b][HID:HID + 1, 2, :], 1.0).then_inc(s["rad_one"], 1)
                A, B = 0, 1
                late = r == 6 and part.third
                u_rows(A)
                scan(A)
                radial_in(A)
                radial_in(B)
                u_rows(B)
                z_stats(A)
                u_scale(A)
                edge_rows_1(A)
                scan(B)
                x2_rows(A)
                z_stats(B)
                if not late:
                    radial_out(A)
                u_scale(B)
                edge_rows_2(A)
                edge_rows_1(B)
                x2_rows(B)
                if not late:
                    radial_out(B)
                edge_rows_2(B)
                if late:
                    radial_out(A)
                    radial_out(B)

            rounds(dve, body)

            def body8(k, new, old):
                def messages(b):
                    g = 2 * k + b
                    q = Steps(dve, s["msg_step"], 7, g)
                    up = rows("r")
                    vec = up[:, :, MUL:4 * MUL].rearrange("p j (c m) -> p j c m", c=3)
                    w = self_in[1][b]
                    yu = y_unit[:, bass.ds(g * J, J), :].unsqueeze(3).to_broadcast([P, J, 3, MUL])
                    ys = y1[:, bass.ds(g * J, J), :].unsqueeze(3).to_broadcast([P, J, 3, MUL])

                    def over_c(x):
                        return x.unsqueeze(2).to_broadcast([P, J, 3, MUL])

                    wait(dve, "mid_T", g - 2)
                    wait_dma(dve, got_w[b], k + 1, LOAD)
                    wait(dve, "up_ps", g)
                    q.inc(v.tensor_tensor(mid[b][:, :, 0:MUL], up[:, :, 0:MUL], w[:, :, 0:MUL], ALU.mult))
                    q.inc(v.tensor_tensor(w1s[b], up[:, :, 0:MUL], w[:, :, MUL:2 * MUL], ALU.mult))
                    q.inc(v.tensor_tensor(mid[b][:, :, 5 * MUL:8 * MUL].rearrange("p j (c m) -> p j c m", c=3),
                                          vec, over_c(w[:, :, 2 * MUL:3 * MUL]), ALU.mult))
                    q.then(v.tensor_tensor(vy[b], vec, yu, ALU.mult))
                    q.inc(v.tensor_tensor(mid[b][:, :, MUL:4 * MUL].rearrange("p j (c m) -> p j c m", c=3),
                                          over_c(w1s[b]), ys, ALU.mult))
                    q.then(v.tensor_tensor(vsum[0][b], vy[b][:, :, 0, :], vy[b][:, :, 1, :], ALU.add))
                    q.then(v.tensor_tensor(vsum[1][b], vsum[0][b], vy[b][:, :, 2, :], ALU.add))
                    q.end()
                    v.tensor_tensor(mid[b][:, :, 4 * MUL:5 * MUL], vsum[1][b], w[:, :, 3 * MUL:4 * MUL],
                                    ALU.mult).then_inc(s["msg"], 1)

                def scan8(b):
                    g = 2 * k - 2 + b
                    wait(dve, "msgo_ps", g)
                    wait(dve, "run_T", g - 2)
                    wait(dve, "scan", 16 * PAIRS + g - 1)
                    v.tensor_tensor_scan(run[b][:, :], mask[:, bass.ds(g * C, C)], ps["xT"][:, 0:C],
                                         run[1 - b][:, C - 1:C], ALU.mult, ALU.add).then_inc(s["scan"], 1)

                def result_stats(b):
                    g = 2 * k - 2 + b
                    q = Steps(dve, s["step8"], 2 * J - 1, g)
                    wait_dma(dve, got_self[b], 8 * PAIRS + k, LOAD)
                    wait(dve, "run_T", g)
                    v.tensor_tensor(e2[b][:, :, :], rows("z"), self_in[0][b][:, :, :], ALU.add
                                    ).then_inc(s["e_ps_free"], 1)
                    wait(dve, "e_ps_free", 6 * PAIRS + g)
                    stats(q, e2[b], e_st[b], e_mv[b]).then_inc(s["e_var"], 1)
                    q.end()

                def result(b):
                    g = 2 * k - 2 + b
                    wait(dve, "e_std", 6 * PAIRS + g)
                    v.reciprocal(e_rs[b][:, :], e_sd[b][:, :]).then_inc(s["e_vv"], 1)
                    wait_dma(dve, put_fin[b], k - 1, 16 * J)
                    dve.wait_ge(s["e_vv"], 12 * PAIRS + g + 1)
                    normed(e_out[b], e2[b], e_mv[b], e_rs[b]).then_inc(s["e_rdy"], 1)

                for b in range(2):
                    if new:
                        messages(b)
                    if old:
                        scan8(b)
                for step in (result_stats, result):
                    if old:
                        step(0)
                        step(1)
            body8(0, True, False)
            body8(1, True, True)
            with dve.Fori(2, PAIRS) as k:
                body8(k, True, True)
            body8(PAIRS, False, True)


def kernel(x, src, dst, edge_attr_3, edge_weight, L0_gnn_W, L0_gnn_b, L2_gnn_W1, L2_gnn_b1, L2_gnn_W2,
           L2_gnn_b2, L2_gnn_W3, L2_gnn_b3, L3_gnn_W_up0, L3_gnn_W_up1, L3_gnn_mlp_w0, L3_gnn_mlp_b0,
           L3_gnn_mlp_w1, L3_gnn_mlp_b1, L3_gnn_mlp_w2, L3_gnn_mlp_b2, L3_gnn_W_out0, L3_gnn_W_out1):
    import numpy as _np
    import concourse.bacc as _bacc
    from concourse import mybir as _mybir
    from concourse.bass_utils import run_bass_kernel_spmd as _run

    src, dst = _np.asarray(src), _np.asarray(dst)
    none = _np.full(1, -1, dst.dtype)
    dst_ext = _np.concatenate([none, dst, none])
    by_tile = lambda v: _np.ascontiguousarray(v.reshape(T, P).T)
    arrays = {
        "x": x, "src": src, "dst_ext": dst_ext, "src_pt": by_tile(src), "dst_pt": by_tile(dst),
        "next_pt": by_tile(dst_ext[2:]),
        "attr_pt": _np.ascontiguousarray(_np.asarray(edge_attr_3).reshape(T, P, 3).transpose(1, 0, 2)),
        "edge_weight": edge_weight, "W_sage": L0_gnn_W, "b_sage": L0_gnn_b, "W1": L2_gnn_W1,
        "b1": L2_gnn_b1, "W2": L2_gnn_W2, "b2": L2_gnn_b2, "W3": L2_gnn_W3, "b3": L2_gnn_b3,
        "W_up0": L3_gnn_W_up0, "W_up1": L3_gnn_W_up1, "mlp_w0": L3_gnn_mlp_w0,
        "mlp_b0": L3_gnn_mlp_b0, "mlp_w1": L3_gnn_mlp_w1, "mlp_b1": L3_gnn_mlp_b1,
        "mlp_w2": L3_gnn_mlp_w2, "mlp_b2": L3_gnn_mlp_b2, "W_out0": L3_gnn_W_out0,
        "W_out1": L3_gnn_W_out1,
    }
    nc = _bacc.Bacc("TRN2", target_bir_lowering=False, num_devices=1)
    held, args = {}, {}
    for name, v in arrays.items():
        v = _np.ascontiguousarray(v)
        held[f"in_{name}_dram"] = v
        args[name] = nc.dram_tensor(f"in_{name}_dram", v.shape, _mybir.dt.from_np(v.dtype),
                                    kind="ExternalInput").ap()
    out = nc.dram_tensor("out_0_dram", (N, D), _mybir.dt.float32, kind="ExternalOutput").ap()
    gnn_kernel(nc, args, out)
    r = _run(nc, [held], core_ids=[0])
    return r.results[0]["out_0_dram"]
```

```python
from contextlib import ExitStack

import concourse.bass as bass
from concourse import mybir

F32 = mybir.dt.float32
BF16 = mybir.dt.bfloat16
I32 = mybir.dt.int32
ALU = mybir.AluOpType
ACT = mybir.ActivationFunctionType
AX_X = mybir.AxisListType.X

N, E, D = 100000, 25000, 128
P = 125
J = 4
C = P * J
T = E // P
PAIRS = E // (2 * C)
NODE_PAIRS = N // (2 * C)
ROUNDS = 9
TK = T // 2
EPS = 1e-5
MUL = 32
NB = 8
HID = 64
SLOPE = 0.01
ALPHA = 0.2
SPLIT = ((0, 112), (112, P))
LOAD = 16 * len(SPLIT)
SRC, NODE = "source rows", "node rows"
A12, B12 = (1.5625 + EPS) / 1.5625, EPS * EPS / 1.5625
A34, B34 = 1.0 + EPS, EPS * EPS


class Steps:

    def __init__(self, eng, sem, per, index):
        self.eng, self.sem, self.per, self.index, self.n = eng, sem, per, index, 0

    def inc(self, ins):
        self.n += 1
        ins.then_inc(self.sem, 1)

    def wait(self):
        self.eng.wait_ge(self.sem, self.index * self.per + self.n)

    def so_far(self):
        return self.index * self.per + self.n

    def then(self, ins):
        self.inc(ins)
        self.wait()

    def end(self):
        assert self.n == self.per, f"{self.n} steps, not {self.per}"


def gnn_kernel(nc, a, out):
    with ExitStack() as ctx:
        def sb(name, shape, dt=F32):
            return ctx.enter_context(nc.sbuf_tensor(name, shape, dt))

        def sem(name):
            return ctx.enter_context(nc.semaphore(name))

        def dram(name, shape):
            return nc.dram_tensor(name, shape, F32, kind="Internal").ap()

        def pair_of(name, shape, dt=F32):
            return [sb(f"{name}_{b}", shape, dt) for b in range(2)]

        def pair_sem(name):
            return [sem(f"{name}_{b}") for b in range(2)]

        table = [dram(f"table{r}", (E + 1 if r < 3 else 2 * E, D)) for r in range(8)]
        radial = dram("radial", (2 * PAIRS, NB, C))
        hidden = dram("hidden", (2 * PAIRS, HID, C))
        edge_w = dram("edge_w", (E, D))

        mask = sb("mask", [128, E], BF16)
        ident = sb("ident", [128, 128])
        ones = sb("ones", [128, C])
        zero_row = sb("zero_row", [1, D])
        src_i = sb("src_i", [P, T], I32)
        dst_i = sb("dst_i", [P, T], I32)
        next_i = sb("next_i", [P, T], I32)
        slot_or_zero = sb("slot_or_zero", [P, T], I32)
        slot_or_local = sb("slot_or_local", [P, T], I32)
        out_row = sb("out_row", [P, T], I32)
        names = ("srcp1 j1 tile1 cnt sq1 dv1 rcnt deg dv2 cnt16 c3 c7 d7 e7 f7 dstf tmpa tmpb own").split()
        col = {n: sb(f"col_{n}", [P, T]) for n in names}
        attr = sb("attr", [P, T, 3])
        y_unit = sb("y_unit", [P, T, 3])
        y1 = sb("y1", [P, T, 3])
        iota1 = sb("iota1", [P, P])
        dst_tile = sb("dst_tile", [TK, 2, 2, P], I32)
        dst_next = sb("dst_next", [TK, 2, 2, P], I32)
        tf = sb("tf", [TK, 2, 2, P])
        tl = sb("tl", [TK, 2, 2, P])
        diff = sb("diff", [TK, 2, P + 1])
        first = sb("first", [TK, 2])
        w_up = sb("w_up", [128, 128])
        w_sage_self = sb("w_sage_self", [128, 128])
        w_sage_neigh = sb("w_sage_neigh", [128, 128])
        w_mean = sb("w_mean", [128, 3])
        w_gcn = [sb(f"w_gcn{i}", [128, 128]) for i in range(3)]
        b_col = sb("b_col", [128, 2])
        b_row = [sb(f"b_row{i}", [128, 128]) for i in range(4)]
        b_rest = sb("b_rest", [128, 128])
        b_part = sb("b_part", [128, 128], BF16)
        b_wide = [sb(f"b_wide{i}", [96, J * 128], BF16) for i in range(2)]
        pick3 = sb("pick3", [96, 128], BF16)
        wo_in = sb("wo_in", [128, 64])
        w_out = [sb(f"w_out{i}", [128, 128]) for i in range(2)]
        mw0 = sb("mw0", [NB, HID])
        mw1 = sb("mw1", [HID, HID])
        mw2 = sb("mw2", [HID + 1, D])
        mb = sb("mb", [HID, 2])
        centre = sb("centre", [NB, 1])
        eps_col = sb("eps_col", [128, 3])

        iw = pair_of("iw", [P, 4 * J], I32)
        g_src = pair_of("g_src", [P, J, D])
        g_dst = pair_of("g_dst", [P, J, D])
        x_in = pair_of("x_in", [P, J, D])
        xT = pair_of("xT", [128, C])
        z_sb = pair_of("z_sb", [P, J, D])
        z_st = pair_of("z_st", [P, J, 6])
        z_mv = pair_of("z_mv", [P, J, 2])
        z_sd = pair_of("z_sd", [P, J])
        z_rs = pair_of("z_rs", [P, J])
        x2 = [pair_of(f"x2_{q}", [P, J, D]) for q in range(2)]
        x2T = pair_of("x2T", [128, C])
        h1T = pair_of("h1T", [128, C])
        h2T = pair_of("h2T", [128, C])
        h3_sb = pair_of("h3_sb", [P, J, D])
        v_sb = pair_of("v_sb", [P, J, D])
        u_st = pair_of("u_st", [P, J, 6])
        u_mv = pair_of("u_mv", [P, J, 2])
        u_sd = pair_of("u_sd", [P, J])
        u_rs = pair_of("u_rs", [P, J])
        u_nb = pair_of("u_nb", [P, J])
        x_out = pair_of("x_out", [P, J, D])
        loc = [pair_of(f"loc{i}", [P, J, D]) for i in range(3)]
        run = pair_of("run", [128, C])
        xdT = pair_of("xdT", [128, C])
        run_self = xdT
        self_in = [g_dst, loc[1], loc[2]]
        e1 = pair_of("e1", [P, J, D])
        e2 = pair_of("e2", [P, J, D])
        e3 = loc[0]
        e_st = pair_of("e_st", [P, J, 6])
        e_mv = pair_of("e_mv", [P, J, 2])
        e_v = pair_of("e_v", [P, J])
        e_sd = pair_of("e_sd", [P, J])
        e_rs = pair_of("e_rs", [P, J])
        e_sc = pair_of("e_sc", [P, J])
        e_nb = sb("e_nb", [P, J])
        e_out = pair_of("e_out", [P, J, D])
        work = pair_of("work", [128, 5, 512])
        ow = pair_of("ow", [P, 2 * J], I32)
        dst_wide = [work[b][:, 0, 0:C + 1].bitcast(I32) for b in range(2)]
        src_wide = [work[b][0:TK, 1, 0:C].bitcast(I32) for b in range(2)]
        step_u = [[work[b][0:TK, 2 + h, 0:C] for b in range(2)] for h in range(2)]
        cnt_row = [work[b][:, 4, 0:C] for b in range(2)]
        found = sb("found", [P, J, P])
        length = [work[b][0:NB, 0, 0:C] for b in range(2)]
        rad_in = [work[b][0:NB, 1, 0:C] for b in range(2)]
        rad_square = [work[b][0:NB, 2, 0:C] for b in range(2)]
        rad_gauss = [work[b][0:NB, 3, 0:C] for b in range(2)]
        rad_emb = [work[b][0:NB, 4, 0:C] for b in range(2)]
        emb_in = [work[b][0:NB, 0, 0:C] for b in range(2)]
        hid1 = [work[b][0:HID, 1, 0:C] for b in range(2)]
        hid2 = [work[b][0:HID + 1, 2, 0:C] for b in range(2)]
        w_rows = [work[b][0:P, 3, :].rearrange("p (j d) -> p j d", j=J) for b in range(2)]
        mid = [work[b][0:P, 0:2, :].rearrange("p q (j d) -> p (q j) d", j=J // 2) for b in range(2)]
        w1s = [work[b][0:P, 2, 0:J * MUL].rearrange("p (j m) -> p j m", j=J) for b in range(2)]
        vy = [work[b][0:P, 3, 0:J * 3 * MUL].rearrange("p (j c m) -> p j c m", j=J, c=3) for b in range(2)]
        vsum = [[work[b][0:P, 4, q * J * MUL:(q + 1) * J * MUL].rearrange("p (j m) -> p j m", j=J)
                 for b in range(2)] for q in range(2)]
        ps = {n: ctx.enter_context(nc.psum_tensor(f"ps_{n}", [128, 512], F32))
              for n in ("xT", "z", "x2T", "h1", "h2", "h3", "e", "r")}

        def rows(name):
            return ps[name][0:P, 0:J * D].rearrange("p (j d) -> p j d", j=J)

        def flat(t):
            return t[:, :, :].rearrange("p j d -> p (j d)")

        s = {n: sem(n) for n in (
            "setup_in setup_pool setup_dve setup_act setup_out cols "
            "p_mask p_count p_step p_find p_found "
            "x_T x_T_sb z_ps z_sb z_var z_std x2_rdy x2_T x2_T_sb h1_ps h1_sb h2_ps h2_sb h3_ps h3_sb h3_used "
            "u_step z_step z_step2 u_step2 ow_rdy rad_one u_var u_std u_scl x_out_rdy loc1_ps loc1_sb loc2_ps loc2_sb v_rdy "
            "e_T e_self_T e_dT_sb scan self_add e_rows e_mean e_ps_free e_var e_std e_rdy e_scaled e_biased e_shift e_w e_vv "
            "step0 step3 step7 step8 "
            "rad_sq rad_x rad_exp rad_rdy m1_ps m1_sb m2_ps m2_sb m3_ps m3_sb "
            "xg_T xg_sb up_ps msg msg_step mid_T mid_sb1 mid_sb2 msgo_ps run_T idx"
        ).split()}
        got_src = pair_sem("got_src")
        got_dst = pair_sem("got_dst")
        got_x = pair_sem("got_x")
        got_self = pair_sem("got_self")
        got_prep = pair_sem("got_prep")
        got_ew = pair_sem("got_ew")
        got_rad = pair_sem("got_rad")
        got_w = pair_sem("got_w")
        put_e = pair_sem("put_e")
        put_x = pair_sem("put_x")
        put_loc = pair_sem("put_loc")
        put_l3 = pair_sem("put_l3")
        put_rad = pair_sem("put_rad")
        put_hid = pair_sem("put_hid")
        got_hid = pair_sem("got_hid")
        put_w = pair_sem("put_w")
        put_fin = pair_sem("put_fin")

        def wait_own(eng, sm, value):
            if isinstance(value, int):
                eng.wait_ge(sm, value)
                return
            held = eng.to_reg(value)
            eng.wait_ge(s["cols"], 1)
            eng.wait_ge(sm, held)

        def wait(eng, name, index, sep=False):
            if isinstance(index, int) and index < 0:
                return
            (wait_own if sep else lambda e, x, v: e.wait_ge(x, v))(eng, s[name], index + 1)

        def wait_dma(eng, sm, times, each, sep=False):
            if isinstance(times, int) and times <= 0:
                return
            (wait_own if sep else lambda e, x, v: e.wait_ge(x, v))(eng, sm, times * each)

        def bc(x, n=D):
            return x.unsqueeze(2).to_broadcast([x.shape[0], x.shape[1], n])

        def cols(name, g):
            return col[name][:, bass.ds(g * J, J)]

        def b4(x):
            return x.unsqueeze(1).to_broadcast([x.shape[0], J, x.shape[1]])

        def edge_rows(t, g, base=0):
            return t[bass.ds(g * C + base, C), :].rearrange("(j p) d -> p j d", p=P)

        def node_rows(t, g):
            return t[bass.ds(g * C, C), :].rearrange("(p j) d -> p j d", j=J)

        def transfer(eng, dst, src, sm):
            for lo, hi in SPLIT:
                eng.dma_start(dst[lo:hi], src[lo:hi]).then_inc(sm, 16)

        FREED = {0: 0, 3: 1, 7: 2, 8: 3}
        CHAIN = {0: 0, 1: 1, 2: 2, 4: 3, 5: 4, 6: 5}
        ALONE = (3, 7)
        PEELED = {0: 3, 1: 3, 6: 3}

        class Parts:

            def __init__(self, r, k, like=None):
                self.r, self.k, self.like = r, k, like
                at = CHAIN.get(r)
                self.K = None if at is None else at * PAIRS + k
                of = None if at is None else at * PAIRS + (k if like is None else like)
                self.first, self.second, self.third = (
                    None if of is None or not 0 <= of - i < PAIRS + NODE_PAIRS
                    else SRC if of - i < PAIRS else NODE for i in range(3))
                self.parity = None if of is None else of % 2
                self.old = None if of is None or of - 2 < 0 else SRC if of - 2 < PAIRS else NODE
                self.beside = r not in ALONE and not (r == 6 and not self.third)

            def before(self):
                if isinstance(self.k, int) and self.k == 0:
                    return None
                return Parts(self.r, self.k - 1, None if self.like is None else self.like - 1)

        def e_bank(r, b):
            return "xT" if b and r in (3, 6, 7) else "e"

        def r_bank(r, b):
            return "z" if b and r in (3, 6, 7) else "r"

        find_bank = ("e", "h1")
        count_bank = ("r", "h2")
        up_bank = ("r", "h3")
        msg_bank = ("xT", "x2T")
        sum_bank = ("z", "x2T")
        hid1_bank = ("h1", "x2T")
        hid2_bank = ("h2", "h3")

        def rounds(eng, body, finish=None):
            for r in range(ROUNDS - 1):
                peeled = PEELED.get(r, 1)
                by = 2
                assert (PAIRS - peeled) % by == 0
                for k in range(peeled):
                    body(r, k, Parts(r, k))
                with eng.Fori(0, (PAIRS - peeled) // by) as step:
                    for i in range(by):
                        k = step * by + (peeled + i)
                        body(r, k, Parts(r, k, peeled + i))
                if finish:
                    finish(r)

        block = ctx.enter_context(nc.Block())
        n_setup_in = [0]

        @block.sync
        def _(sp):
            def setup(dst, src):
                sp.dma_start(dst, src).then_inc(s["setup_in"], 16)
                n_setup_in[0] += 16

            setup(src_i[:, :], a["src_pt"])
            setup(dst_i[:, :], a["dst_pt"])
            setup(next_i[:, :], a["next_pt"])
            setup(attr[:, :, :], a["attr_pt"])
            tiles = a["dst_ext"][1:1 + E].rearrange("(t p) -> t p", p=P)
            nexts = a["dst_ext"][2:2 + E].rearrange("(t p) -> t p", p=P)
            for h in range(2):
                setup(dst_tile[:, h, 1, :], tiles[h * TK:(h + 1) * TK, :])
                setup(dst_next[:, h, 1, :], nexts[h * TK:(h + 1) * TK, :])
                lo = 1 if h == 0 else 0
                setup(dst_tile[lo:TK, h, 0, :], tiles[h * TK + lo - 1:(h + 1) * TK - 1, :])
                setup(dst_next[lo:TK, h, 0, :], nexts[h * TK + lo - 1:(h + 1) * TK - 1, :])
            setup(w_sage_self[:, :], a["W_sage"][0:D, :])
            setup(w_sage_neigh[:, :], a["W_sage"][D:2 * D, :])
            for i in range(3):
                setup(w_gcn[i][:, :], a[f"W{i + 1}"])
            for i in range(2):
                setup(b_col[:, i:i + 1], a[f"b{i + 1}"].rearrange("(p o) -> p o", o=1))
            for i, n in enumerate(("b_sage", "b1", "b2", "b3")):
                setup(b_row[i][:, :], a[n].unsqueeze(0).to_broadcast([128, D]))
            for i in range(2):
                setup(wo_in[0:MUL, i * MUL:(i + 1) * MUL], a["W_out0"][i * MUL:(i + 1) * MUL, :])
                for c in range(3):
                    setup(wo_in[MUL * (c + 1):MUL * (c + 2), i * MUL:(i + 1) * MUL],
                          a["W_out1"][i * MUL:(i + 1) * MUL, :])
            setup(mw0[:, :], a["mlp_w0"])
            setup(mw1[:, :], a["mlp_w1"])
            setup(mw2[0:HID, :], a["mlp_w2"])
            setup(mw2[HID:HID + 1, :], a["mlp_b2"].unsqueeze(0))
            for i in range(2):
                setup(mb[:, i:i + 1], a[f"mlp_b{i}"].rearrange("(p o) -> p o", o=1))
            sp.wait_ge(s["setup_dve"], 2)
            for r in range(3):
                sp.dma_start(table[r][E:E + 1, :], zero_row[:, :]).then_inc(s["setup_out"], 16)
            sp.dma_start(w_up[0:MUL, 0:MUL], a["W_up0"]).then_inc(s["setup_out"], 16)
            for c in range(3):
                sp.dma_start(w_up[MUL + c:MUL + c + 3 * (MUL - 1) + 1:3, MUL * (c + 1):MUL * (c + 2)],
                             a["W_up1"]).then_inc(s["setup_out"], 16)

            def prep_load(k, b):
                g = 2 * k + b
                if not isinstance(k, int):
                    wait_own(sp, s["p_mask"], 3 * g - 3)
                sp.dma_start(dst_wide[b], a["dst_ext"][bass.ds(g * C, C + 1)].unsqueeze(0)
                             .to_broadcast([128, C + 1])).then_inc(got_prep[b], 16)
                sp.dma_start(src_wide[b], a["src"][bass.ds(g * C, C)].unsqueeze(0)
                             .to_broadcast([TK, C])).then_inc(got_prep[b], 16)
            for b in range(2):
                prep_load(0, b)
            with sp.Fori(1, PAIRS) as k:
                for b in range(2):
                    prep_load(k, b)

            selfs = {3: (0, 1, 2), 4: (3,), 5: (4,), 6: (5,), 7: (6, 3)}

            def loads(r, k, part):
                for b in range(2):
                    g = 2 * k + b
                    if part.first == NODE:
                        wait(sp, "x_T", 2 * part.K + b - 2, sep=True)
                        transfer(sp, x_in[b][:, :, :], node_rows(a["x"], 2 * (part.K - PAIRS) + b), got_x[b])
                    if r in selfs:
                        if r == 3:
                            if not isinstance(k, int) or k:
                                wait(sp, "e_var", 2 * PAIRS + g - 2, sep=True)
                        elif r == 7:
                            wait(sp, "e_w", 2 * g - 3, sep=True)
                        elif r != 4 or not isinstance(k, int) or k:
                            wait(sp, "e_self_T", 2 * (r - 4) * PAIRS + g - 2, sep=True)
                        for i, t in enumerate(selfs[r]):
                            transfer(sp, self_in[i][b][:, :, :], edge_rows(table[t], g), got_self[b])
                    if r == 3:
                        wait(sp, "rad_rdy", g - 2, sep=True)
                        sp.dma_start(length[b], a["edge_weight"][bass.ds(g * C, C)].unsqueeze(0)
                                     .to_broadcast([NB, C])).then_inc(got_ew[b], 16)
                    if r == 6:
                        wait(sp, "m1_ps", g - 2, sep=True)
                        sp.dma_start(emb_in[b], radial[bass.ds(g, 1)].rearrange("o n c -> (o n) c")
                                     ).then_inc(got_rad[b], 16)
                    if r == 7:
                        wait(sp, "m3_ps", g - 2, sep=True)
                        sp.dma_start(hid2[b][0:HID], hidden[bass.ds(g, 1)].rearrange("o n c -> (o n) c")
                                     ).then_inc(got_hid[b], 16)

            def stores(r, k, part):
                for b in range(2):
                    g = 2 * k + b
                    if part.third == SRC:
                        t = 2 * (part.K - 2) + b
                        wait(sp, "h3_sb", t, sep=True)
                        transfer(sp, edge_rows(table[6], t, E), loc[2][b][:, :, :], put_l3[b])
                    if part.third:
                        t = 2 * (part.K - 2) + b
                        wait(sp, "x_out_rdy", t, sep=True)
                        to = edge_rows(table[7], t, E) if part.third == SRC else node_rows(out, t - 2 * PAIRS)
                        transfer(sp, to, x_out[b][:, :, :], put_x[b])
                    if part.second == SRC:
                        m = 2 * (part.K - 1) + b
                        for nm in ("x2_rdy", "loc1_sb", "loc2_sb"):
                            wait(sp, nm, m, sep=True)
                        for t, buf in ((3, x2[1 - part.parity][b]), (4, loc[0][b]), (5, loc[1][b])):
                            transfer(sp, edge_rows(table[t], m, E), buf[:, :, :], put_loc[b])
                    wait(sp, "e_rdy", 2 * (r * PAIRS + k) + b, sep=True)
                    transfer(sp, edge_rows(table[r], g), e_out[b][:, :, :], put_e[b])
                    if r == 3:
                        wait(sp, "rad_rdy", g, sep=True)
                        sp.dma_start(radial[bass.ds(g, 1)].rearrange("o n c -> (o n) c"), rad_emb[b]
                                     ).then_inc(put_rad[b], 16)
                    if r == 6:
                        wait(sp, "m2_sb", g, sep=True)
                        sp.dma_start(hidden[bass.ds(g, 1)].rearrange("o n c -> (o n) c"), hid2[b][0:HID]
                                     ).then_inc(put_hid[b], 16)
                    if r == 7:
                        wait(sp, "m3_sb", g, sep=True)
                        transfer(sp, edge_rows(edge_w, g), w_rows[b], put_w[b])

            for r in range(ROUNDS - 1):
                if r:
                    for b in range(2):
                        sp.wait_ge(put_e[b], LOAD * PAIRS * r)
                        if r == 3:
                            sp.wait_ge(put_loc[b], 3 * LOAD * PAIRS)
                            sp.wait_ge(put_l3[b], LOAD * PAIRS)
                        if r == 6:
                            sp.wait_ge(put_rad[b], 16 * PAIRS)
                        if r == 7:
                            sp.wait_ge(put_hid[b], 16 * PAIRS)
                peeled = PEELED.get(r, 1)
                by = 2
                loads(r, 0, Parts(r, 0))
                for k in range(1, peeled + 1):
                    loads(r, k, Parts(r, k))
                    stores(r, k - 1, Parts(r, k - 1))
                left = 2
                with sp.Fori(0, (PAIRS - left - peeled) // by) as step:
                    for i in range(by):
                        k = step * by + (peeled + i)
                        loads(r, k + 1, Parts(r, k + 1, peeled + i + 1))
                        stores(r, k, Parts(r, k, peeled + i))
                for k in range(PAIRS - left, PAIRS):
                    if k + 1 < PAIRS:
                        loads(r, k + 1, Parts(r, k + 1))
                    stores(r, k, Parts(r, k))

            for b in range(2):
                sp.wait_ge(put_e[b], LOAD * PAIRS * (ROUNDS - 1))
                sp.wait_ge(put_w[b], LOAD * PAIRS)

            def loads8(k):
                for b in range(2):
                    if not (isinstance(k, int) and k >= PAIRS):
                        g = 2 * k + b
                        if not isinstance(k, int):
                            wait(sp, "msg", g - 2, sep=True)
                        transfer(sp, self_in[1][b][:, :, :], edge_rows(edge_w, g), got_w[b])
                    if not (isinstance(k, int) and k == 0):
                        g = 2 * k + b - 2
                        wait(sp, "e_ps_free", 6 * PAIRS + g - 2, sep=True)
                        transfer(sp, self_in[0][b][:, :, :], edge_rows(table[7], g), got_self[b])
            loads8(0)
            with sp.Fori(1, PAIRS) as k:
                loads8(k)
            loads8(PAIRS)
            for b in range(2):
                sp.wait_ge(put_x[b], LOAD * (PAIRS + NODE_PAIRS))
                sp.wait_ge(put_fin[b], 16 * J * PAIRS)

        @block.gpsimd
        def _(pool):
            pool.memset(ident[:, :], 0.0).then_inc(s["setup_pool"], 1)
            pool.iota(iota1[:, :], pattern=[[1, P]], base=1, channel_multiplier=0,
                      allow_small_or_imprecise_dtypes=True).then_inc(s["setup_pool"], 1)
            pool.iota(col["own"][:, :], pattern=[[P, T]], base=E, channel_multiplier=1,
                      allow_small_or_imprecise_dtypes=True).then_inc(s["setup_pool"], 1)
            pool.iota(centre[:, :], pattern=[[0, 1]], base=0, channel_multiplier=-1,
                      allow_small_or_imprecise_dtypes=True).then_inc(s["setup_pool"], 1)
            pool.wait_ge(s["setup_pool"], 4)
            pool.affine_select(out=ident[:, :], in_=ident[:, :], compare_op=ALU.not_equal, fill=1.0,
                               base=0, pattern=[[-1, 128]], channel_multiplier=1
                               ).then_inc(s["setup_pool"], 1)
            pool.wait_ge(s["setup_in"], n_setup_in[0])

            def gather(dst, src, index, sm):
                for j in range(J):
                    pool.indirect_dma_start(
                        out=dst[:, j, :], out_offset=None, in_=src,
                        in_offset=bass.IndirectOffsetOnAxis(ap=index[:, j:j + 1], axis=0)
                    ).then_inc(sm, 16)

            def indices(r, k, q):
                index = src_i if r == 0 else slot_or_zero if r < 4 else slot_or_local
                pair = bass.ds(k * 2 * J, 2 * J)
                pool.tensor_copy(iw[q][:, 0:2 * J], index[:, pair]).then_inc(s["idx"], 1)
                if r == 0:
                    pool.tensor_copy(iw[q][:, 2 * J:4 * J], dst_i[:, pair]).then_inc(s["idx"], 1)

            def indices_there(r, k):
                wait_own(pool, s["idx"], 2 * (k + 1) if r == 0 else (r + 1) * PAIRS + k + 1)

            def body(r, k, q, more=True):
                G = 2 * (r * PAIRS + k)
                indices_there(r, k)
                for b in range(2):
                    def from_src():
                        gather(g_src[b], a["x"] if r == 0 else table[r - 1], iw[q][:, b * J:(b + 1) * J],
                               got_src[b])

                    if r == 0:
                        wait(pool, "x_T", G + b - 2, sep=True)
                        from_src()
                    wait(pool, "e_T", G + b - 2, sep=True)
                    if b and more:
                        indices(r, k + 1, 1 - q)
                    if r == 0:
                        gather(g_dst[b], a["x"], iw[q][:, (2 + b) * J:(3 + b) * J], got_dst[b])
                    else:
                        from_src()

            for r in range(ROUNDS - 1):
                if r:
                    wait(pool, "e_T", 2 * r * PAIRS - 1)
                    pool.wait_ge(s["cols"], 3)
                    pool.wait_ge(s["setup_out"], 7 * 16)
                indices(r, 0, 0)
                if r:
                    for b in range(2):
                        pool.wait_ge(put_e[b], LOAD * PAIRS * r)
                        if r >= 4:
                            pool.wait_ge(put_loc[b], 3 * LOAD * PAIRS)
                            pool.wait_ge(put_l3[b], LOAD * PAIRS)
                body(r, 0, 0)
                with pool.Fori(0, (PAIRS - 3) // 2) as step:
                    for i in (1, 2):
                        body(r, step * 2 + i, i % 2)
                body(r, PAIRS - 2, 1)
                body(r, PAIRS - 1, 0, more=False)

            wait(pool, "e_T", 16 * PAIRS - 1)
            indices(8, 0, 0)
            for b in range(2):
                pool.wait_ge(put_e[b], LOAD * PAIRS * (ROUNDS - 1))
                pool.wait_ge(put_x[b], LOAD * (PAIRS + NODE_PAIRS))

            def gather8(k, q, more=True):
                indices_there(8, k)
                for b in range(2):
                    wait(pool, "xg_T", 2 * k + b - 2, sep=True)
                    if b and more:
                        indices(8, k + 1, 1 - q)
                    gather(g_src[b], table[7], iw[q][:, b * J:(b + 1) * J], got_src[b])

            def scatter8(k, q):
                wait_own(pool, s["ow_rdy"], k + 1)
                for b in range(2):
                    wait(pool, "e_rdy", 2 * (8 * PAIRS + k) + b, sep=True)
                    for j in range(J):
                        i = b * J + j
                        pool.indirect_dma_start(
                            out=out, out_offset=bass.IndirectOffsetOnAxis(ap=ow[q][:, i:i + 1], axis=0),
                            in_=e_out[b][:, j, :], in_offset=None, bounds_check=N - 1,
                            oob_is_err=False).then_inc(put_fin[b], 16)

            def targets(k, q):
                for b in range(2):
                    wait_dma(pool, put_fin[b], k - 1, 16 * J, sep=True)
                pool.tensor_copy(ow[q][:, :], out_row[:, bass.ds(k * 2 * J, 2 * J)]).then_inc(s["ow_rdy"], 1)

            gather8(0, 0)
            targets(0, 0)
            gather8(1, 1)
            gather8(2, 0)
            scatter8(0, 0)
            def step8(k, q, more=True):
                gather8(k, q, more)
                targets(k - 2, q)
                scatter8(k - 2, q)

            with pool.Fori(0, (PAIRS - 5) // 2) as step:
                for i in (3, 4):
                    step8(step * 2 + i, i % 2)
            step8(PAIRS - 2, 1)
            step8(PAIRS - 1, 0, more=False)
            for k in (PAIRS - 2, PAIRS - 1):
                targets(k, k % 2)
                scatter8(k, k % 2)
            for b in range(2):
                pool.wait_ge(put_fin[b], 16 * J * PAIRS)

        @block.tensor
        def _(pe):
            mm = nc.tensor.matmul

            def to_cols(bank, src):
                for j in range(J):
                    i = nc.tensor.transpose(ps[bank][:, j * P:(j + 1) * P], src(j), ident[0:P, 0:P])
                return i

            def to_rows(bank, src):
                for j in range(J):
                    i = nc.tensor.transpose(rows(bank)[:, j, :], src[:, j * P:(j + 1) * P], ident[:, :])
                return i

            def by_rows(bank, lhs, w, bias=None):
                for j in range(J):
                    i = mm(rows(bank)[:, j, :], lhs[:, j * P:(j + 1) * P], w, start=(j == 0 if bias is not None else True),
                           stop=bias is None, skip_group_check=True)
                if bias is not None:
                    i = mm(ps[bank][0:P, 0:J * D], pick3[:, 0:P], b_wide[bias][:, :], start=False,
                           stop=True, skip_group_check=True)
                return i

            last_first = {3: 6 * PAIRS - 1, 6: 2 * (PAIRS + NODE_PAIRS) - 1}
            pe.wait_ge(s["setup_pool"], 5)
            pe.wait_ge(s["cols"], 1)
            def find(k):
                for b in range(2):
                    g = 2 * k + b
                    pe.wait_ge(s["p_mask"], 3 * g + 3)
                    pe.wait_ge(s["p_count"], g + 1)
                    if not isinstance(k, int):
                        pe.wait_ge(s["p_found"], g - 1)
                    fr = ps[find_bank[b]][0:P, 0:J * (P + 1)].rearrange("p (j c) -> p j c", j=J)
                    for j in range(J):
                        for h in range(2):
                            mm(fr[:, j, :], step_u[h][b][:, j * P:(j + 1) * P], diff[:, h, :],
                               start=(h == 0), stop=(h == 1))
                    for j in range(J):
                        i = mm(ps[count_bank[b]][0:P, j:j + 1], cnt_row[b][:, j * P:(j + 1) * P], ident[:, 0:1],
                               start=True, stop=True)
                    i.then_inc(s["p_find"], 1)
            find(0)
            with pe.Fori(0, (PAIRS - 1) // 2) as step:
                for i in (1, 2):
                    find(step * 2 + i)
            pe.wait_ge(s["p_found"], 2 * PAIRS)

            def body(r, k, part):
                K = r * PAIRS + k

                def edge_in(b):
                    G, g = 2 * K + b, 2 * k + b
                    if r == 0:
                        wait(pe, "e_ps_free", g - 1)
                        wait_dma(pe, got_dst[b], k + 1, 16 * J)
                        to_cols("e", lambda j: g_dst[b][:, j, :]).then_inc(s["e_T"], 1)
                        return
                    before = 1 if e_bank(r, b) == e_bank(r, 1 - b) else 2
                    if isinstance(k, int) and k == 0 and b == 0:
                        wait(pe, "e_rdy", G - 1)
                        if r in (3, 6):
                            wait(pe, "z_sb", last_first[r])
                    if r in (4, 5, 6):
                        wait(pe, "e_scaled", 2 * (K - 4 * PAIRS) + b - before)
                    else:
                        wait(pe, "scan", G - before)
                    wait_dma(pe, got_src[b], K + 1, 16 * J)
                    to_cols(e_bank(r, b), lambda j: g_src[b][:, j, :]).then_inc(s["e_T"], 1)
                    if r in (4, 5, 6):
                        wait_dma(pe, got_self[b], 3 * PAIRS + (r - 4) * PAIRS + k + 1, LOAD)
                        to_cols(r_bank(r, b), lambda j: self_in[0][b][:, j, :]).then_inc(s["e_self_T"], 1)

                def edge_out(b):
                    G, g = 2 * K + b, 2 * k + b
                    if r == 0:
                        wait(pe, "e_dT_sb", 2 * k + b)
                        by_rows("r", xdT[b], w_sage_self[:, :], bias=0)
                        wait(pe, "scan", G)
                        by_rows("e", run[b], w_sage_neigh[:, :]).then_inc(s["e_rows"], 1)
                    elif r in (4, 5, 6):
                        wait(pe, "self_add", 2 * (K - 4 * PAIRS) + b)
                        by_rows(e_bank(r, b), run_self[b], w_gcn[r - 4][:, :]).then_inc(s["e_rows"], 1)
                    else:
                        if r in (1, 2):
                            wait(pe, "e_rdy", G - 1)
                        elif not isinstance(k, int):
                            wait(pe, "e_ps_free", FREED[r] * 2 * PAIRS + g - 2)
                        wait(pe, "scan", G)
                        to_rows(r_bank(r, b), run[b]).then_inc(s["e_rows"], 1)

                if part.K is not None:
                    n0, m0, t0 = 2 * part.K, 2 * (part.K - 1), 2 * (part.K - 2)

                def x_to_cols(b):
                    if not part.first:
                        return
                    n = n0 + b
                    wait(pe, "x_T_sb", n - 1)
                    if r == 4 and b == 0 and isinstance(k, int):
                        wait(pe, "e_rdy", 2 * K - 1)
                    if r == 0:
                        wait_dma(pe, got_src[b], k + 1, 16 * J)
                        to_cols("xT", lambda j: g_src[b][:, j, :]).then_inc(s["x_T"], 1)
                    else:
                        wait_dma(pe, got_x[b], part.K - PAIRS + 1, LOAD)
                        to_cols("xT", lambda j: x_in[b][:, j, :]).then_inc(s["x_T"], 1)

                def sage(b):
                    if not part.first:
                        return
                    n = n0 + b
                    wait(pe, "z_sb", n - 1)
                    wait(pe, "x_T_sb", n)
                    by_rows("z", xT[b], w_sage_self[:, :], bias=0).then_inc(s["z_ps"], 1)

                def x2_to_cols(b):
                    if not part.second:
                        return
                    m = m0 + b
                    wait(pe, "x2_T_sb", m - 1)
                    wait(pe, "x2_rdy", m)
                    to_cols("x2T", lambda j: x2[1 - part.parity][b][:, j, :]).then_inc(s["x2_T"], 1)

                def gcn1(b):
                    if not part.second:
                        return
                    m = m0 + b
                    wait(pe, "h1_sb", m - 1)
                    if r < 2:
                        wait(pe, "loc1_sb", m - 1 if part.second == SRC else 2 * PAIRS - 1)
                    wait(pe, "x2_T_sb", m)
                    mm(ps["h1"][:, 0:C], w_gcn[0][:, :], x2T[b][:, :], start=True, stop=True
                       ).then_inc(s["h1_ps"], 1)

                def gcn2(b):
                    if not part.second:
                        return
                    m = m0 + b
                    wait(pe, "h2_sb", m - 1)
                    if r < 2:
                        wait(pe, "loc2_sb", m - 1 if part.second == SRC else 2 * PAIRS - 1)
                    wait(pe, "h1_sb", m)
                    mm(ps["h2"][:, 0:C], w_gcn[1][:, :], h1T[b][:, :], start=True, stop=True
                       ).then_inc(s["h2_ps"], 1)

                def gcn3(b):
                    if not part.third:
                        return
                    t = t0 + b
                    wait(pe, "h3_sb", t - 1)
                    if r == 6 and k == 1:
                        wait(pe, "m2_sb", 1)
                    wait(pe, "h2_sb", t)
                    by_rows("h3", h2T[b], w_gcn[2][:, :], bias=1).then_inc(s["h3_ps"], 1)

                def local_rows(b, i):
                    if part.second != SRC:
                        return
                    wait(pe, f"h{i}_sb", m0 + b)
                    to_rows(f"h{i}", (h1T, h2T)[i - 1][b]).then_inc(s[f"loc{i}_ps"], 1)

                last = 2 * (PAIRS + NODE_PAIRS) - 1

                def radial_1(b):
                    g = 2 * k + b
                    if r == 6:
                        wait(pe, "m1_sb", g - 2)
                        if isinstance(k, int):
                            wait(pe, "h1_sb", last)
                            wait(pe, "x2_T_sb", last)
                        wait_dma(pe, got_rad[b], k + 1, 16)
                        mm(ps[hid1_bank[b]][0:HID, 0:C], mw0[:, :], emb_in[b], start=True, stop=True
                           ).then_inc(s["m1_ps"], 1)

                def radial_2(b):
                    g = 2 * k + b
                    if r == 6:
                        wait(pe, "m2_sb", g - 2, sep=True)
                        if isinstance(k, int):
                            wait(pe, "h2_sb", last)
                            wait(pe, "h3_sb", last - (2 if k == 0 else 0))
                        wait(pe, "m1_sb", g, sep=True)
                        mm(ps[hid2_bank[b]][0:HID, 0:C], mw1[:, :], hid1[b], start=True, stop=True
                           ).then_inc(s["m2_ps"], 1)

                def radial_3(b):
                    g = 2 * k + b
                    if r == 7:
                        wait(pe, "m3_sb", g - 2)
                        if isinstance(k, int):
                            wait(pe, "m2_sb", 2 * PAIRS - 1)
                        wait_dma(pe, got_hid[b], k + 1, 16)
                        pe.wait_ge(s["rad_one"], 2)
                        by_rows(hid2_bank[b], hid2[b], mw2[:, :]).then_inc(s["m3_ps"], 1)

                A, B = 0, 1
                if not part.beside:
                    edge_in(A)
                    radial_1(A)
                    edge_in(B)
                    radial_1(B)
                    edge_out(A)
                    radial_2(A)
                    edge_out(B)
                    radial_2(B)
                    radial_3(A)
                    radial_3(B)
                    return
                gcn3(A)
                x2_to_cols(A)
                x_to_cols(A)
                edge_in(A)
                gcn1(A)
                gcn3(B)
                x2_to_cols(B)
                sage(A)
                x_to_cols(B)
                edge_out(A)
                local_rows(A, 1)
                gcn2(A)
                gcn1(B)
                if r:
                    edge_in(B)
                    sage(B)
                    local_rows(A, 2)
                    local_rows(B, 1)
                    gcn2(B)
                    edge_out(B)
                    local_rows(B, 2)
                else:
                    sage(B)
                    edge_in(B)
                    local_rows(A, 2)
                    local_rows(B, 1)
                    edge_out(B)
                    gcn2(B)
                    local_rows(B, 2)
                for stage in (radial_1, radial_2):
                    stage(A)
                    stage(B)

            rounds(pe, body)

            def body8(k, new, old):
                def up(b):
                    wait(pe, "msg", 2 * k + b - 2)
                    wait(pe, "xg_sb", 2 * k + b)
                    by_rows(up_bank[b], xdT[b], w_up[:, :]).then_inc(s["up_ps"], 1)

                def gathered(b):
                    wait(pe, "xg_sb", 2 * k + b - 1)
                    wait_dma(pe, got_src[b], 8 * PAIRS + k + 1, 16 * J)
                    to_cols("e", lambda j: g_src[b][:, j, :]).then_inc(s["xg_T"], 1)

                def mids(b):
                    g = 2 * k + b
                    wait(pe, "msg", g)
                    wait(pe, "mid_sb1", g - 1)
                    wait(pe, "mid_sb2", g - 1)
                    to_cols("h1", lambda j: mid[b][:, j, 0:D])
                    to_cols("h2", lambda j: mid[b][:, j, D:2 * D]).then_inc(s["mid_T"], 1)

                def w_outs(b):
                    g = 2 * k - 2 + b
                    bank = ps[msg_bank[b]][:, 0:C]
                    wait(pe, "mid_sb1", g)
                    wait(pe, "mid_sb2", g)
                    wait(pe, "scan", 16 * PAIRS + g - 2)
                    wait(pe, "e_ps_free", 6 * PAIRS + g - 2)
                    mm(bank, w_out[0][:, :], h1T[b][:, :], start=True, stop=False)
                    mm(bank, w_out[1][:, :], h2T[b][:, :], start=False, stop=True
                       ).then_inc(s["msgo_ps"], 1)

                def sums(b):
                    g = 2 * k - 2 + b
                    wait(pe, "e_ps_free", 6 * PAIRS + g - 2)
                    wait(pe, "scan", 16 * PAIRS + g)
                    to_rows(sum_bank[b], run[b]).then_inc(s["run_T"], 1)

                if old:
                    w_outs(0)
                    w_outs(1)
                if new:
                    for b in range(2):
                        gathered(b)
                        up(b)
                if old:
                    sums(0)
                    sums(1)
                if new:
                    mids(0)
                    mids(1)
            body8(0, True, False)
            body8(1, True, True)
            with pe.Fori(2, PAIRS) as k:
                body8(k, True, True)
            body8(PAIRS, False, True)

        @block.scalar
        def _(act):
            def f(out_, in_, func, bias=0.0, scale=1.0):
                return nc.scalar.activation(out_, in_, func, bias=bias, scale=scale)

            act.wait_ge(s["cols"], 2)
            f(col["sq1"][:, :], col["cnt"][:, :], ACT.Sqrt).then_inc(s["setup_act"], 1)
            f(col["tmpb"][:, :], col["deg"][:, :], ACT.Sqrt).then_inc(s["setup_act"], 1)
            f(col["tmpa"][:, :], col["dstf"][:, :], ACT.Sqrt).then_inc(s["setup_act"], 1)

            def x_result(part, b):
                if part.third:
                    t = 2 * (part.K - 2) + b
                    wait_dma(act, put_x[b], part.K - 2, LOAD)
                    wait(act, "u_scl", t)
                    for j in range(J):
                        i = f(x_out[b][:, j, :], v_sb[b][:, j, :], ACT.Identity,
                              bias=u_nb[b][:, j:j + 1], scale=u_rs[b][:, j:j + 1])
                    i.then_inc(s["x_out_rdy"], 1)

            def by_col(out_, in_, name, g, func=ACT.Copy):
                for j in range(J):
                    i = f(out_[:, j, :], in_[:, j, :], func,
                          scale=col[name][:, bass.ds(g * J + j, 1)])
                return i

            def edge_2(r, k, b):
                K = r * PAIRS + k
                G, g = 2 * K + b, 2 * k + b
                if r in (0, 3, 7):
                    nth = {0: 0, 3: 1, 7: 2}[r] * 2 * PAIRS + g
                    wait(act, "e_var", nth)
                    f(e_sd[b][:, :], e_mv[b][:, :, 1] if r == 0 else e_v[b][:, :], ACT.Sqrt,
                      bias=eps_col[0:P, 0:1]).then_inc(s["e_std"], 1)
                if r in (4, 5, 6):
                    wait_dma(act, put_e[b], K, LOAD)
                    wait(act, "e_biased", 2 * (K - 4 * PAIRS) + b, sep=True)
                    by_col(e_out[b], e2[b], "dv2", g, ACT.Relu if r < 6 else ACT.Copy
                           ).then_inc(s["e_rdy"], 1)

            def normed_b(k):
                wait(act, "e_shift", k)
                wait_dma(act, put_e[1], 7 * PAIRS + k, LOAD)
                for j in range(J):
                    i = f(e_out[1][:, j, :], e2[1][:, j, :], ACT.Identity,
                          bias=e_nb[:, j:j + 1], scale=e_sc[1][:, j:j + 1])
                i.then_inc(s["e_rdy"], 1)

            def late(part, stage):
                if part is None or not part.beside:
                    return
                if part.r == 0 and stage == 0:
                    edge_2(part.r, part.k, 1)
                if stage == 0:
                    x_result(part, 1)
                elif part.r:
                    edge_2(part.r, part.k, 1)

            def body(r, k, part):
                K = r * PAIRS + k
                if part.K is not None:
                    n0, m0, t0 = 2 * part.K, 2 * (part.K - 1), 2 * (part.K - 2)

                def dst_cols(b):
                    if r == 0:
                        wait(act, "e_T", 2 * k + b)
                        wait(act, "e_rows", 2 * k + b - 2)
                        f(xdT[b][:, :], ps["e"][:, 0:C], ACT.Copy).then_inc(s["e_dT_sb"], 1)

                def x_cols(b):
                    if part.first:
                        wait(act, "x_T", n0 + b)
                        wait(act, "z_ps", n0 + b - 2)
                        if r == 0:
                            wait(act, "scan", 2 * K + b - 2)
                        f(xT[b][:, :], ps["xT"][:, 0:C], ACT.Copy).then_inc(s["x_T_sb"], 1)

                def z_rows(b):
                    if part.first:
                        wait(act, "z_ps", n0 + b)
                        wait(act, "x2_rdy", n0 + b - 2)
                        f(flat(z_sb[b]), ps["z"][0:P, :], ACT.Copy).then_inc(s["z_sb"], 1)

                def z_root(b):
                    if part.first:
                        wait(act, "z_var", n0 + b)
                        f(z_sd[b][:, :], z_mv[b][:, :, 1], ACT.Sqrt, bias=eps_col[0:P, 1:2], scale=A12
                          ).then_inc(s["z_std"], 1)

                def x2_cols(b):
                    if part.second:
                        wait(act, "x2_T", m0 + b)
                        wait(act, "h1_ps", m0 + b - 2)
                        f(x2T[b][:, :], ps["x2T"][:, 0:C], ACT.Copy).then_inc(s["x2_T_sb"], 1)

                def relu(b, i):
                    if part.second:
                        m = m0 + b
                        wait(act, f"h{i}_ps", m)
                        wait(act, f"h{i + 1}_ps", m - 2)
                        if r < 2:
                            wait(act, f"loc{i}_ps", m - 2 if part.second == SRC else 2 * PAIRS - 1)
                        f((h1T, h2T)[i - 1][b][:, :], ps[f"h{i}"][:, 0:C], ACT.Relu,
                          bias=b_col[:, i - 1:i]).then_inc(s[f"h{i}_sb"], 1)

                def local(b, i):
                    if part.second == SRC:
                        wait(act, f"loc{i}_ps", m0 + b)
                        wait_dma(act, put_loc[b], part.K - 1, 3 * LOAD)
                        f(flat(loc[i - 1][b]), ps[f"h{i}"][0:P, :], ACT.Copy).then_inc(s[f"loc{i}_sb"], 1)

                def h3_rows(b):
                    if part.third:
                        t = t0 + b
                        wait(act, "h3_ps", t)
                        wait(act, "h3_used", t - 2)
                        if part.third == SRC:
                            wait_dma(act, put_l3[b], part.K - 2, LOAD)
                        f(flat((loc[2] if part.third == SRC else h3_sb)[b]), ps["h3"][0:P, :], ACT.Copy
                          ).then_inc(s["h3_sb"], 1)

                def u_root(b):
                    if part.third:
                        wait(act, "u_var", t0 + b)
                        wait(act, "u_scl", t0 + b - 2)
                        src_mode = part.third == SRC
                        f(u_sd[b][:, :], u_mv[b][:, :, 1], ACT.Sqrt,
                          bias=eps_col[0:P, 0:1] if src_mode else eps_col[0:P, 2:3],
                          scale=1.0 if src_mode else A34).then_inc(s["u_std"], 1)

                def edge_1(b):
                    G, g = 2 * K + b, 2 * k + b
                    if r == 0:
                        wait(act, "e_rows", G)
                        wait(act, "e_ps_free", g - 2, sep=True)
                        by_col(e1[b], rows("e"), "rcnt", g).then_inc(s["e_mean"], 1)
                    if r == 3:
                        wait(act, "e_rows", G)
                        if not isinstance(k, int):
                            wait(act, "e_var", 2 * PAIRS + g - 2, sep=True)
                        by_col(e1[b], rows(r_bank(r, b)), "rcnt", g).then_inc(s["e_ps_free"], 1)
                    if r in (4, 5, 6):
                        wait(act, "e_rows", G)
                        wait(act, "e_biased", 2 * (K - 4 * PAIRS) + b - 2, sep=True)
                        by_col(e1[b], rows(e_bank(r, b)), "dv2", g).then_inc(s["e_scaled"], 1)
                    if r == 7:
                        wait_dma(act, got_self[b], 6 * PAIRS + 2 * (k + 1), LOAD)
                        if not isinstance(k, int):
                            wait(act, "e_var", 4 * PAIRS + g - 2, sep=True)
                        by_col(e1[b], self_in[0][b], "c7", g).then_inc(s["e_w"], 1)
                        by_col(e3[b], self_in[1][b], "d7", g).then_inc(s["e_w"], 1)

                def radial_emb():
                    if r == 3:
                        for b in range(2):
                            wait(act, "rad_x", 2 * k + b)
                            f(rad_square[b], rad_in[b], ACT.Square, bias=centre[:, 0:1], scale=float(NB - 1)
                              ).then_inc(s["rad_sq"], 1)
                        for b in range(2):
                            wait(act, "rad_sq", 2 * k + b)
                            wait(act, "rad_rdy", 2 * k + b - 2)
                            f(rad_gauss[b], rad_square[b], ACT.Exp, scale=-0.5).then_inc(s["rad_exp"], 1)

                def w_to_sb(b):
                    g = 2 * k + b
                    if r == 7:
                        wait_dma(act, put_w[b], k, LOAD)
                        wait(act, "m3_ps", g)
                        f(w_rows[b], rows(hid2_bank[b]), ACT.Copy).then_inc(s["m3_sb"], 1)

                def radial_mlp(b, i):
                    g = 2 * k + b
                    if r == 6:
                        wait(act, f"m{i}_ps", g)
                        if i == 1:
                            wait(act, "m2_ps", g - 2)
                        else:
                            wait_dma(act, put_hid[b], k, 16)
                        f((hid1[b], hid2[b][0:HID, :])[i - 1], ps[(hid1_bank, hid2_bank)[i - 1][b]][0:HID, 0:C],
                          ACT.Silu, bias=mb[:, i - 1:i]).then_inc(s[f"m{i}_sb"], 1)

                A, B = 0, 1
                if not part.beside:
                    late(part.before(), 0)
                    late(part.before(), 1)
                    radial_mlp(A, 1)
                    edge_1(A)
                    if r == 7 and part.before():
                        normed_b(k - 1)
                    radial_mlp(B, 1)
                    edge_1(B)
                    w_to_sb(A)
                    w_to_sb(B)
                    if r == 6:
                        edge_2(r, k, A)
                        radial_mlp(A, 2)
                        edge_2(r, k, B)
                        radial_mlp(B, 2)
                    radial_emb()
                    if r != 6:
                        edge_2(r, k, A)
                        edge_2(r, k, B)
                    return
                h3_rows(A)
                x2_cols(A)
                x_cols(A)
                dst_cols(A)
                late(part.before(), 0)
                relu(A, 1)
                h3_rows(B)
                x2_cols(B)
                z_rows(A)
                x_cols(B)
                u_root(A)
                edge_1(A)
                late(part.before(), 1)
                local(A, 1)
                relu(A, 2)
                relu(B, 1)
                u_root(B)
                z_root(A)
                x_result(part, A)
                dst_cols(B)
                edge_2(r, k, A)
                local(A, 2)
                local(B, 1)
                z_rows(B)
                edge_1(B)
                relu(B, 2)
                z_root(B)
                local(B, 2)
                for i in (1, 2):
                    radial_mlp(A, i)
                    radial_mlp(B, i)

            def finish(r):
                late(Parts(r, PAIRS - 1), 0)
                late(Parts(r, PAIRS - 1), 1)
                if r == 7:
                    normed_b(PAIRS - 1)

            act.wait_ge(s["cols"], 3)
            rounds(act, body, finish)

            def body8(k, new, old):
                def gathered(b):
                    wait(act, "xg_T", 2 * k + b)
                    wait(act, "up_ps", 2 * k + b - 2)
                    f(xdT[b][:, :], ps["e"][:, 0:C], ACT.Copy).then_inc(s["xg_sb"], 1)

                def mids(b):
                    g = 2 * k + b
                    wait(act, "mid_T", g)
                    wait(act, "msgo_ps", g - 2)
                    f(h1T[b][:, :], ps["h1"][:, 0:C], ACT.Copy).then_inc(s["mid_sb1"], 1)
                    f(h2T[b][:, :], ps["h2"][:, 0:C], ACT.Copy).then_inc(s["mid_sb2"], 1)

                def root(b):
                    wait(act, "e_var", 6 * PAIRS + 2 * k - 2 + b)
                    f(e_sd[b][:, :], e_mv[b][:, :, 1], ACT.Sqrt, bias=eps_col[0:P, 0:1]
                      ).then_inc(s["e_std"], 1)

                if new:
                    gathered(0)
                    gathered(1)
                for b in range(2):
                    if new:
                        mids(b)
                    if old:
                        root(b)
            body8(0, True, False)
            body8(1, True, True)
            with act.Fori(2, PAIRS) as k:
                body8(k, True, True)
            body8(PAIRS, False, True)

        @block.vector
        def _(dve):
            v = nc.vector
            st = Steps(dve, s["setup_dve"], 0, 0)
            st.inc(v.memset(zero_row[:, :], 0.0))
            st.inc(v.memset(w_up[:, :], 0.0))
            st.inc(v.memset(ones[:, :], 1.0))
            st.inc(v.memset(eps_col[:, 0:1], EPS))
            st.inc(v.memset(eps_col[:, 1:2], B12))
            st.inc(v.memset(eps_col[:, 2:3], B34))
            st.inc(v.memset(pick3[:, :], 0.0))
            for i in range(2):
                st.inc(v.memset(w_out[i][:, :], 0.0))
                st.inc(v.memset(run[i][:, :], 0.0))
                st.inc(v.memset(cnt_row[i], 0.0))
            st.inc(v.memset(dst_tile[0:1, 0, 0, :], 0))
            st.inc(v.memset(dst_next[0:1, 0, 0, :], 0))
            st.wait()
            for q in range(3):
                st.inc(v.memset(pick3[32 * q:32 * q + 1, :], 1.0))
            dve.wait_ge(s["setup_in"], n_setup_in[0])
            dve.wait_ge(s["setup_pool"], 5)
            st.inc(v.tensor_copy(tf[:, :, :, :], dst_tile[:, :, :, :]))
            st.inc(v.tensor_copy(first[:, :], dst_tile[:, :, 1, 0]))
            st.inc(v.tensor_tensor(tl[:, :, :, :], dst_tile[:, :, :, :], dst_next[:, :, :, :], ALU.not_equal))
            st.inc(v.tensor_tensor(w_sage_self[:, :], w_sage_self[:, :], ident[:, :], ALU.add))
            st.inc(v.tensor_copy(col["srcp1"][:, :], src_i[:, :]))
            st.inc(v.tensor_copy(col["dstf"][:, :], dst_i[:, :]))
            st.inc(v.tensor_tensor(col["tmpa"][:, :], dst_i[:, :], next_i[:, :], ALU.not_equal))
            st.inc(v.tensor_scalar(mw0[:, :], mw0[:, :], float(NB) ** 0.5, None, ALU.mult))
            for i in range(2):
                for c in range(4):
                    p0 = MUL * c
                    dst = w_out[i][0:MUL, 0:MUL] if c == 0 else \
                        w_out[i][p0:p0 + MUL, MUL + c - 1:MUL + c - 1 + 3 * (MUL - 1) + 1:3]
                    st.inc(v.tensor_scalar(dst, wo_in[p0:p0 + MUL, i * MUL:(i + 1) * MUL],
                                           1.0 / (8.0 * 16.0), None, ALU.mult))
            st.wait()
            for i, w in enumerate((w_sage_self, w_sage_neigh, b_row[0])):
                st.inc(v.tensor_reduce(w_mean[:, i:i + 1], w[:, :], AX_X, ALU.add))
            st.wait()
            st.then(v.tensor_scalar(w_mean[:, :], w_mean[:, :], 1.0 / D, None, ALU.mult))
            for i, w in enumerate((w_sage_self, w_sage_neigh, b_row[0])):
                st.inc(v.tensor_scalar(w[:, :], w[:, :], w_mean[:, i:i + 1], None, ALU.subtract))
            st.wait()
            for i, row in ((0, b_row[0]), (1, b_row[3])):
                st.then(v.tensor_copy(b_rest[:, :], row[:, :]))
                for q in range(3):
                    p0 = 32 * q
                    st.then(v.tensor_copy(b_part[:, :], b_rest[:, :]))
                    st.inc(v.tensor_copy(b_wide[i][p0:p0 + 32, 0:D], b_part[p0:p0 + 32, :]))
                    st.then(v.tensor_tensor(b_rest[:, :], b_rest[:, :], b_part[:, :], ALU.subtract))
                for j in range(1, J):
                    st.inc(v.tensor_copy(b_wide[i][:, j * D:(j + 1) * D], b_wide[i][:, 0:D]))
            st.wait()
            st.then(v.scalar_tensor_tensor(out=tf[:, :, :, :].rearrange("p h q c -> p (h q c)"),
                                           in0=tl[:, :, :, :].rearrange("p h q c -> p (h q c)"), scalar=0.5,
                                           in1=tf[:, :, :, :].rearrange("p h q c -> p (h q c)"),
                                           op0=ALU.mult, op1=ALU.add))
            st.then(v.tensor_scalar(tf[:, :, :, :], tf[:, :, :, :], 0.5, None, ALU.add))
            st.then(v.tensor_tensor(diff[:, :, 0:P], tf[:, :, 1, :], tf[:, :, 0, :], ALU.subtract))
            st.then(v.tensor_copy(diff[0:1, 0, 0:P], tf[0:1, 0, 1, :]))
            st.inc(v.memset(diff[:, :, P:P + 1], 1.0))
            st.inc(v.tensor_scalar(col["srcp1"][:, :], col["srcp1"][:, :], 1.0, None, ALU.add))
            st.then(v.tensor_scalar(col["dstf"][:, :], col["dstf"][:, :], float(-N), None, ALU.add))
            st.then(v.tensor_tensor(col["dstf"][:, :], col["dstf"][:, :], col["tmpa"][:, :], ALU.mult))
            st.then(v.tensor_scalar(col["dstf"][:, :], col["dstf"][:, :], float(N), None, ALU.add))
            st.inc(v.tensor_copy(out_row[:, :], col["dstf"][:, :]))
            st.inc(v.tensor_tensor(y1[:, :, :], attr[:, :, :], attr[:, :, :], ALU.mult))
            dve.wait_ge(s["setup_out"], 7 * 16)
            st.inc(v.tensor_scalar(w_up[:, :], w_up[:, :], float(MUL) ** -0.5, None, ALU.mult))
            st.wait()
            st.then(v.tensor_reduce(col["dstf"][:, :], y1[:, :, :], AX_X, ALU.add))
            v.memset(found[:, :, :], 0.0).then_inc(s["cols"], 1)
            dve.wait_ge(s["cols"], 1)

            def run_starts(k, b):
                g = 2 * k + b
                wait_dma(dve, got_prep[b], k + 1, 32)
                v.tensor_tensor(mask[:, bass.ds(g * C, C)], dst_wide[b][:, 1:C + 1],
                                dst_wide[b][:, 0:C], ALU.is_equal).then_inc(s["p_mask"], 1)
                if not isinstance(k, int):
                    dve.wait_ge(s["p_find"], g - 1)
                for h in range(2):
                    v.tensor_scalar(step_u[h][b], src_wide[b], first[:, h:h + 1], None,
                                    ALU.is_ge).then_inc(s["p_mask"], 1)

            def run_counts(k, b):
                g = 2 * k + b
                dve.wait_ge(s["p_mask"], 3 * g + 1)
                if not (isinstance(k, int) and b == 0):
                    dve.wait_ge(s["p_count"], g)
                v.tensor_tensor_scan(cnt_row[b], mask[:, bass.ds(g * C, C)], ones[:, :],
                                     cnt_row[1 - b][:, C - 1:C], ALU.mult, ALU.add
                                     ).then_inc(s["p_count"], 1)

            def read_found(k, b):
                g = 2 * k + b
                wait_own(dve, s["p_find"], g + 1)
                fr = ps[find_bank[b]][0:P, 0:J * (P + 1)].rearrange("p (j c) -> p j c", j=J)
                for j in range(J):
                    v.scalar_tensor_tensor(out=found[:, j, :], in0=fr[:, j, 0:P],
                                           scalar=col["srcp1"][:, bass.ds(g * J + j, 1)],
                                           in1=iota1[:, :], op0=ALU.is_equal, op1=ALU.mult
                                           ).then_inc(s["p_step"], 1)
                v.tensor_copy(col["cnt"][:, bass.ds(g * J, J)], ps[count_bank[b]][0:P, 0:J]
                              ).then_inc(s["p_step"], 1)
                v.tensor_copy(col["tile1"][:, bass.ds(g * J, J)], fr[:, :, P]).then_inc(s["p_step"], 1)
                wait_own(dve, s["p_step"], 6 * (g + 1))
                v.tensor_reduce(col["j1"][:, bass.ds(g * J, J)], found[:, :, :], AX_X, ALU.add
                                ).then_inc(s["p_found"], 1)
                dve.wait_ge(s["p_found"], g + 1)

            def prepare(k, new, old):
                if new:
                    run_starts(k, 0)
                    run_counts(k, 0)
                if old:
                    read_found(k - 1, 0)
                if new:
                    run_starts(k, 1)
                    run_counts(k, 1)
                if old:
                    read_found(k - 1, 1)

            prepare(0, True, False)
            with dve.Fori(0, (PAIRS - 1) // 2) as step:
                for i in (1, 2):
                    prepare(step * 2 + i, True, True)
            prepare(PAIRS, False, True)

            v.tensor_scalar(col["deg"][:, :], col["cnt"][:, :], 1.0, None, ALU.add).then_inc(s["cols"], 1)
            st.inc(v.tensor_scalar(col["tile1"][:, :], col["tile1"][:, :], float(P), float(-P - 1), ALU.mult, ALU.add))
            st.inc(v.tensor_scalar(col["d7"][:, :], col["j1"][:, :], 0.5, None, ALU.is_ge))
            st.wait()
            st.then(v.tensor_tensor(col["j1"][:, :], col["j1"][:, :], col["tile1"][:, :], ALU.add))
            st.inc(v.tensor_scalar(col["c7"][:, :], col["j1"][:, :], float(-E), None, ALU.add))
            st.then(v.tensor_tensor(col["e7"][:, :], col["j1"][:, :], col["own"][:, :], ALU.subtract))
            st.inc(v.tensor_tensor(col["c7"][:, :], col["c7"][:, :], col["d7"][:, :], ALU.mult))
            st.then(v.tensor_tensor(col["e7"][:, :], col["e7"][:, :], col["d7"][:, :], ALU.mult))
            st.inc(v.tensor_scalar(col["c7"][:, :], col["c7"][:, :], float(E), None, ALU.add))
            st.then(v.tensor_tensor(col["e7"][:, :], col["e7"][:, :], col["own"][:, :], ALU.add))
            st.inc(v.tensor_copy(slot_or_zero[:, :], col["c7"][:, :]))
            st.then(v.tensor_copy(slot_or_local[:, :], col["e7"][:, :]))
            dve.wait_ge(s["cols"], 2)
            dve.wait_ge(s["setup_act"], 3)
            st.inc(v.reciprocal(col["rcnt"][:, :], col["cnt"][:, :]))
            st.inc(v.reciprocal(col["dv1"][:, :], col["sq1"][:, :]))
            st.inc(v.reciprocal(col["dv2"][:, :], col["tmpb"][:, :]))
            st.inc(v.tensor_scalar(col["cnt16"][:, :], col["cnt"][:, :], 1.0 / 16.0, None, ALU.mult))
            st.inc(v.tensor_scalar(col["c7"][:, :], col["deg"][:, :], ALPHA / (1 - ALPHA), 1.0, ALU.mult, ALU.add))
            st.inc(v.tensor_scalar(col["d7"][:, :], col["deg"][:, :], 1.0 / (1 - ALPHA), None, ALU.mult))
            st.then(v.tensor_scalar(col["tmpa"][:, :], col["tmpa"][:, :], 1e-12, None, ALU.add))
            st.then(v.reciprocal(col["tmpb"][:, :], col["tmpa"][:, :]))
            st.inc(v.tensor_tensor(y_unit[:, :, :], attr[:, :, :], bc(col["tmpb"][:, :], 3), ALU.mult))
            st.inc(v.tensor_tensor(col["c3"][:, :], col["sq1"][:, :], col["dv2"][:, :], ALU.mult))
            st.inc(v.tensor_tensor(col["e7"][:, :], col["dv2"][:, :], col["dv2"][:, :], ALU.mult))
            st.inc(v.tensor_scalar(col["f7"][:, :], col["dv2"][:, :], 1 - ALPHA, None, ALU.mult))
            st.wait()
            st.inc(v.tensor_scalar(col["c3"][:, :], col["c3"][:, :], 0.25, None, ALU.mult))
            st.inc(v.tensor_scalar(col["e7"][:, :], col["e7"][:, :], (1 - ALPHA) ** 2, None, ALU.mult))
            st.inc(v.tensor_scalar(y1[:, :, :], y_unit[:, :, :], 3.0 ** 0.5, None, ALU.mult))
            st.wait()
            v.memset(found[:, :, :], 0.0).then_inc(s["cols"], 1)

            def stats(q, x, sts, mv):
                for j in range(J):
                    q.inc(v.bn_stats(sts[:, j, :], x[:, j, :]))
                wait_own(dve, q.sem, q.so_far())
                for j in range(J):
                    i = v.bn_aggr(mv[:, j, :], sts[:, j, :])
                    if j < J - 1:
                        q.inc(i)
                return i

            def normed(x_, x, mv, scale):
                for j in range(J):
                    i = v.tensor_scalar(x_[:, j, :], x[:, j, :], mv[:, j, 0:1], scale[:, j:j + 1],
                                        ALU.subtract, ALU.mult)
                return i

            def edge_rows_2(r, k, b):
                if r not in (0, 3, 7):
                    return
                K = r * PAIRS + k
                g = 2 * k + b
                nth = {0: 0, 3: 1, 7: 2}[r] * 2 * PAIRS + g
                wait(dve, "e_std", nth)
                v.reciprocal(e_rs[b][:, :], e_sd[b][:, :]).then_inc(s["e_vv"], 1)
                dve.wait_ge(s["e_vv"], 2 * nth + 1)
                v.tensor_tensor(e_sc[b][:, :], e_rs[b][:, :], cols({0: "dv1", 3: "c3", 7: "f7"}[r], g),
                                ALU.mult).then_inc(s["e_vv"], 1)
                wait_dma(dve, put_e[b], K, LOAD)
                dve.wait_ge(s["e_vv"], 2 * nth + 2)
                if r == 7 and b == 0:
                    normed(e_out[b], e2[b], e_mv[b], e_sc[b]).then_inc(s["e_rdy"], 1)
                elif r == 7:
                    v.scalar_tensor_tensor(out=e_nb[:, :], in0=e_mv[b][:, :, 0], scalar=-1.0,
                                           in1=e_sc[b][:, :], op0=ALU.mult, op1=ALU.mult
                                           ).then_inc(s["e_shift"], 1)
                else:
                    v.tensor_tensor(e_out[b][:, :, :], e2[b][:, :, :], bc(e_sc[b][:, :]), ALU.mult
                                    ).then_inc(s["e_rdy"], 1)

            def body(r, k, part):
                K = r * PAIRS + k
                if part.K is not None:
                    n0, t0 = 2 * part.K, 2 * (part.K - 2)

                def scan(b):
                    G, g = 2 * K + b, 2 * k + b
                    if r == 0:
                        wait(dve, "x_T_sb", G)
                    else:
                        wait(dve, "e_T", G)
                    wait(dve, "e_rows", G - 2)
                    wait(dve, "scan", G - 1)
                    v.tensor_tensor_scan(run[b][:, :], mask[:, bass.ds(g * C, C)],
                                         xT[b][:, :] if r == 0 else ps[e_bank(r, b)][:, 0:C], run[1 - b][:, C - 1:C],
                                         ALU.mult, ALU.add).then_inc(s["scan"], 1)
                    if r in (4, 5, 6):
                        q = 2 * (K - 4 * PAIRS) + b
                        wait(dve, "scan", G)
                        wait(dve, "e_self_T", q)
                        v.tensor_tensor(run_self[b][:, :], ps[r_bank(r, b)][:, 0:C], run[b][:, :], ALU.add
                                        ).then_inc(s["self_add"], 1)

                def z_stats(b):
                    if part.first:
                        n = n0 + b
                        wait(dve, "z_sb", n)
                        q = Steps(dve, s["z_step"], 2 * J - 1, n)
                        stats(q, z_sb[b], z_st[b], z_mv[b]).then_inc(s["z_var"], 1)
                        q.end()

                def x2_rows(b):
                    if part.first:
                        n = n0 + b
                        wait(dve, "x2_T", n - 4)
                        wait(dve, "v_rdy", n - 4)
                        if part.old == SRC:
                            wait_dma(dve, put_loc[b], part.K - 1, 3 * LOAD)
                        wait(dve, "z_std", n)
                        v.reciprocal(z_rs[b][:, :], z_sd[b][:, :]).then_inc(s["z_step2"], 1)
                        dve.wait_ge(s["z_step2"], n + 1)
                        v.tensor_tensor(x2[part.parity][b][:, :, :], z_sb[b][:, :, :], bc(z_rs[b][:, :]), ALU.mult
                                        ).then_inc(s["x2_rdy"], 1)

                def u_rows(b):
                    if part.third:
                        n = t0 + b
                        q = Steps(dve, s["u_step"], 2 * J - 1, n)
                        wait(dve, "x_out_rdy", n - 2)
                        wait(dve, "x2_rdy", n)
                        wait(dve, "h3_sb", n)
                        h3 = flat((loc[2] if part.third == SRC else h3_sb)[b])
                        v.scalar_tensor_tensor(out=flat(v_sb[b]), in0=h3, scalar=SLOPE, in1=h3,
                                               op0=ALU.mult, op1=ALU.max).then_inc(s["h3_used"], 1)
                        wait(dve, "h3_used", n)
                        v.tensor_tensor(flat(v_sb[b]), flat(v_sb[b]), flat(x2[part.parity][b]), ALU.add
                                        ).then_inc(s["v_rdy"], 1)
                        wait(dve, "v_rdy", n)
                        stats(q, v_sb[b], u_st[b], u_mv[b]).then_inc(s["u_var"], 1)
                        q.end()

                def u_scale(b):
                    if part.third:
                        n = t0 + b
                        wait(dve, "u_std", n)
                        v.reciprocal(u_rs[b][:, :], u_sd[b][:, :]).then_inc(s["u_step2"], 1)
                        dve.wait_ge(s["u_step2"], n + 1)
                        v.scalar_tensor_tensor(out=u_nb[b][:, :], in0=u_mv[b][:, :, 0], scalar=-1.0,
                                               in1=u_rs[b][:, :], op0=ALU.mult, op1=ALU.mult
                                               ).then_inc(s["u_scl"], 1)

                def edge_rows_1(b):
                    G, g = 2 * K + b, 2 * k + b
                    if r in (4, 5, 6):
                        n = 2 * (K - 4 * PAIRS) + b
                        wait(dve, "e_scaled", n)
                        wait(dve, "e_rdy", G - 2)
                        v.tensor_tensor(e2[b][:, :, :], e1[b][:, :, :], b4(b_row[r - 3][0:P, :]), ALU.add
                                        ).then_inc(s["e_biased"], 1)
                        return
                    wait(dve, "e_rows", G)
                    if r in (1, 2):
                        wait_dma(dve, put_e[b], K, LOAD)
                        v.tensor_tensor(e_out[b][:, :, :], rows("r"), bc(cols("rcnt", g)), ALU.mult
                                        ).then_inc(s["e_rdy"], 1)
                        return
                    if r == 0:
                        q = Steps(dve, s["step0"], 2 * J - 1, g)
                        wait(dve, "e_mean", g)
                        v.tensor_tensor(e2[b][:, :, :], rows("r"), e1[b][:, :, :], ALU.add
                                        ).then_inc(s["e_ps_free"], 1)
                        wait(dve, "e_ps_free", G)
                        stats(q, e2[b], e_st[b], e_mv[b]).then_inc(s["e_var"], 1)
                        q.end()
                    if r == 3:
                        q = Steps(dve, s["step3"], 2 * J + 3, g)
                        wait_dma(dve, got_self[b], 3 * (k + 1), LOAD)
                        q.inc(v.tensor_tensor(e3[b][:, :, :], self_in[1][b][:, :, :], self_in[2][b][:, :, :], ALU.add))
                        wait(dve, "e_ps_free", 2 * PAIRS + g)
                        q.wait()
                        q.then(v.tensor_tensor(e1[b][:, :, :], e1[b][:, :, :], e3[b][:, :, :], ALU.add))
                        wait(dve, "e_rdy", G - 2)
                        q.then(v.scalar_tensor_tensor(out=flat(e2[b]), in0=flat(self_in[0][b]), scalar=5.0,
                                                      in1=flat(e1[b]), op0=ALU.mult, op1=ALU.add))
                        q.then(stats(q, e2[b], e_st[b], e_mv[b]))
                        v.tensor_tensor(e_v[b][:, :], e_mv[b][:, :, 1], cols("cnt16", g), ALU.mult
                                        ).then_inc(s["e_var"], 1)
                        q.end()
                    if r == 7:
                        q = Steps(dve, s["step7"], 2 * J + 2, g)
                        wait(dve, "e_w", 2 * g + 1)
                        wait(dve, "e_rdy", G - 2)
                        v.tensor_tensor(e2[b][:, :, :], rows(r_bank(r, b)), e1[b][:, :, :], ALU.add
                                        ).then_inc(s["e_ps_free"], 1)
                        wait(dve, "e_ps_free", 4 * PAIRS + g)
                        q.then(v.scalar_tensor_tensor(out=flat(e1[b]), in0=flat(e2[b]), scalar=SLOPE,
                                                      in1=flat(e2[b]), op0=ALU.mult, op1=ALU.max))
                        q.then(v.tensor_tensor(e2[b][:, :, :], e1[b][:, :, :], e3[b][:, :, :], ALU.add))
                        q.then(stats(q, e2[b], e_st[b], e_mv[b]))
                        v.tensor_tensor(e_v[b][:, :], e_mv[b][:, :, 1], cols("e7", g), ALU.mult
                                        ).then_inc(s["e_var"], 1)
                        q.end()

                def radial_in(b):
                    g = 2 * k + b
                    if r == 3:
                        wait(dve, "rad_sq", g - 2)
                        wait_dma(dve, got_ew[b], k + 1, 16)
                        v.tensor_scalar(rad_in[b], length[b], 0.0, 1.0, ALU.max, ALU.min
                                        ).then_inc(s["rad_x"], 1)

                def radial_out(b):
                    g = 2 * k + b
                    if r == 3:
                        wait_dma(dve, put_rad[b], k, 16)
                        wait(dve, "rad_exp", g)
                        v.scalar_tensor_tensor(out=rad_emb[b], in0=length[b], scalar=1.0,
                                               in1=rad_gauss[b], op0=ALU.is_le, op1=ALU.mult
                                               ).then_inc(s["rad_rdy"], 1)

                if r == 7 and isinstance(k, int):
                    for b in range(2):
                        v.memset(work[b][HID:HID + 1, 2, :], 1.0).then_inc(s["rad_one"], 1)
                A, B = 0, 1
                if not part.beside:
                    scan(A)
                    scan(B)
                    for b in range(2):
                        if r in ALONE and not isinstance(k, int):
                            edge_rows_2(r, k - 1, b)
                        radial_in(b)
                    edge_rows_1(A)
                    radial_out(A)
                    edge_rows_1(B)
                    radial_out(B)
                    return
                u_rows(A)
                scan(A)
                if r == 0 and part.before():
                    edge_rows_2(r, k - 1, B)
                u_rows(B)
                u_scale(A)
                z_stats(A)
                edge_rows_1(A)
                scan(B)
                x2_rows(A)
                u_scale(B)
                z_stats(B)
                edge_rows_2(r, k, A)
                edge_rows_1(B)
                x2_rows(B)
                if r:
                    edge_rows_2(r, k, B)

            def finish(r):
                if r == 0:
                    edge_rows_2(r, PAIRS - 1, B)
                if r in ALONE:
                    edge_rows_2(r, PAIRS - 1, A)
                    edge_rows_2(r, PAIRS - 1, B)

            A, B = 0, 1
            rounds(dve, body, finish)

            def body8(k, new, old):
                def messages(b):
                    g = 2 * k + b
                    q = Steps(dve, s["msg_step"], 7, g)
                    up = rows(up_bank[b])
                    vec = up[:, :, MUL:4 * MUL].rearrange("p j (c m) -> p j c m", c=3)
                    w = self_in[1][b]
                    yu = y_unit[:, bass.ds(g * J, J), :].unsqueeze(3).to_broadcast([P, J, 3, MUL])
                    ys = y1[:, bass.ds(g * J, J), :].unsqueeze(3).to_broadcast([P, J, 3, MUL])

                    def over_c(x):
                        return x.unsqueeze(2).to_broadcast([P, J, 3, MUL])

                    wait(dve, "mid_T", g - 2)
                    wait_dma(dve, got_w[b], k + 1, LOAD)
                    wait(dve, "up_ps", g)
                    q.inc(v.tensor_tensor(mid[b][:, :, 0:MUL], up[:, :, 0:MUL], w[:, :, 0:MUL], ALU.mult))
                    q.inc(v.tensor_tensor(w1s[b], up[:, :, 0:MUL], w[:, :, MUL:2 * MUL], ALU.mult))
                    q.inc(v.tensor_tensor(mid[b][:, :, 5 * MUL:8 * MUL].rearrange("p j (c m) -> p j c m", c=3),
                                          vec, over_c(w[:, :, 2 * MUL:3 * MUL]), ALU.mult))
                    q.then(v.tensor_tensor(vy[b], vec, yu, ALU.mult))
                    q.inc(v.tensor_tensor(mid[b][:, :, MUL:4 * MUL].rearrange("p j (c m) -> p j c m", c=3),
                                          over_c(w1s[b]), ys, ALU.mult))
                    q.then(v.tensor_tensor(vsum[0][b], vy[b][:, :, 0, :], vy[b][:, :, 1, :], ALU.add))
                    q.then(v.tensor_tensor(vsum[1][b], vsum[0][b], vy[b][:, :, 2, :], ALU.add))
                    q.end()
                    v.tensor_tensor(mid[b][:, :, 4 * MUL:5 * MUL], vsum[1][b], w[:, :, 3 * MUL:4 * MUL],
                                    ALU.mult).then_inc(s["msg"], 1)

                def scan8(b):
                    g = 2 * k - 2 + b
                    wait(dve, "msgo_ps", g)
                    wait(dve, "run_T", g - 2)
                    wait(dve, "scan", 16 * PAIRS + g - 1)
                    v.tensor_tensor_scan(run[b][:, :], mask[:, bass.ds(g * C, C)], ps[msg_bank[b]][:, 0:C],
                                         run[1 - b][:, C - 1:C], ALU.mult, ALU.add).then_inc(s["scan"], 1)

                def result_stats(b):
                    g = 2 * k - 2 + b
                    q = Steps(dve, s["step8"], 2 * J - 1, g)
                    wait_dma(dve, got_self[b], 8 * PAIRS + k, LOAD)
                    wait(dve, "run_T", g)
                    v.tensor_tensor(e2[b][:, :, :], rows(sum_bank[b]), self_in[0][b][:, :, :], ALU.add
                                    ).then_inc(s["e_ps_free"], 1)
                    wait(dve, "e_ps_free", 6 * PAIRS + g)
                    stats(q, e2[b], e_st[b], e_mv[b]).then_inc(s["e_var"], 1)
                    q.end()

                def result(b):
                    g = 2 * k - 2 + b
                    wait(dve, "e_std", 6 * PAIRS + g)
                    v.reciprocal(e_rs[b][:, :], e_sd[b][:, :]).then_inc(s["e_vv"], 1)
                    wait_dma(dve, put_fin[b], k - 1, 16 * J)
                    dve.wait_ge(s["e_vv"], 12 * PAIRS + g + 1)
                    normed(e_out[b], e2[b], e_mv[b], e_rs[b]).then_inc(s["e_rdy"], 1)

                if old:
                    scan8(0)
                    scan8(1)
                for b in range(2):
                    if new:
                        messages(b)
                    if old:
                        result_stats(b)
                if old:
                    result(0)
                    result(1)
            body8(0, True, False)
            body8(1, True, True)
            with dve.Fori(2, PAIRS) as k:
                body8(k, True, True)
            body8(PAIRS, False, True)


def kernel(x, src, dst, edge_attr_3, edge_weight, L0_gnn_W, L0_gnn_b, L2_gnn_W1, L2_gnn_b1, L2_gnn_W2,
           L2_gnn_b2, L2_gnn_W3, L2_gnn_b3, L3_gnn_W_up0, L3_gnn_W_up1, L3_gnn_mlp_w0, L3_gnn_mlp_b0,
           L3_gnn_mlp_w1, L3_gnn_mlp_b1, L3_gnn_mlp_w2, L3_gnn_mlp_b2, L3_gnn_W_out0, L3_gnn_W_out1):
    import numpy as _np
    import concourse.bacc as _bacc
    from concourse import mybir as _mybir
    from concourse.bass_utils import run_bass_kernel_spmd as _run

    src, dst = _np.asarray(src), _np.asarray(dst)
    none = _np.full(1, -1, dst.dtype)
    dst_ext = _np.concatenate([none, dst, none])
    by_tile = lambda v: _np.ascontiguousarray(v.reshape(T, P).T)
    arrays = {
        "x": x, "src": src, "dst_ext": dst_ext, "src_pt": by_tile(src), "dst_pt": by_tile(dst),
        "next_pt": by_tile(dst_ext[2:]),
        "attr_pt": _np.ascontiguousarray(_np.asarray(edge_attr_3).reshape(T, P, 3).transpose(1, 0, 2)),
        "edge_weight": edge_weight, "W_sage": L0_gnn_W, "b_sage": L0_gnn_b, "W1": L2_gnn_W1,
        "b1": L2_gnn_b1, "W2": L2_gnn_W2, "b2": L2_gnn_b2, "W3": L2_gnn_W3, "b3": L2_gnn_b3,
        "W_up0": L3_gnn_W_up0, "W_up1": L3_gnn_W_up1, "mlp_w0": L3_gnn_mlp_w0,
        "mlp_b0": L3_gnn_mlp_b0, "mlp_w1": L3_gnn_mlp_w1, "mlp_b1": L3_gnn_mlp_b1,
        "mlp_w2": L3_gnn_mlp_w2, "mlp_b2": L3_gnn_mlp_b2, "W_out0": L3_gnn_W_out0,
        "W_out1": L3_gnn_W_out1,
    }
    nc = _bacc.Bacc("TRN2", target_bir_lowering=False, num_devices=1)
    held, args = {}, {}
    for name, v in arrays.items():
        v = _np.ascontiguousarray(v)
        held[f"in_{name}_dram"] = v
        args[name] = nc.dram_tensor(f"in_{name}_dram", v.shape, _mybir.dt.from_np(v.dtype),
                                    kind="ExternalInput").ap()
    out = nc.dram_tensor("out_0_dram", (N, D), _mybir.dt.float32, kind="ExternalOutput").ap()
    gnn_kernel(nc, args, out)
    r = _run(nc, [held], core_ids=[0])
    return r.results[0]["out_0_dram"]
```
